# Optimizing a Trainium2 kernel written in Bass

```python
import numpy as np
import jax
import jax.numpy as jnp

def _softmax(x, axis=-1):
    return jax.nn.softmax(x, axis=axis)

def _gelu(x):
    return jax.nn.gelu(x, approximate=True)

def _silu(x):
    return jax.nn.silu(x)

def _sigmoid(x):
    return jax.nn.sigmoid(x)

def _layernorm(x, axis=-1, eps=1e-05):
    m = jnp.mean(x, axis=axis, keepdims=True)
    v = jnp.var(x, axis=axis, keepdims=True)
    return (x - m) / jnp.sqrt(v + eps)

def _scatter_add(tgt, idx, src, axis=0):
    return tgt.at[idx].add(src)

def _segment_sum(src, seg, n):
    return jax.ops.segment_sum(src, seg, n)
kernel_name = 'mk_gnn_ffn_d2_gnn_r32_7d6529'

def setup_inputs(seed: int=0):
    np.random.seed(seed)
    _w = jnp.asarray

    def _rec_inputs():
        import jax
        import jax.numpy as jnp
        _gk = jax.random.key(seed)
        x = 7.22e-05 + 1 * jax.random.normal(jax.random.fold_in(_gk, 1), (512, 512), jnp.float32)
        src = jax.random.randint(jax.random.fold_in(_gk, 2), (16384,), 0, 512, jnp.int32)
        dst = jnp.minimum((512 * jax.random.uniform(jax.random.fold_in(_gk, 3), (16384,)) ** 2.0).astype(jnp.int32), 16383)
        _o = jnp.argsort(dst, stable=True)
        src = src[_o]
        dst = dst[_o]
        edge_attr_16 = -0.000585658 + 0.999949 * jax.random.normal(jax.random.fold_in(_gk, 12), (16384, 16), jnp.float32)
        edge_weight = jax.random.uniform(jax.random.fold_in(_gk, 14), (16384,), jnp.float32, 0.0, 0.999996)
        return (x, src, dst, edge_attr_16, edge_weight)
    x, src, dst, edge_attr_16, edge_weight = _rec_inputs()

    def _L0_gnn_setup():
        import jax, jax.numpy as jnp
        import numpy as np
        B = 32
        N = 512
        HID = 512
        H = 8
        E = 8192
        ED = 16
        key = jax.random.key(seed)
        ks = jax.random.split(key, 12)
        x = jax.random.normal(ks[0], (B * N, HID), jnp.float32)
        batch = jnp.repeat(jnp.arange(B, dtype=jnp.int64), N)
        g = jax.random.randint(ks[1], (E,), 0, B)
        src = g * N + jax.random.randint(ks[2], (E,), 0, N)
        dst = g * N + jax.random.randint(ks[3], (E,), 0, N)
        edge_index = jnp.stack([src, dst]).astype(jnp.int64)
        edge_attr = jax.random.normal(ks[4], (E, ED), jnp.float32)
        s = 1.0 / np.sqrt(HID).astype(np.float32)
        Wq = jax.random.normal(ks[5], (HID, HID), jnp.float32) * s
        Wk = jax.random.normal(ks[6], (HID, HID), jnp.float32) * s
        Wv = jax.random.normal(ks[7], (HID, HID), jnp.float32) * s
        Wo = jax.random.normal(ks[8], (HID, HID), jnp.float32) * s
        We = jax.random.normal(ks[9], (ED, H), jnp.float32) * (1.0 / np.sqrt(ED).astype(np.float32))
        bq = jnp.zeros((HID,), jnp.float32)
        bk = jnp.zeros((HID,), jnp.float32)
        bv = jnp.zeros((HID,), jnp.float32)
        bo = jnp.zeros((HID,), jnp.float32)
        be = jnp.zeros((H,), jnp.float32)
        return dict(x=x, batch=batch, edge_index=edge_index, edge_attr=edge_attr, Wq=Wq, bq=bq, Wk=Wk, bk=bk, Wv=Wv, bv=bv, Wo=Wo, bo=bo, We=We, be=be, num_graphs=B)
    _L0_gnn_all = _L0_gnn_setup()
    _L0_gnn_in = {k: v for k, v in _L0_gnn_all.items() if k in ('Wq', 'bq', 'Wk', 'bk', 'Wv', 'bv', 'Wo', 'bo', 'We', 'be')}
    del _L0_gnn_all

    def _L0_ffn_setup():
        import jax, jax.numpy as jnp
        import numpy as np
        TOP_K = 2

        def quick_gelu(x):
            return x * jax.nn.sigmoid(1.702 * x)
        key = jax.random.key(seed)
        ks = jax.random.split(key, 6)
        B, S, H, I, E = (8, 128, 512, 1024, 8)
        s_h = 1.0 / np.sqrt(H).astype(np.float32)
        s_i = 1.0 / np.sqrt(I).astype(np.float32)
        return {'hidden_states': jax.random.normal(ks[0], (B, S, H), jnp.float32), 'router_w': jax.random.normal(ks[1], (H, E), jnp.float32) * s_h, 'router_b': jnp.zeros((E,), jnp.float32), 'gate_up_proj': jax.random.normal(ks[2], (E, H, 2 * I), jnp.float32) * s_h, 'gate_up_proj_bias': jnp.zeros((E, 2 * I), jnp.float32), 'down_proj': jax.random.normal(ks[3], (E, I, H), jnp.float32) * s_i, 'down_proj_bias': jnp.zeros((E, H), jnp.float32)}
    _L0_ffn_all = _L0_ffn_setup()
    _L0_ffn_in = {k: v for k, v in _L0_ffn_all.items() if k in ('router_w', 'router_b', 'gate_up_proj', 'gate_up_proj_bias', 'down_proj', 'down_proj_bias')}
    del _L0_ffn_all

    def _L1_gnn_setup():
        import jax, jax.numpy as jnp
        import numpy as np
        N, E, D, K = (625, 5000, 512, 5)
        key = jax.random.key(seed)
        ks = jax.random.split(key, 8)
        return {'x': jax.random.normal(ks[0], (N, D), dtype=jnp.float32), 'edge_index': jax.random.randint(ks[1], (2, E), 0, N, dtype=jnp.int64), 'edge_weight': jax.random.uniform(ks[2], (E,), dtype=jnp.float32), 'ln_gamma': jnp.ones((D,), jnp.float32), 'ln_beta': jnp.zeros((D,), jnp.float32), 'cheb_W': jax.random.normal(ks[3], (K, D, D), dtype=jnp.float32) / np.sqrt(D), 'cheb_b': jnp.zeros((D,), jnp.float32), 'lin_W': jax.random.normal(ks[4], (D, D), dtype=jnp.float32) / np.sqrt(D), 'lin_b': jnp.zeros((D,), jnp.float32)}
    _L1_gnn_all = _L1_gnn_setup()
    _L1_gnn_in = {k: v for k, v in _L1_gnn_all.items() if k in ('ln_gamma', 'ln_beta', 'cheb_W', 'cheb_b', 'lin_W', 'lin_b')}
    del _L1_gnn_all

    def _L1_ffn_setup():
        import jax, jax.numpy as jnp
        import numpy as np
        B, S, D, H, E = (4, 64, 512, 1024, 8)
        key = jax.random.key(seed)
        ks = jax.random.split(key, 4)
        x = jax.random.normal(ks[0], (B, S, D), jnp.float32)
        Wr = jax.random.normal(ks[1], (E, D), jnp.float32) * 0.02
        br = jnp.zeros((E,), jnp.float32)
        W1 = jax.random.normal(ks[2], (E, D, H), jnp.float32) * 0.02
        b1 = jnp.zeros((E, H), jnp.float32)
        W2 = jax.random.normal(ks[3], (E, H, D), jnp.float32) * 0.02
        b2 = jnp.zeros((E, D), jnp.float32)
        return {'x': x, 'Wr': Wr, 'br': br, 'W1': W1, 'b1': b1, 'W2': W2, 'b2': b2}
    _L1_ffn_all = _L1_ffn_setup()
    _L1_ffn_in = {k: v for k, v in _L1_ffn_all.items() if k in ('Wr', 'br', 'W1', 'b1', 'W2', 'b2')}
    del _L1_ffn_all
    return {'x': x, 'src': src, 'dst': dst, 'edge_attr_16': edge_attr_16, 'edge_weight': edge_weight, 'L0_gnn_Wq': _L0_gnn_in['Wq'], 'L0_gnn_bq': _L0_gnn_in['bq'], 'L0_gnn_Wk': _L0_gnn_in['Wk'], 'L0_gnn_bk': _L0_gnn_in['bk'], 'L0_gnn_Wv': _L0_gnn_in['Wv'], 'L0_gnn_bv': _L0_gnn_in['bv'], 'L0_gnn_Wo': _L0_gnn_in['Wo'], 'L0_gnn_bo': _L0_gnn_in['bo'], 'L0_gnn_We': _L0_gnn_in['We'], 'L0_gnn_be': _L0_gnn_in['be'], 'L0_ffn_router_w': _L0_ffn_in['router_w'], 'L0_ffn_router_b': _L0_ffn_in['router_b'], 'L0_ffn_gate_up_proj': _L0_ffn_in['gate_up_proj'], 'L0_ffn_gate_up_proj_bias': _L0_ffn_in['gate_up_proj_bias'], 'L0_ffn_down_proj': _L0_ffn_in['down_proj'], 'L0_ffn_down_proj_bias': _L0_ffn_in['down_proj_bias'], 'L1_gnn_ln_gamma': _L1_gnn_in['ln_gamma'], 'L1_gnn_ln_beta': _L1_gnn_in['ln_beta'], 'L1_gnn_cheb_W': _L1_gnn_in['cheb_W'], 'L1_gnn_cheb_b': _L1_gnn_in['cheb_b'], 'L1_gnn_lin_W': _L1_gnn_in['lin_W'], 'L1_gnn_lin_b': _L1_gnn_in['lin_b'], 'L1_ffn_Wr': _L1_ffn_in['Wr'], 'L1_ffn_br': _L1_ffn_in['br'], 'L1_ffn_W1': _L1_ffn_in['W1'], 'L1_ffn_b1': _L1_ffn_in['b1'], 'L1_ffn_W2': _L1_ffn_in['W2'], 'L1_ffn_b2': _L1_ffn_in['b2']}

def reference(x, src, dst, edge_attr_16, edge_weight, L0_gnn_Wq, L0_gnn_bq, L0_gnn_Wk, L0_gnn_bk, L0_gnn_Wv, L0_gnn_bv, L0_gnn_Wo, L0_gnn_bo, L0_gnn_We, L0_gnn_be, L0_ffn_router_w, L0_ffn_router_b, L0_ffn_gate_up_proj, L0_ffn_gate_up_proj_bias, L0_ffn_down_proj, L0_ffn_down_proj_bias, L1_gnn_ln_gamma, L1_gnn_ln_beta, L1_gnn_cheb_W, L1_gnn_cheb_b, L1_gnn_lin_W, L1_gnn_lin_b, L1_ffn_Wr, L1_ffn_br, L1_ffn_W1, L1_ffn_b1, L1_ffn_W2, L1_ffn_b2):
    import jax
    import jax.numpy as jnp

    def _L0_gnn_ref(x, batch, edge_index, edge_attr, Wq, bq, Wk, bk, Wv, bv, Wo, bo, We, be, num_graphs):
        import jax, jax.numpy as jnp
        import numpy as np
        B = 32
        N = 512
        HID = 512
        H = 8
        E = 8192
        ED = 16
        n_total, hid = x.shape
        n = n_total // num_graphs
        hd = hid // H
        scale = 1.0 / jnp.sqrt(jnp.asarray(hd, x.dtype))
        q = (x @ Wq + bq).reshape(num_graphs, n, H, hd)
        k = (x @ Wk + bk).reshape(num_graphs, n, H, hd)
        v = (x @ Wv + bv).reshape(num_graphs, n, H, hd)
        attn = jnp.einsum('bnhd,bmhd->bnmh', q, k) * scale
        eb = edge_attr @ We + be
        b_idx = edge_index[0] // n
        loc_src = edge_index[0] % n
        loc_dst = edge_index[1] % n
        attn = attn.at[b_idx, loc_src, loc_dst].add(eb)
        attn = jax.nn.softmax(attn, axis=2)
        out = jnp.einsum('bnmh,bmhd->bnhd', attn, v).reshape(n_total, hid)
        return out @ Wo + bo

    def _L0_ffn_ref(hidden_states, router_w, router_b, gate_up_proj, gate_up_proj_bias, down_proj, down_proj_bias):
        import jax, jax.numpy as jnp
        import numpy as np
        TOP_K = 2

        def quick_gelu(x):
            return x * jax.nn.sigmoid(1.702 * x)
        B, S, H = hidden_states.shape
        E = router_b.shape[0]
        x = hidden_states.reshape(-1, H)
        T = x.shape[0]
        logits = x @ router_w + router_b
        top_w, sel = jax.lax.top_k(logits, TOP_K)
        top_w = jax.nn.softmax(top_w, axis=-1)
        tok_w = jnp.zeros((T, E), x.dtype).at[jnp.arange(T)[:, None], sel].add(top_w)

        def body(acc, params):
            Wgu, bgu, Wd, bd, w_e = params
            gu = x @ Wgu + bgu
            gate, up = jnp.split(gu, 2, axis=-1)
            act = (up + 1.0) * quick_gelu(gate)
            out = act @ Wd + bd
            return (acc + out * w_e[:, None], None)
        acc0 = jnp.zeros((T, H), x.dtype)
        acc, _ = jax.lax.scan(body, acc0, (gate_up_proj, gate_up_proj_bias, down_proj, down_proj_bias, tok_w.T))
        return acc.reshape(B, S, H)

    def _L1_gnn_ref(x, edge_index, edge_weight, ln_gamma, ln_beta, cheb_W, cheb_b, lin_W, lin_b):
        import jax, jax.numpy as jnp
        import numpy as np
        N, E, D, K = (625, 5000, 512, 5)
        n = x.shape[0]
        mu = jnp.mean(x, axis=-1, keepdims=True)
        var = jnp.mean((x - mu) ** 2, axis=-1, keepdims=True)
        xn = (x - mu) * jax.lax.rsqrt(var + 1e-05) * ln_gamma + ln_beta
        row, col = (edge_index[0], edge_index[1])
        deg = jax.ops.segment_sum(edge_weight, row, num_segments=n)
        dinv = jnp.where(deg > 0, jax.lax.rsqrt(jnp.where(deg > 0, deg, 1.0)), 0.0)
        norm_w = -dinv[row] * edge_weight * dinv[col]

        def prop(h):
            return jax.ops.segment_sum(norm_w[:, None] * h[row], col, num_segments=n)
        Tx0 = xn
        out = jnp.einsum('nd,fd->nf', Tx0, cheb_W[0])
        Tx1 = prop(Tx0)
        out = out + jnp.einsum('nd,fd->nf', Tx1, cheb_W[1])
        for k in range(2, cheb_W.shape[0]):
            Tx2 = 2.0 * prop(Tx1) - Tx0
            out = out + jnp.einsum('nd,fd->nf', Tx2, cheb_W[k])
            Tx0, Tx1 = (Tx1, Tx2)
        out = out + cheb_b
        x_graph = jnp.where(out >= 0, out, 0.01 * out)
        return xn @ lin_W.T + lin_b + x_graph

    def _L1_ffn_ref(x, Wr, br, W1, b1, W2, b2):
        import jax, jax.numpy as jnp
        import numpy as np
        B, S, D, H, E = (4, 64, 512, 1024, 8)
        b, s, d = x.shape
        n = b * s
        e = Wr.shape[0]
        xf = x.reshape(n, d)
        logits = xf @ Wr.T + br
        probs = jax.nn.softmax(logits, axis=-1)
        top2_prob, top2_idx = jax.lax.top_k(probs, 2)
        comb = jnp.zeros((n, e), x.dtype).at[jnp.arange(n)[:, None], top2_idx].add(top2_prob)
        h = jax.nn.gelu(jnp.einsum('nd,edh->enh', xf, W1) + b1[:, None, :], approximate=False)
        o = jnp.einsum('enh,ehd->end', h, W2) + b2[:, None, :]
        y = jnp.einsum('ne,end->nd', comb, o)
        return y.reshape(b, s, d)
    edge_index = jnp.stack([src, dst])
    batch0 = jnp.zeros((512,), jnp.int32)
    x = x + _L0_gnn_ref(_layernorm(x, axis=-1), batch0, edge_index, edge_attr_16, L0_gnn_Wq, L0_gnn_bq, L0_gnn_Wk, L0_gnn_bk, L0_gnn_Wv, L0_gnn_bv, L0_gnn_Wo, L0_gnn_bo, L0_gnn_We, L0_gnn_be, 32)
    x = x + _L0_ffn_ref(_layernorm(x, axis=-1)[None], L0_ffn_router_w, L0_ffn_router_b, L0_ffn_gate_up_proj, L0_ffn_gate_up_proj_bias, L0_ffn_down_proj, L0_ffn_down_proj_bias)[0]
    x = x + _L1_gnn_ref(_layernorm(x, axis=-1), edge_index, edge_weight, L1_gnn_ln_gamma, L1_gnn_ln_beta, L1_gnn_cheb_W, L1_gnn_cheb_b, L1_gnn_lin_W, L1_gnn_lin_b)
    x = x + _L1_ffn_ref(_layernorm(x, axis=-1)[None], L1_ffn_Wr, L1_ffn_br, L1_ffn_W1, L1_ffn_b1, L1_ffn_W2, L1_ffn_b2)[0]
    return x

_drawn_inputs = setup_inputs


def setup_inputs(seed=0):
    import zlib

    import numpy as np

    out = dict(_drawn_inputs(seed))
    spreads = {'L0_gnn_bq': (0.0, 0.1),
     'L0_gnn_bk': (0.0, 0.8),
     'L0_gnn_bv': (0.0, 0.1),
     'L0_gnn_bo': (0.0, 0.1),
     'L0_gnn_be': (0.0, 0.1),
     'L0_ffn_router_b': (0.0, 0.1),
     'L0_ffn_gate_up_proj_bias': (0.0, 0.1),
     'L0_ffn_down_proj_bias': (0.0, 0.1),
     'L1_gnn_ln_gamma': (1.0, 0.2),
     'L1_gnn_ln_beta': (0.0, 0.1),
     'L1_gnn_cheb_b': (0.0, 0.1),
     'L1_gnn_lin_b': (0.0, 0.1),
     'L1_ffn_br': (0.0, 0.8),
     'L1_ffn_b1': (0.0, 0.8),
     'L1_ffn_b2': (0.0, 0.59)}
    factors = {}
    for name, (base, spread) in spreads.items():
        noise = np.random.default_rng([zlib.crc32(name.encode()), seed]).standard_normal(out[name].shape)
        drawn = base * np.exp(spread * noise) if base else spread * noise
        out[name] = jnp.asarray(drawn.astype(out[name].dtype))
    for name, factor in factors.items():
        out[name] = (out[name] * factor).astype(out[name].dtype)
    return out
```

```python
from contextlib import ExitStack

import concourse.bass as bass
from concourse import mybir
from concourse.alu_op_type import AluOpType as ALU

ACT = mybir.ActivationFunctionType
F32 = mybir.dt.float32
F16 = mybir.dt.float16
I32 = mybir.dt.int32
U32 = mybir.dt.uint32
AX_X = mybir.AxisListType.X

P = 128

X_SCALE = 16.0
W_SCALE = 256.0
XW_BACK = 1.0 / (X_SCALE * W_SCALE)
EDGE_SCALE = 4096.0
EB_SCALE = 64.0
LAP_SCALE = 64.0
B_SCALE = 64.0
LN_EPS = 1e-5
QGELU = 1.702


class Chain:

    def __init__(self, eng, sem):
        self.eng, self.sem, self.base, self.k = eng, sem, 0, 0

    def link(self, ins):
        self.k += 1
        ins.then_inc(self.sem, 1)
        self.eng.wait_ge(self.sem, self.base + self.k)


def build_network(nc, a, out):
    N, D = a["x"].shape
    T = N // P
    K = D // P
    E_EDGES = a["src"].shape[0]
    C = E_EDGES // P
    ED, H = a["We"].shape
    HD = D // H
    NG = 32
    GN = N // NG
    GP = P // GN
    NE = a["router_b"].shape[0]
    I0 = a["down"].shape[1]
    I1 = a["W2"].shape[1]
    J = I0 // P
    W = 64
    assert I1 == I0 and D == 512 and N == 512 and T == 4 and C % 8 == 0 and GN * H == P

    ctx = ExitStack()
    with ctx:
        def sb(name, shape, dt):
            return ctx.enter_context(nc.sbuf_tensor(name, shape, dt))

        def sem(name):
            return ctx.enter_context(nc.semaphore(name))

        KB = 256
        r_stage = sb("r_stage", [P, 24 * KB], F32)
        r_split = sb("r_split", [P, 48 * KB], F32)
        r_gnn = sb("r_gnn", [P, 48 * KB], F32)
        r_work = sb("r_work", [P, 28 * KB], F32)
        r_mid = sb("r_mid", [P, 16 * KB], F32)
        x_sb = sb("x_sb", [P, T, D], F32)
        r_xT = sb("r_xT", [P, 8 * KB], F32)
        r_lap = sb("r_lap", [P, 8 * KB], F32)

        def view(region, start_kb, n, dt, pattern=None, **sizes):
            per = 2 if dt == F16 else 1
            ap = region[:, int(start_kb * KB):int(start_kb * KB) + n // per]
            if dt != F32:
                ap = ap.bitcast(dt)
            return ap.rearrange(pattern, **sizes) if pattern else ap

        xT_hi = view(r_xT, 0, K * N, F16, "p (k n) -> p k n", k=K)
        xT_lo = view(r_xT, 4, K * N, F16, "p (k n) -> p k n", k=K)
        adj = view(r_split, 40, T * N, F32, "p (t n) -> p t n", t=T)
        lap_hi = view(r_lap, 0, T * N, F16, "p (t n) -> p t n", t=T)
        lap_lo = view(r_lap, 4, T * N, F16, "p (t n) -> p t n", t=T)

        attrT = view(r_work, 0, 4096, F32)
        xn = view(r_work, 16, T * D, F32, "p (t d) -> p t d", t=T)
        score_m = [view(r_work, 4 * b, H * P, F32, "p (h j k) -> p h j k", h=H, j=GP) for b in range(2)]
        w_raw = [view(r_split, 8 * m, K * D, F32) for m in range(4)]
        qT = view(r_split, 32, K * N, F32, "p (k n) -> p k n", k=K)
        kT = view(r_split, 40, K * N, F32, "p (k n) -> p k n", k=K)
        qkvo_hi = [view(r_gnn, 8 * m, K * D, F16, "p (k n) -> p k n", k=K) for m in range(4)]
        qkvo_lo = [view(r_gnn, 8 * m + 4, K * D, F16, "p (k n) -> p k n", k=K) for m in range(4)]
        v_sb = view(r_mid, 0, T * D, F32, "p (t d) -> p t d", t=T)
        score = view(r_mid, 8, T * P, F32, "p (t k h) -> p t k h", t=T, k=GN)
        iota_i = view(r_mid, 10, N, F32).bitcast(I32)
        eb_f = view(r_mid, 12, C * H, F32, "p (c h) -> p c h", h=H)
        dl_hot = view(r_gnn, 32, C * GN, F16, "p (c g) -> p c g", g=GN)
        eb_hi = view(r_gnn, 36, C * H, F16, "p (c h) -> p c h", h=H)
        eb_lo = view(r_gnn, 38, C * H, F16, "p (c h) -> p c h", h=H)
        bv_bc = view(r_gnn, 40, D, F32)
        bo_bc = view(r_gnn, 42, D, F32)
        we_sb = view(r_gnn, 44, H, F32)
        be_bc = view(r_gnn, 45, H, F32)
        src_i = view(r_gnn, 46, C, F32).bitcast(I32)
        dst_i = view(r_gnn, 46.5, C, F32).bitcast(I32)
        w_f = view(r_gnn, 47, C, F32)
        src_r = view(r_mid, 8, P, F32)
        dst_r = view(r_mid, 8.5, P, F32)
        rel_r = view(r_mid, 9, P, F32)

        GC = 4
        src_hot = [view(r_work, 14 * b, GC * N, F16, "p (c n) -> p c n", c=GC) for b in range(2)]
        dst_hi = [view(r_work, 14 * b + 4, GC * N, F16, "p (c n) -> p c n", c=GC) for b in range(2)]
        dst_lo = [view(r_work, 14 * b + 8, GC * N, F16, "p (c n) -> p c n", c=GC) for b in range(2)]
        ebd = [view(r_work, 14 * b + 12, GC * 2 * P, F16, "p (c s q) -> p c s q", c=GC, s=2) for b in range(2)]

        prob = [view(r_work, 4 * b, H * P, F32, "p (h j k) -> p h j k", h=H, j=GP) for b in range(2)]
        probT = [view(r_work, 8 + 4 * b, H * P, F32, "p (h q) -> p h q", h=H) for b in range(2)]
        oT_hi = [view(r_work, 16 + 2 * b, K * P, F16, "p (k n) -> p k n", k=K) for b in range(2)]
        oT_lo = [view(r_work, 17 + 2 * b, K * P, F16, "p (k n) -> p k n", k=K) for b in range(2)]
        lap_f = [view(r_work, 20 + 2 * t, N, F32) for t in range(T)]

        sg_b = [view(r_work, 2 * b, N, F32) for b in range(2)]
        up_b = [view(r_work, 4 + 2 * b, N, F32) for b in range(2)]
        ga_b = [view(r_work, 8 + 2 * b, N, F32) for b in range(2)]
        ac_b = [view(r_work, 12 + 2 * b, N, F32) for b in range(2)]
        ah_b = [view(r_work, 16 + b, N, F16) for b in range(4)]
        al_b = [view(r_work, 20 + b, N, F16) for b in range(4)]

        cheb_raw = view(r_mid, 0, K * D, F32, "p (k n) -> p k n", k=K)
        cheb_all = r_gnn[:, :].bitcast(F16)
        bk = [view(r_mid, 8 * b, T * D, F32, "p (t d) -> p t d", t=T) for b in range(2)]
        bk_hi = view(r_work, 0, T * D, F16, "p (t d) -> p t d", t=T)
        bk_lo = view(r_work, 4, T * D, F16, "p (t d) -> p t d", t=T)
        xT_f = [view(r_work, 2 * k, N, F32) for k in range(K)]
        out_t = [view(r_work, 16 + 2 * t, D, F32) for t in range(T)]

        iota_n = sb("iota_n", [P, N], F16)
        ident = sb("ident", [P, P], F32)
        ones = sb("ones", [P, P], F32)
        diag = sb("diag", [P, T, P], F32)
        mask = sb("mask", [P, GP], F32)
        iota_e = sb("iota_e", [P, 8], F32)
        zeros = sb("zeros", [P, P], F16)
        span = sb("span", [C, 3], F32)
        base_i = view(r_lap, 3, C, F32)[0:1, :].bitcast(I32)
        flag_f = sb("flag_f", [1, 2], F32)
        flag_i = sb("flag_i", [1, 1], I32)
        dst_rel = view(r_lap, 2, C, F32)
        src_f = view(r_lap, 0, C, F32)
        dst_f = view(r_lap, 0.5, C, F32)
        dl_h = view(r_lap, 2.5, C, F16)
        w_hi = view(r_lap, 1, C, F32)
        w_lo = view(r_lap, 1.5, C, F32)
        w_h16 = view(r_lap, 2.75, C, F16)
        neg_half = sb("neg_half", [P, T], F32)
        stats = sb("stats", [P, T, 6], F32)
        mv = sb("mv", [P, T, 2], F32)
        var_eps = sb("var_eps", [P, T], F32)
        rstd = sb("rstd", [P, T], F32)
        hmax = sb("hmax", [P, T, H], F32)
        hsum = sb("hsum", [P, T, H], F32)
        deg = sb("deg", [P, T], F32)
        has = sb("has", [P, T], F32)
        ndinv = sb("ndinv", [P, T], F32)
        dinv = sb("dinv", [P, T], F32)
        cols = sb("cols", [P, 4, K], F32)
        rows = [view(r_mid, 0.5 * i, P, F32) for i in range(2)]
        cb_bc = sb("cb_bc", [P, D], F32)
        lb_bc = sb("lb_bc", [P, D], F32)
        rt_raw = [sb(f"rt_raw{f}", [P, K, NE], F32) for f in range(2)]
        rt_hi = [sb(f"rt_hi{f}", [P, K, NE], F16) for f in range(2)]
        rt_lo = [sb(f"rt_lo{f}", [P, K, NE], F16) for f in range(2)]
        rt_b = [sb(f"rt_b{f}", [P, NE], F32) for f in range(2)]
        b_in = [sb("b_in0", [P, NE, 2 * J], F32), sb("b_in1", [P, NE, J], F32)]
        b_sig = sb("b_sig", [P, NE, J], F32)
        b_out = [sb(f"b_out{f}", [NE, D], F32) for f in range(2)]
        logit = sb("logit", [P, T, NE], F32)
        rsum = sb("rsum", [P, T], F32)
        rmax = sb("rmax", [P, T], F32)
        top = sb("top", [P, T, 8], F32)
        top_i = sb("top_i", [P, T, 8], U32)
        top_f = sb("top_f", [P, T, 8], F32)
        tw = sb("tw", [P, T, 2], F32)
        pick = sb("pick", [P, 2, T, NE], F32)
        comb = sb("comb", [P, T, NE], F32)
        comb_s = sb("comb_s", [P, T, NE], F32)
        combT = view(r_work, 24, N, F32)[0:NE, :]

        pb = [ctx.enter_context(nc.psum_tensor(f"pb{i}", [P, 512], F32)) for i in range(8)]

        rows_psum = sem("rows_psum")
        rows_read = sem("rows_read")
        x_in = sem("x_in")
        edges_in = sem("edges_in")
        edge_rows = sem("edge_rows")
        edge_cols = sem("edge_cols")
        base_ready = sem("base_ready")
        attr_in = sem("attr_in")
        wraw_in = [sem(f"wraw_in{m}") for m in range(4)]
        small_in = sem("small_in")
        tables = sem("tables")
        iota_step = sem("iota_step")
        dch = sem("dve_chain")
        ach = sem("act_chain")
        var_ready = sem("var_ready")
        rstd_ready = sem("rstd_ready")
        xn_ready = sem("xn_ready")
        eb_psum = sem("eb_psum")
        eb_read = sem("eb_read")
        xt_psum = sem("xt_psum")
        xf_ready = sem("xf_ready")
        xhi_ready = sem("xhi_ready")
        xlo_ready = sem("xlo_ready")
        qw_hi = sem("qw_hi")
        qw_lo = sem("qw_lo")
        qk_psum = sem("qk_psum")
        qk_ready = sem("qk_ready")
        v_psum = sem("v_psum")
        v_ready = sem("v_ready")
        score_psum = sem("score_psum")
        score_read = sem("score_read")
        hot_ready = sem("hot_ready")
        hot_used = sem("hot_used")
        scatter_psum = sem("scatter_psum")
        adj_ready = sem("adj_ready")
        bias_read = sem("bias_read")
        logits_ready = sem("logits_ready")
        exp_ready = sem("exp_ready")
        prob_ready = sem("prob_ready")
        probT_psum = sem("probT_psum")
        probT_ready = sem("probT_ready")
        o_psum = sem("o_psum")
        ohi_ready = sem("ohi_ready")
        olo_ready = sem("olo_ready")
        proj_psum = sem("proj_psum")
        x1_ready = sem("x1_ready")
        deg_ready = sem("deg_ready")
        dinv_pow = sem("dinv_pow")
        diag_ready = sem("diag_ready")
        dinv_psum = sem("dinv_psum")
        lapf_ready = sem("lapf_ready")
        laphi_ready = sem("laphi_ready")
        laplo_ready = sem("laplo_ready")
        rt_split = sem("rt_split")
        rt_split_lo = sem("rt_split_lo")
        rt_psum = sem("rt_psum")
        rt_logit = sem("rt_logit")
        rt_exp = sem("rt_exp")
        comb_ready = sem("comb_ready")
        combT_psum = sem("combT_psum")
        combT_ready = sem("combT_ready")
        bout_psum = sem("bout_psum")
        cheb_in = sem("cheb_in")
        cheb_hi = sem("cheb_hi")
        cheb_lo = sem("cheb_lo")
        term_psum = sem("term_psum")
        term_ready = sem("term_ready")
        bhi_ready = sem("bhi_ready")
        blo_ready = sem("blo_ready")
        lin_psum = sem("lin_psum")
        out_done = sem("out_done")

        class Expert:

            def __init__(self, f):
                self.f = f
                self.parts = 2 - f
                self.pair = (self.parts * K * 2 * P) + 2 * D
                self.w_in = [sem(f"f{f}_w_in{b}") for b in range(2)]
                self.whi = sem(f"f{f}_whi_ready")
                self.wlo = sem(f"f{f}_wlo_ready")
                self.hid_psum = sem(f"f{f}_hid_psum")
                self.sig = sem(f"f{f}_sig_ready")
                self.up = sem(f"f{f}_up_ready")
                self.gated = sem(f"f{f}_gated_ready")
                self.act = sem(f"f{f}_act_ready")
                self.ahi = sem(f"f{f}_ahi_ready")
                self.alo = sem(f"f{f}_alo_ready")
                self.down = sem(f"f{f}_down_done")
                self.o_read = sem(f"f{f}_out_read")

            def stage(self, b):
                return view(r_stage, 12 * b, self.pair, F32)

            def hi(self, slot):
                return view(r_split, 12 * slot, self.pair, F16)

            def lo(self, slot):
                return view(r_split, 12 * slot + 6, self.pair, F16)

            def hid_w(self, ap, part, k, jo):
                o = part * K * 2 * P + k * 2 * P + jo * P
                return ap[:, o:o + P]

            def out_w(self, ap, jo):
                o = self.parts * K * 2 * P + jo * D
                return ap[:, o:o + D]

        ex = [Expert(0), Expert(1)]
        PAIRS = J // 2
        AHEAD = 2
        LAG = 2

        block = ctx.enter_context(nc.Block())

        def bc(ap, pos, n):
            shape = list(ap.shape)
            u = ap.unsqueeze(pos)
            shape.insert(pos, n)
            return u.to_broadcast(shape)


        def at_expert(ap, e, col):
            return ap[:, bass.ds(e, 1), col:col + 1].rearrange("p e c -> p (e c)")

        def at_tile(ap, t, e):
            return ap[:, t:t + 1, bass.ds(e, 1)].rearrange("p t e -> p (t e)")

        def cheb_at(m, k, part):
            o = (m * 2 + part) * (K * D) + k * D
            return cheb_all[:, o:o + D]

        def cheb_part(m, k, part):
            return cheb_all[:, bass.ds(m * (2 * K * D) + (part * K * D + k * D), D)]

        @block.sync
        def _(sp):
            sp.dma_start(x_sb[:, :, :], a["x"].rearrange("(t p) d -> p t d", p=P)).then_inc(x_in, 16)
            for dst, name in ((src_i, "src"), (dst_i, "dst"), (w_f, "edge_weight")):
                sp.dma_start(dst, a[name].rearrange("(c p) -> c p", p=P)).then_inc(edges_in, 16)
            for g in range(4):
                sp.dma_start(attrT[32 * g:32 * g + ED, :], a["attrT"][g]).then_inc(attr_in, 16)
                sp.dma_start(we_sb[32 * g:32 * g + ED, :], a["We"]).then_inc(attr_in, 16)
            for m, name in enumerate(("Wq", "Wk", "Wv", "Wo")):
                sp.dma_start(w_raw[m].rearrange("p (k n) -> p k n", k=K),
                             a[name].rearrange("(k p) n -> p k n", p=P)).then_inc(wraw_in[m], 16)

            def load_pair(f, e, q):
                x, st, n = ex[f], ex[f].stage(q % 2), 2 * P
                if f == 0:
                    into = [a["gate_up"][:, :, i * I0:(i + 1) * I0] for i in range(2)]
                    down = a["down"]
                else:
                    into, down = [a["W1"]], a["W2"]
                for part, s in enumerate(into):
                    o = part * K * n
                    s = s.rearrange("e (k p) i -> p e k i", p=P)
                    sp.dma_start(st[:, o:o + K * n].rearrange("p (k i) -> p k i", k=K),
                                 s[:, bass.ds(e, 1), :, q * n:(q + 1) * n].rearrange("p e k i -> p (e k) i"))\
                        .then_inc(x.w_in[q % 2], 16)
                o = x.parts * K * n
                down = down.rearrange("e (j p) d -> p e j d", p=P)
                sp.dma_start(st[:, o:o + 2 * D].rearrange("p (j d) -> p j d", j=2),
                             down[:, bass.ds(e, 1), 2 * q:2 * q + 2, :].rearrange("p e j d -> p (e j) d"))\
                    .then_inc(x.w_in[q % 2], 16)

            def stage_free(f, n):
                sp.wait_ge(ex[f].whi, 2 * (n - 1))
                sp.wait_ge(ex[f].wlo, 2 * (n - 1))

            for f in range(2):
                if f == 1:
                    sp.wait_ge(ex[0].whi, 2 * PAIRS * NE)
                    sp.wait_ge(ex[0].wlo, 2 * PAIRS * NE)
                for q in range(PAIRS):
                    if q >= 2:
                        stage_free(f, q)
                    load_pair(f, 0, q)
                if f == 0:
                    sp.wait_ge(o_psum, T)
                    sp.wait_ge(prob_ready, T)

                def load_expert(e, matrix):
                    for q in range(PAIRS):
                        stage_free(f, e * PAIRS + q)
                        load_pair(f, e, q)
                        if matrix and q == 1:
                            if not isinstance(e, int):
                                sp.wait_ge(cheb_hi, (e - 1) * K)
                                sp.wait_ge(cheb_lo, (e - 1) * K)
                            m = a["cheb_lin"].rearrange("m (k p) n -> p m k n", p=P)
                            sp.dma_start(cheb_raw, m[:, bass.ds(e - 1, 1), :, :].rearrange("p m k n -> p (m k) n"))\
                                .then_inc(cheb_in, 16)

                load_expert(1, f == 0)
                with sp.Fori(2, NE - 1) as e:
                    load_expert(e, f == 0)
                load_expert(NE - 1, False)
            for t in range(T):
                sp.wait_ge(ex[1].o_read, T * (NE - 1) + t + 1)
                sp.dma_start(out.rearrange("(t p) d -> p t d", p=P)[:, t, :], x_sb[:, t, :]).then_inc(out_done, 16)
            sp.wait_ge(out_done, 16 * T)

        @block.gpsimd
        def _(pool):
            nc.gpsimd.memset(ident[:, :], 0.0).then_inc(iota_step, 1)
            nc.gpsimd.memset(mask[:, :], 1.0).then_inc(iota_step, 1)
            nc.gpsimd.memset(zeros[:, :], 0.0).then_inc(tables, 1)
            nc.gpsimd.iota(iota_i, pattern=[[1, N]], base=0, channel_multiplier=0).then_inc(iota_step, 1)
            pool.wait_ge(iota_step, 3)
            nc.gpsimd.affine_select(out=ident[:, :], in_=ident[:, :], compare_op=ALU.not_equal, fill=1.0,
                                    base=0, pattern=[[-1, P]], channel_multiplier=1).then_inc(tables, 1)
            nc.gpsimd.affine_select(out=mask[:, :], in_=mask[:, :], compare_op=ALU.is_ge, fill=0.0,
                                    base=0, pattern=[[-GN, GP]], channel_multiplier=1).then_inc(iota_step, 1)
            pool.wait_ge(iota_step, 4)
            nc.gpsimd.affine_select(out=mask[:, :], in_=mask[:, :], compare_op=ALU.is_ge, fill=0.0,
                                    base=GN - 1, pattern=[[GN, GP]], channel_multiplier=-1).then_inc(tables, 1)
            nc.gpsimd.tensor_copy(iota_n[:, :], iota_i).then_inc(tables, 1)
            nc.gpsimd.tensor_copy(iota_e[:, :], iota_i[:, 0:8]).then_inc(tables, 1)
            nc.gpsimd.memset(neg_half[:, :], -0.5).then_inc(tables, 1)
            nc.gpsimd.memset(ones[:, :], 1.0).then_inc(tables, 1)

            def inv_sqrt(n):
                pool.wait_ge(var_ready, n + 1)
                nc.gpsimd.tensor_tensor(rstd[:, :], var_eps[:, :], neg_half[:, :], ALU.pow).then_inc(rstd_ready, 1)

            pool.wait_ge(tables, 7)
            inv_sqrt(0)
            pool.wait_ge(deg_ready, 1)
            nc.gpsimd.tensor_tensor(dinv[:, :], deg[:, :], neg_half[:, :], ALU.pow).then_inc(dinv_pow, 1)
            for n in range(1, 5):
                inv_sqrt(n)

        @block.scalar
        def _(act):
            ch = Chain(act, ach)
            rows1 = [("b1", 0, NE * J), ("bq", NE * J, K), ("bk", NE * J + K, K),
                     ("gamma", NE * J + 2 * K, K), ("beta", NE * J + 3 * K, K)]
            act.dma_start(rows[0][:, :], a["gate_up_bias"].rearrange("e (j p) -> (e j) p", p=P)).then_inc(small_in, 16)
            for name, r, n in rows1:
                s = a[name].rearrange("e (j p) -> (e j) p" if name == "b1" else "(j p) -> j p", p=P)
                act.dma_start(rows[1][r:r + n, :], s).then_inc(small_in, 16)
            for dst, name in ((bv_bc, "bv"), (bo_bc, "bo"), (be_bc, "be"), (cb_bc[:, :], "cheb_b"),
                              (lb_bc[:, :], "lin_b"), (rt_b[0][:, :], "router_b"), (rt_b[1][:, :], "br")):
                act.dma_start(dst, a[name].partition_broadcast(P)).then_inc(small_in, 16)
            for f, name in enumerate(("router_w", "WrT")):
                act.dma_start(rt_raw[f][:, :, :], a[name].rearrange("(k p) e -> p k e", p=P)).then_inc(small_in, 16)
            for f, name in enumerate(("down_bias", "b2")):
                act.dma_start(b_out[f][:, :], a[name]).then_inc(small_in, 16)

            def x_hi(n):
                for k in range(K):
                    act.wait_ge(xt_psum, K * n + k + 1)
                    nc.scalar.activation(xT_hi[:, k, :], pb[4 + k][:, :], ACT.Copy, scale=X_SCALE)\
                        .then_inc(xhi_ready, 1)

            def weight_hi(f, e, q, half, slot_free=None):
                x = ex[f]
                if half == 0:
                    act.wait_ge(x.w_in[q % 2], (e * (PAIRS // 2) + q // 2 + 1) * (16 * (x.parts + 1)))
                    if slot_free is not None:
                        act.wait_ge(x.down, slot_free * T)
                o, w = half * x.pair // 2, x.pair // 2
                nc.scalar.activation(x.hi(q % PAIRS)[:, o:o + w], x.stage(q % 2)[:, o:o + w], ACT.Copy,
                                     scale=W_SCALE).then_inc(x.whi, 1)

            for m in range(3):
                act.wait_ge(wraw_in[m], 16)
                nc.scalar.activation(qkvo_hi[m], w_raw[m].rearrange("p (k n) -> p k n", k=K), ACT.Copy,
                                     scale=W_SCALE).then_inc(qw_hi, 1)
                if m == 0:
                    x_hi(0)
            act.wait_ge(rows_read, 1)
            for i in range(2 * K):
                act.wait_ge(qk_psum, i + 1)
                dst, c = (qT, i) if i < K else (kT, i - K)
                nc.scalar.activation(dst[:, c, :], pb[i][:, :], ACT.Identity, bias=cols[:, i // K, c:c + 1],
                                     scale=XW_BACK).then_inc(qk_ready, 1)
            act.wait_ge(wraw_in[3], 16)
            nc.scalar.activation(qkvo_hi[3], w_raw[3].rearrange("p (k n) -> p k n", k=K), ACT.Copy,
                                 scale=W_SCALE).then_inc(qw_hi, 1)
            act.wait_ge(small_in, 16 * 17)
            for f in range(2):
                nc.scalar.activation(rt_hi[f][:, :, :], rt_raw[f][:, :, :], ACT.Copy, scale=W_SCALE)\
                    .then_inc(rt_split, 1)
            act.wait_ge(qw_lo, 4)
            for q in range(AHEAD):
                for half in range(2):
                    weight_hi(0, 0, q, half)

            act.wait_ge(scatter_psum, 1)
            act.wait_ge(score_psum, T)
            for t in range(T):
                nc.scalar.activation(adj[:, t, :], pb[t][:, :], ACT.Copy, scale=1.0 / EDGE_SCALE,
                                     accum_out=deg[:, t:t + 1]).then_inc(adj_ready, 1)
            act.wait_ge(logits_ready, 1)
            nc.scalar.activation(score, score, ACT.Exp).then_inc(exp_ready, 1)

            def prob_t(t):
                act.wait_ge(probT_psum, t + 1)
                if t >= 2:
                    act.wait_ge(o_psum, t - 1)
                b0 = 6 if t % 2 == 0 else 4
                for i in range(2):
                    nc.scalar.activation(probT[t % 2][:, 4 * i:4 * i + 4, :],
                                         pb[b0 + i][:, :].rearrange("p (h q) -> p h q", h=4), ACT.Copy)\
                        .then_inc(probT_ready, 1)

            def head_out(t):
                act.wait_ge(o_psum, t + 1)
                if t >= 2:
                    act.wait_ge(proj_psum, t - 1)
                nc.scalar.activation(oT_hi[t % 2], pb[t % 2][:, :].rearrange("p (k n) -> p k n", k=K), ACT.Copy,
                                     scale=X_SCALE).then_inc(ohi_ready, 1)

            for t in range(T + 1):
                if t < T:
                    prob_t(t)
                if t >= 1:
                    head_out(t - 1)

            x_hi(1)

            act.wait_ge(rt_logit, 2)
            nc.scalar.activation(tw[:, :, 1], rsum[:, :], ACT.Exp).then_inc(rt_exp, 1)
            for t in range(T):
                act.wait_ge(lapf_ready, t + 1)
                nc.scalar.activation(lap_hi[:, t, :], lap_f[t], ACT.Copy).then_inc(laphi_ready, 1)

            def expert_step(f, e, j, prepare, matrix):
                x, b, s = ex[f], j % 2, e * J + j
                first = isinstance(e, int) and e == 0
                act.wait_ge(x.hid_psum, s + 1)
                if f == 0:
                    if not (first and j < 2):
                        act.wait_ge(x.act, s - 1)
                    nc.scalar.activation(sg_b[b], pb[b][:, :], ACT.Sigmoid, bias=at_expert(b_sig, e, j),
                                         scale=QGELU * XW_BACK).then_inc(x.sig, 1)
                    nc.scalar.activation(up_b[b], pb[2 + b][:, :], ACT.Identity, bias=at_expert(b_in[0], e, J + j),
                                         scale=XW_BACK * X_SCALE * XW_BACK).then_inc(x.up, 1)
                else:
                    if not (first and j < 2):
                        act.wait_ge(x.alo, s - 1)
                    nc.scalar.activation(ac_b[b], pb[b][:, :], ACT.Gelu, bias=at_expert(b_in[1], e, j),
                                         scale=XW_BACK).then_inc(x.act, 1)
                if prepare:
                    q = j // 2 + AHEAD
                    if first and q < PAIRS:
                        if f == 0 and j == 0:
                            act.wait_ge(lapf_ready, T)
                        weight_hi(f, e, q, j % 2)
                    else:
                        weight_hi(f, e, q, j % 2, s - j % 2 - 2)
                if matrix and 2 <= j < 2 + K:
                    if j == 2:
                        act.wait_ge(cheb_in, e * 16)
                    nc.scalar.activation(cheb_part(e - 1, j - 2, 0), cheb_raw[:, j - 2, :], ACT.Copy,
                                         scale=W_SCALE).then_inc(cheb_hi, 1)
                act.wait_ge(x.act, s + 1)
                if not (first and j < 4):
                    act.wait_ge(x.down, (s - 3) * T)
                nc.scalar.activation(ah_b[j % 4], ac_b[b], ACT.Copy,
                                     scale=1.0 if f == 0 else X_SCALE).then_inc(x.ahi, 1)

            def experts(f):
                for j in range(J):
                    expert_step(f, 0, j, True, False)
                with act.Fori(1, NE - 1) as e:
                    for j in range(J):
                        expert_step(f, e, j, True, f == 0)
                for j in range(J):
                    expert_step(f, NE - 1, j, j // 2 + AHEAD < PAIRS, False)

            experts(0)

            for k in range(K):
                act.wait_ge(xt_psum, 2 * K + k + 1)
                nc.scalar.activation(xT_f[k], pb[4 + k][:, :], ACT.Identity, bias=cols[:, 3, k:k + 1],
                                     scale=cols[:, 2, k:k + 1]).then_inc(xf_ready, 1)
                act.wait_ge(xf_ready, k + 1)
                nc.scalar.activation(xT_hi[:, k, :], xT_f[k], ACT.Copy).then_inc(xhi_ready, 1)
            act.wait_ge(ex[0].down, NE * J * T)
            for q in range(AHEAD):
                for half in range(2):
                    weight_hi(1, 0, q, half)
            for i in range(4):
                for t in range(T):
                    act.wait_ge(term_ready, T * i + t + 1)
                    if i >= 1:
                        act.wait_ge(term_psum, T * (i + 1))
                    nc.scalar.activation(bk_hi[:, t, :], bk[i % 2][:, t, :], ACT.Copy,
                                         scale=B_SCALE if i < 3 else B_SCALE / 2).then_inc(bhi_ready, 1)
            x_hi(3)
            act.wait_ge(rt_logit, 4)
            nc.scalar.activation(logit[:, :, :], logit[:, :, :], ACT.Exp).then_inc(rt_exp, 1)
            experts(1)

        @block.vector
        def _(dve):
            ch = Chain(dve, dch)
            V = nc.vector

            def layernorm(n, dst):
                src = xn if n == 3 else x_sb
                for t in range(T):
                    ins = V.bn_stats(stats[:, t, :], src[:, t, :])
                    ch.link(ins)
                for t in range(T):
                    ch.link(V.bn_aggr(mv[:, t, :], stats[:, t, :]))
                V.tensor_scalar(var_eps[:, :], mv[:, :, 1], LN_EPS, None, ALU.add).then_inc(var_ready, 1)
                dve.wait_ge(rstd_ready, n + 1)
                for t in range(T):
                    V.tensor_scalar(dst[:, t, :], src[:, t, :], mv[:, t, 0:1], rstd[:, t:t + 1], ALU.subtract,
                                    ALU.mult).then_inc(xn_ready, 1)

            def x_lo(n):
                for k in range(K):
                    dve.wait_ge(xhi_ready, K * n + k + 1)
                    V.scalar_tensor_tensor(xT_lo[:, k, :], pb[4 + k][:, :], X_SCALE, xT_hi[:, k, :], ALU.mult,
                                           ALU.subtract).then_inc(xlo_ready, 1)

            def weight_lo(f, e, q, half):
                x = ex[f]
                dve.wait_ge(x.whi, (e * PAIRS + q) * 2 + half + 1)
                o, w = half * x.pair // 2, x.pair // 2
                V.scalar_tensor_tensor(x.lo(q % PAIRS)[:, o:o + w], x.stage(q % 2)[:, o:o + w], W_SCALE,
                                       x.hi(q % PAIRS)[:, o:o + w], ALU.mult, ALU.subtract).then_inc(x.wlo, 1)

            dve.wait_ge(x_in, 16)
            layernorm(0, xn)
            dve.wait_ge(edges_in, 48)
            dve.wait_ge(tables, 7)
            V.tensor_copy(src_r, src_i)
            ch.link(V.tensor_copy(dst_r, dst_i))
            V.tensor_reduce(span[:, 1:2], dst_r, AX_X, ALU.max)
            ch.link(V.tensor_reduce(span[:, 0:1], dst_r, AX_X, ALU.min))
            ch.link(V.tensor_scalar(span[:, 0:1], span[:, 0:1], float(N - W), None, ALU.min))
            V.tensor_tensor(span[:, 2:3], span[:, 1:2], span[:, 0:1], ALU.subtract)
            V.tensor_scalar(rel_r, dst_r, span[:, 0:1], None, ALU.subtract).then_inc(edge_rows, 1)
            dve.wait_ge(edge_cols, 1)
            V.tensor_copy(src_f[:, :], pb[5][:, 0:C])
            ch.link(V.tensor_copy(dst_f[:, :], pb[5][:, P:P + C]))
            V.tensor_copy(dst_rel[:, :], pb[5][:, 2 * P:2 * P + C])
            ch.link(V.tensor_scalar(w_lo[:, :], pb[5][:, 3 * P:3 * P + C], EDGE_SCALE, None, ALU.mult))
            V.tensor_copy(base_i[:, :], pb[6][0:1, 0:C])
            ch.link(V.tensor_reduce(flag_f[:, 0:1], pb[6][0:1, P:P + C], AX_X, ALU.max))
            ch.link(V.tensor_scalar(flag_f[:, 1:2], flag_f[:, 0:1], float(W), None, ALU.is_lt))
            V.tensor_copy(flag_i[:, :], flag_f[:, 1:2]).then_inc(base_ready, 1)
            ch.link(V.tensor_copy(w_h16[:, :], w_lo[:, :]))
            ch.link(V.tensor_copy(w_hi[:, :], w_h16[:, :]))
            ch.link(V.tensor_tensor(w_lo[:, :], w_lo[:, :], w_hi[:, :], ALU.subtract))
            ch.link(V.tensor_copy(dst_i, dst_f[:, :]))
            ch.link(V.tensor_scalar(dst_i, dst_i, GN - 1, None, ALU.bitwise_and))
            ch.link(V.tensor_copy(dl_h[:, :], dst_i))
            ch.link(V.tensor_tensor(dl_hot, bc(iota_n[:, 0:GN], 1, C), bc(dl_h[:, :], 2, GN), ALU.is_equal))
            dve.wait_ge(small_in, 16 * 17)
            dve.wait_ge(rows_psum, 2)
            n0, n1 = 2 * NE * J, NE * J
            cols0 = pb[4][:, 0:n0].rearrange("p (e j) -> p e j", e=NE)
            V.tensor_scalar(b_sig[:, :, :], cols0[:, :, 0:J], QGELU, None, ALU.mult)
            V.tensor_scalar(b_in[0][:, :, 0:J], cols0[:, :, 0:J], 1.0 / XW_BACK, None, ALU.mult)
            V.tensor_scalar(b_in[0][:, :, J:2 * J], cols0[:, :, J:2 * J], 1.0, X_SCALE * XW_BACK, ALU.add, ALU.mult)
            V.tensor_copy(b_in[1][:, :, :], pb[4][:, n0:n0 + n1].rearrange("p (e j) -> p e j", e=NE))
            V.tensor_copy(cols[:, 0:2, :], pb[4][:, n0 + n1:n0 + n1 + 2 * K].rearrange("p (v k) -> p v k", v=2))
            V.tensor_scalar(cols[:, 2:4, :], pb[4][:, n0 + n1 + 2 * K:n0 + n1 + 4 * K]
                            .rearrange("p (v k) -> p v k", v=2), X_SCALE, None, ALU.mult).then_inc(rows_read, 1)
            for g in range(4):
                dve.wait_ge(eb_psum, g + 1)
                V.tensor_tensor(eb_f[:, C // 4 * g:C // 4 * (g + 1), :],
                                pb[g][:, 0:C // 4 * H].rearrange("p (c h) -> p c h", h=H), bc(be_bc, 1, C // 4),
                                ALU.add).then_inc(eb_read, 1)
            dve.wait_ge(eb_read, 4)
            ch.link(V.tensor_scalar(eb_hi, eb_f, EB_SCALE, None, ALU.mult))
            ch.link(V.scalar_tensor_tensor(eb_lo, eb_f, EB_SCALE, eb_hi, ALU.mult, ALU.subtract))
            x_lo(0)

            def qkvo_lo_part(m):
                dve.wait_ge(qw_hi, m + 1)
                V.scalar_tensor_tensor(qkvo_lo[m].rearrange("p k n -> p (k n)"), w_raw[m], W_SCALE,
                                       qkvo_hi[m].rearrange("p k n -> p (k n)"), ALU.mult, ALU.subtract)\
                    .then_inc(qw_lo, 1)

            for m in range(3):
                qkvo_lo_part(m)
            for t in range(T):
                dve.wait_ge(v_psum, t + 1)
                V.scalar_tensor_tensor(v_sb[:, t, :], pb[t][:, :], XW_BACK, bv_bc, ALU.mult, ALU.add)\
                    .then_inc(v_ready, 1)
            for t in range(T):
                dve.wait_ge(score_psum, t + 1)
                for i in range(2):
                    ins = V.tensor_tensor(score_m[t % 2][:, i:H:2, :, :],
                                          pb[4 + 2 * (t % 2) + i][:, :].rearrange("p (h j k) -> p h j k", h=4, j=GP),
                                          bc(bc(mask[:, :], 1, 4), 3, GN), ALU.mult)
                    ins.then_inc(score_read, 1)
                dve.wait_ge(score_read, 2 * t + 2)
                ch.link(V.tensor_reduce(score[:, t, :, :].rearrange("p k h -> p h k"),
                                        score_m[t % 2].rearrange("p h j k -> p h k j"), AX_X, ALU.add))
            ch.link(V.tensor_tensor(x_sb[:, :, :], x_sb[:, :, :], bc(bo_bc, 1, T), ALU.add))
            qkvo_lo_part(3)
            for f in range(2):
                dve.wait_ge(rt_split, f + 1)
                V.scalar_tensor_tensor(rt_lo[f][:, :, :].rearrange("p k e -> p (k e)"),
                                       rt_raw[f][:, :, :].rearrange("p k e -> p (k e)"), W_SCALE,
                                       rt_hi[f][:, :, :].rearrange("p k e -> p (k e)"), ALU.mult, ALU.subtract)\
                    .then_inc(rt_split_lo, 1)

            def one_hots(i, b, free, windowed):
                if free:
                    dve.wait_ge(hot_used, i * 2 + (b - 1))
                n = W if windowed else N
                dst = dst_rel if windowed else dst_f
                for c in range(GC):
                    at = bass.ds(i * (2 * GC) + (b * GC + c), 1)
                    V.tensor_scalar(src_hot[b][:, c, :], iota_n[:, :], src_f[:, at], None, ALU.is_equal)
                    V.tensor_scalar(dst_hi[b][:, c, 0:n], iota_n[:, 0:n], dst[:, at], w_hi[:, at], ALU.is_equal,
                                    ALU.mult)
                    V.tensor_scalar(dst_lo[b][:, c, 0:n], iota_n[:, 0:n], dst[:, at], w_lo[:, at], ALU.is_equal,
                                    ALU.mult)
                at = bass.ds(i * (2 * GC) + b * GC, GC)
                for s, eb in enumerate((eb_hi, eb_lo)):
                    last = V.tensor_tensor(ebd[b][:, :, s, :].rearrange("p c (g h) -> p c g h", h=H),
                                           bc(dl_hot[:, at, :], 3, H), bc(eb[:, at, :], 2, GN), ALU.mult)
                last.then_inc(hot_ready, 1)

            def all_one_hots(windowed):
                one_hots(0, 0, False, windowed)
                one_hots(0, 1, False, windowed)
                with dve.Fori(1, C // (2 * GC)) as i:
                    one_hots(i, 0, True, windowed)
                    one_hots(i, 1, True, windowed)

            dve.wait_ge(score_psum, T)
            dve.wait_ge(base_ready, 1)
            narrow = dve.value_load(flag_i[0:1, 0:1], min_val=0, max_val=1)
            with dve.If(narrow):
                all_one_hots(True)
            with dve.Else():
                all_one_hots(False)
            for q in range(AHEAD):
                for half in range(2):
                    weight_lo(0, 0, q, half)

            dve.wait_ge(scatter_psum, 1)
            flat = score.rearrange("p t k h -> p t (k h)")
            ch.link(V.tensor_scalar(score, score, float(HD) ** -0.5, None, ALU.mult))
            for s in range(2):
                for i in range(2):
                    ins = V.scalar_tensor_tensor(
                        flat[:, 2 * i:2 * i + 2, :],
                        pb[4 + i][:, :].rearrange("p (t s q) -> p t s q", t=2, s=2)[:, :, s, :],
                        1.0 / EB_SCALE, flat[:, 2 * i:2 * i + 2, :], ALU.mult, ALU.add)
                    ch.link(ins)
            by_head = score.rearrange("p t k h -> p t h k")
            ch.link(V.tensor_reduce(hmax[:, :, :], by_head, AX_X, ALU.max))
            V.tensor_tensor(score, score, bc(hmax[:, :, :], 2, GN), ALU.subtract).then_inc(logits_ready, 1)
            dve.wait_ge(exp_ready, 1)
            ch.link(V.tensor_reduce(hsum[:, :, :], by_head, AX_X, ALU.add))
            ch.link(V.reciprocal(hsum[:, :, :], hsum[:, :, :]))
            ch.link(V.tensor_tensor(score, score, bc(hsum[:, :, :], 2, GN), ALU.mult))

            def spread(t):
                if t >= 2:
                    dve.wait_ge(probT_psum, t - 1)
                V.tensor_tensor(prob[t % 2], bc(score[:, t, :, :].rearrange("p k h -> p h k"), 2, GP),
                                bc(bc(mask[:, :], 1, H), 3, GN), ALU.mult).then_inc(prob_ready, 1)

            def head_lo(t):
                dve.wait_ge(ohi_ready, t + 1)
                V.scalar_tensor_tensor(oT_lo[t % 2].rearrange("p k n -> p (k n)"), pb[t % 2][:, :], X_SCALE,
                                       oT_hi[t % 2].rearrange("p k n -> p (k n)"), ALU.mult, ALU.subtract)\
                    .then_inc(olo_ready, 1)

            def project(t):
                dve.wait_ge(proj_psum, t + 1)
                ins = V.scalar_tensor_tensor(x_sb[:, t, :], pb[2 + t % 2][:, :], XW_BACK, x_sb[:, t, :], ALU.mult,
                                             ALU.add)
                ins.then_inc(x1_ready, 1)

            dve.wait_ge(adj_ready, T)
            ch.link(V.tensor_scalar(has[:, :], deg[:, :], 0.0, None, ALU.is_gt))
            ch.link(V.tensor_tensor(deg[:, :], deg[:, :], has[:, :], ALU.mult))
            ch.link(V.scalar_tensor_tensor(deg[:, :], has[:, :], -1.0, deg[:, :], ALU.mult, ALU.add))
            V.tensor_scalar(deg[:, :], deg[:, :], 1.0, None, ALU.add).then_inc(deg_ready, 1)

            for t in range(T + 2):
                if t < T:
                    spread(t)
                if 1 <= t <= T:
                    head_lo(t - 1)
                if t >= 2:
                    project(t - 2)
            dve.wait_ge(dinv_pow, 1)
            ch.link(V.tensor_tensor(dinv[:, :], dinv[:, :], has[:, :], ALU.mult))
            V.tensor_scalar(ndinv[:, :], dinv[:, :], -2.0 * LAP_SCALE, None, ALU.mult)
            for t in range(T):
                V.tensor_scalar(diag[:, t, :], ident[:, :], dinv[:, t:t + 1], None, ALU.mult).then_inc(diag_ready, 1)

            dve.wait_ge(x1_ready, T)
            layernorm(1, xn)
            x_lo(1)

            def choose(f):
                vals = logit
                for t in range(T):
                    ch.link(V.max(top[:, t, :], vals[:, t, :]))
                for t in range(T):
                    ch.link(V.max_index(top_i[:, t, :], top[:, t, :], vals[:, t, :]))
                ch.link(V.tensor_copy(top_f[:, :, :], top_i[:, :, :]))
                if f == 0:
                    V.tensor_tensor(rsum[:, :], top[:, :, 1], top[:, :, 0], ALU.subtract).then_inc(rt_logit, 1)
                    dve.wait_ge(rt_exp, 1)
                    ch.link(V.tensor_scalar(rsum[:, :], tw[:, :, 1], 1.0, None, ALU.add))
                    ch.link(V.reciprocal(tw[:, :, 0], rsum[:, :]))
                    ch.link(V.tensor_tensor(tw[:, :, 1], tw[:, :, 1], tw[:, :, 0], ALU.mult))
                else:
                    ch.link(V.tensor_copy(tw[:, :, :], top[:, :, 0:2]))
                for t in range(T):
                    for r in range(2):
                        ch.link(V.tensor_scalar(pick[:, r, t, :], iota_e[:, 0:NE], top_f[:, t, r:r + 1],
                                                tw[:, t, r:r + 1], ALU.is_equal, ALU.mult))
                ch.link(V.tensor_tensor(comb[:, :, :], pick[:, 0, :, :], pick[:, 1, :, :], ALU.add))
                V.tensor_scalar(comb_s[:, :, :], comb[:, :, :], XW_BACK, None, ALU.mult).then_inc(comb_ready, 1)

            def logits(f):
                dve.wait_ge(rt_psum, f + 1)
                V.scalar_tensor_tensor(logit[:, :, :], pb[2][:, 0:T * NE].rearrange("p (t e) -> p t e", t=T), XW_BACK,
                                       bc(rt_b[f][:, :], 1, T), ALU.mult, ALU.add).then_inc(rt_logit, 1)
                dve.wait_ge(rt_logit, 1 if f == 0 else 3)

            logits(0)
            choose(0)
            for t in range(T):
                dve.wait_ge(dinv_psum, T)
                V.scalar_tensor_tensor(lap_f[t], adj[:, t, :], ndinv[:, t:t + 1], pb[1][:, :], ALU.mult, ALU.mult)\
                    .then_inc(lapf_ready, 1)
            for t in range(T):
                dve.wait_ge(laphi_ready, t + 1)
                V.tensor_tensor(lap_lo[:, t, :], lap_f[t], lap_hi[:, t, :], ALU.subtract).then_inc(laplo_ready, 1)

            def add_output(f, e):
                x = ex[f]
                for t in range(T):
                    dve.wait_ge(x.down, e * (J * T) + ((J - 1) * T + t + 1))
                    V.scalar_tensor_tensor(x_sb[:, t, :], pb[4 + t][:, :], at_tile(comb_s, t, e), x_sb[:, t, :],
                                           ALU.mult, ALU.add).then_inc(x.o_read, 1)

            def expert_step(f, e, j, prepare, matrix):
                x, b, s = ex[f], j % 2, e * J + j
                first = isinstance(e, int) and e == 0
                if f == 0:
                    dve.wait_ge(x.sig, s + 1)
                    V.scalar_tensor_tensor(ga_b[b], pb[b][:, :], at_expert(b_in[0], e, j), sg_b[b], ALU.add, ALU.mult)\
                        .then_inc(x.gated, 1)
                    dve.wait_ge(x.up, s + 1)
                    dve.wait_ge(x.gated, s + 1)
                    V.tensor_tensor(ac_b[b], ga_b[b], up_b[b], ALU.mult).then_inc(x.act, 1)
                if prepare:
                    weight_lo(f, e, j // 2 + AHEAD, j % 2)
                if matrix and 2 <= j < 2 + K:
                    dve.wait_ge(cheb_hi, (e - 1) * K + (j - 1))
                    V.scalar_tensor_tensor(cheb_part(e - 1, j - 2, 1), cheb_raw[:, j - 2, :], W_SCALE,
                                           cheb_part(e - 1, j - 2, 0), ALU.mult, ALU.subtract).then_inc(cheb_lo, 1)
                dve.wait_ge(x.ahi, s + 1)
                if f == 0:
                    V.tensor_tensor(al_b[j % 4], ac_b[b], ah_b[j % 4], ALU.subtract).then_inc(x.alo, 1)
                else:
                    V.scalar_tensor_tensor(al_b[j % 4], ac_b[b], X_SCALE, ah_b[j % 4], ALU.mult, ALU.subtract)\
                        .then_inc(x.alo, 1)
                if j == LAG - 1 and not first:
                    add_output(f, e - 1)

            def experts(f):
                for j in range(J):
                    expert_step(f, 0, j, True, False)
                with dve.Fori(1, NE - 1) as e:
                    for j in range(J):
                        expert_step(f, e, j, True, f == 0)
                for j in range(J):
                    expert_step(f, NE - 1, j, j // 2 + AHEAD < PAIRS, False)
                dve.wait_ge(combT_psum, f + 1)
                V.tensor_copy(combT, pb[0][0:NE, :]).then_inc(combT_ready, 1)
                dve.wait_ge(ex[f].o_read, T * (NE - 1))
                for t in range(T):
                    dve.wait_ge(bout_psum, T * f + t + 1)
                    ch.link(V.tensor_tensor(x_sb[:, t, :], x_sb[:, t, :], pb[t][:, :], ALU.add))
                add_output(f, NE - 1)
                dve.wait_ge(ex[f].o_read, T * NE)

            experts(0)

            layernorm(2, xn)
            dve.wait_ge(xn_ready, 3 * T)
            layernorm(3, xn)
            for k in range(K):
                dve.wait_ge(xhi_ready, 2 * K + k + 1)
                V.tensor_tensor(xT_lo[:, k, :], xT_f[k], xT_hi[:, k, :], ALU.subtract).then_inc(xlo_ready, 1)
            for q in range(AHEAD):
                for half in range(2):
                    weight_lo(1, 0, q, half)

            def term(i, t):
                dve.wait_ge(term_psum, T * i + t + 1)
                p = pb[4 * (i % 2) + t][:, :]
                if i < 2:
                    ins = V.tensor_scalar(bk[i][:, t, :], p, XW_BACK, None, ALU.mult)
                else:
                    ins = V.scalar_tensor_tensor(bk[i % 2][:, t, :], p, XW_BACK, bk[i % 2][:, t, :], ALU.mult,
                                                 ALU.subtract)
                ins.then_inc(term_ready, 1)

            def term_lo(i, t):
                dve.wait_ge(bhi_ready, T * i + t + 1)
                V.scalar_tensor_tensor(bk_lo[:, t, :], bk[i % 2][:, t, :], B_SCALE if i < 3 else B_SCALE / 2,
                                       bk_hi[:, t, :], ALU.mult, ALU.subtract).then_inc(blo_ready, 1)

            for i in range(4):
                for t in range(T):
                    term(i, t)
                    if t >= 1:
                        term_lo(i, t - 1)
                term_lo(i, T - 1)
            for t in range(T):
                term(4, t)
            for t in range(T):
                dve.wait_ge(term_ready, 4 * T + t + 1)
                ch.link(V.tensor_tensor(out_t[t], bk[0][:, t, :], cb_bc[:, :], ALU.add))
                ch.link(V.scalar_tensor_tensor(out_t[t], out_t[t], 0.01, out_t[t], ALU.mult, ALU.max))
                ch.link(V.tensor_tensor(x_sb[:, t, :], x_sb[:, t, :], out_t[t], ALU.add))
                ch.link(V.tensor_tensor(x_sb[:, t, :], x_sb[:, t, :], lb_bc[:, :], ALU.add))
            for t in range(T):
                dve.wait_ge(lin_psum, t + 1)
                ch.link(V.scalar_tensor_tensor(x_sb[:, t, :], pb[4 + t][:, :], XW_BACK, x_sb[:, t, :], ALU.mult,
                                               ALU.add))

            layernorm(4, xn)
            x_lo(3)
            logits(1)
            for t in range(T):
                ch.link(V.tensor_reduce(rmax[:, t:t + 1], logit[:, t, :], AX_X, ALU.max))
            V.tensor_tensor(logit[:, :, :], logit[:, :, :], bc(rmax[:, :], 2, NE), ALU.subtract).then_inc(rt_logit, 1)
            dve.wait_ge(rt_exp, 2)
            ch.link(V.tensor_reduce(rsum[:, :], logit[:, :, :], AX_X, ALU.add))
            ch.link(V.reciprocal(rsum[:, :], rsum[:, :]))
            ch.link(V.tensor_tensor(logit[:, :, :], logit[:, :, :], bc(rsum[:, :], 2, NE), ALU.mult))
            choose(1)
            experts(1)

        @block.tensor
        def _(pe):
            MM = nc.tensor.matmul

            def mm3(o, sh, sl, mh, ml, start, stop):
                MM(o, sh, mh, start=start, stop=False)
                MM(o, sh, ml, start=False, stop=False)
                return MM(o, sl, mh, start=False, stop=stop)

            def transpose_x(n):
                for k in range(K):
                    for t in range(T):
                        pe.wait_ge(xn_ready, T * (n if n < 2 else n + 1) + t + 1)
                        last = nc.tensor.transpose(pb[4 + k][:, t * P:(t + 1) * P], xn[:, t, k * P:(k + 1) * P],
                                                   ident[:, :])
                    last.then_inc(xt_psum, 1)

            def x_split(n):
                pe.wait_ge(xhi_ready, K * (n + 1))
                pe.wait_ge(xlo_ready, K * (n + 1))

            pe.wait_ge(tables, 7)
            pe.wait_ge(small_in, 16 * 17)
            nr = NE * J + 4 * K
            nc.tensor.transpose(pb[4][:, 0:P], rows[0][:, :], ident[:, :]).then_inc(rows_psum, 1)
            nc.tensor.transpose(pb[4][:, P:P + nr], rows[1][0:nr, :], ident[0:nr, 0:nr]).then_inc(rows_psum, 1)

            pe.wait_ge(edge_rows, 1)
            for n, r in enumerate((src_r, dst_r, rel_r, w_f)):
                nc.tensor.transpose(pb[5][:, n * P:n * P + C], r, ident[:, :])
            nc.tensor.transpose(pb[6][0:1, 0:C], span[:, 0:1], ident[:, :])
            nc.tensor.transpose(pb[6][0:1, P:P + C], span[:, 2:3], ident[:, :]).then_inc(edge_cols, 1)

            pe.wait_ge(attr_in, 16 * 8)
            for g in range(4):
                for c in range(C // 4):
                    last = MM(pb[g][:, c * H:(c + 1) * H], attrT[32 * g:32 * g + ED, c * P:(c + 1) * P],
                              we_sb[32 * g:32 * g + ED, :], start=True, stop=True)
                last.then_inc(eb_psum, 1)

            pe.wait_ge(rows_read, 1)
            pe.wait_ge(base_ready, 1)
            transpose_x(0)
            x_split(0)
            pe.wait_ge(eb_read, 4)
            for m in range(2):
                pe.wait_ge(qw_hi, m + 1)
                pe.wait_ge(qw_lo, m + 1)
                for c in range(K):
                    for k in range(K):
                        at = slice(c * P, (c + 1) * P)
                        last = mm3(pb[4 * m + c][:, :], qkvo_hi[m][:, k, at], qkvo_lo[m][:, k, at],
                                   xT_hi[:, k, :], xT_lo[:, k, :], k == 0, k == K - 1)
                    last.then_inc(qk_psum, 1)
            pe.wait_ge(qw_hi, 3)
            pe.wait_ge(qw_lo, 3)
            for t in range(T):
                pe.wait_ge(qk_ready, t + 1)
                at = slice(t * P, (t + 1) * P)
                for k in range(K):
                    last = mm3(pb[t][:, :], xT_hi[:, k, at], xT_lo[:, k, at], qkvo_hi[2][:, k, :],
                               qkvo_lo[2][:, k, :], k == 0, k == K - 1)
                last.then_inc(v_psum, 1)
            pe.wait_ge(qk_ready, 2 * K)
            for t in range(T):
                if t >= 2:
                    pe.wait_ge(score_read, 2 * (t - 1))
                at = slice(t * P, (t + 1) * P)
                for h in range(H):
                    r = slice(HD * (h % 2), HD * (h % 2) + HD)
                    o = pb[4 + 2 * (t % 2) + h % 2][:, (h // 2) * P:(h // 2 + 1) * P]
                    last = MM(o, qT[r, h // 2, at], kT[r, h // 2, at], start=True, stop=True)
                last.then_inc(score_psum, 1)

            def scatter(i, b, windowed, firsts):
                pe.wait_ge(hot_ready, i * 2 + (b + 1))
                for c in range(GC):
                    if windowed:
                        cols, n = bass.ds(firsts[b * GC + c], W), W
                    else:
                        cols, n = slice(0, N), N
                    for t in range(T):
                        w = src_hot[b][:, c, t * P:(t + 1) * P]
                        MM(pb[t][:, cols], w, dst_hi[b][:, c, 0:n], start=False, stop=False, skip_group_check=True)
                        MM(pb[t][:, cols], w, dst_lo[b][:, c, 0:n], start=False, stop=False, skip_group_check=True)
                        last = MM(pb[4 + t // 2][:, 256 * (t % 2):256 * (t % 2) + 256], w,
                                  ebd[b][:, c, :, :].rearrange("p s q -> p (s q)"), start=False, stop=False,
                                  skip_group_check=True)
                last.then_inc(hot_used, 1)

            def all_scatter(windowed):
                with pe.Fori(0, C // (2 * GC)) as i:
                    firsts = None
                    if windowed:
                        firsts = nc.values_load_multi_w_load_instructions(
                            base_i[0:1, bass.ds(i * (2 * GC), 2 * GC)], engines=[mybir.EngineType.PE], min_val=0,
                            max_val=N - W, skip_runtime_bounds_check_because="a minimum with N - W made them")[1]
                    for b in range(2):
                        scatter(i, b, windowed, firsts)

            pe.wait_ge(v_ready, T)
            pe.wait_ge(score_read, 2 * T)
            for t in range(T + 2):
                MM(pb[t][:, :], zeros[:, :], iota_n[:, :], start=True, stop=False, skip_group_check=True)
            narrow = pe.value_load(flag_i[0:1, 0:1], min_val=0, max_val=1)
            with pe.If(narrow):
                all_scatter(True)
            with pe.Else():
                all_scatter(False)
            for t in range(T + 2):
                last = MM(pb[t][:, :], zeros[:, :], iota_n[:, :], start=False, stop=True, skip_group_check=True)
            last.then_inc(scatter_psum, 1)

            def transpose_prob(t):
                pe.wait_ge(prob_ready, t + 1)
                if t >= 2:
                    pe.wait_ge(probT_ready, 2 * (t - 1))
                for h in range(H):
                    o = pb[(6 if t % 2 == 0 else 4) + h // 4][:, (h % 4) * P:(h % 4 + 1) * P]
                    last = nc.tensor.transpose(o, prob[t % 2][:, h, :, :].rearrange("p j k -> p (j k)"), ident[:, :])
                last.then_inc(probT_psum, 1)

            def attend(t):
                pe.wait_ge(probT_ready, 2 * (t + 1))
                if t < 2:
                    pe.wait_ge(adj_ready, T)
                else:
                    pe.wait_ge(ohi_ready, t - 1)
                    pe.wait_ge(olo_ready, t - 1)
                for h in range(H):
                    o = pb[t % 2][HD * (h % 2):HD * (h % 2) + HD, (h // 2) * P:(h // 2 + 1) * P]
                    last = MM(o, v_sb[:, t, h * HD:(h + 1) * HD], probT[t % 2][:, h, :], start=True, stop=True)
                last.then_inc(o_psum, 1)

            def project(t):
                pe.wait_ge(ohi_ready, t + 1)
                pe.wait_ge(olo_ready, t + 1)
                if t >= 2:
                    pe.wait_ge(x1_ready, t - 1)
                for k in range(K):
                    last = mm3(pb[2 + t % 2][:, :], oT_hi[t % 2][:, k, :], oT_lo[t % 2][:, k, :], qkvo_hi[3][:, k, :],
                               qkvo_lo[3][:, k, :], k == 0, k == K - 1)
                last.then_inc(proj_psum, 1)

            pe.wait_ge(qw_lo, 4)
            for t in range(T + 2):
                if t < T:
                    transpose_prob(t)
                if 1 <= t <= T:
                    attend(t - 1)
                if t >= 2:
                    project(t - 2)

            for t in range(T):
                pe.wait_ge(diag_ready, t + 1)
                MM(pb[1][:, t * P:(t + 1) * P], ones[:, :], diag[:, t, :], start=True, stop=True)\
                    .then_inc(dinv_psum, 1)

            def route(f):
                pe.wait_ge(rt_split_lo, 2)
                for t in range(T):
                    at = slice(t * P, (t + 1) * P)
                    for k in range(K):
                        last = mm3(pb[2][:, t * NE:(t + 1) * NE], xT_hi[:, k, at], xT_lo[:, k, at], rt_hi[f][:, k, :],
                                   rt_lo[f][:, k, :], k == 0, k == K - 1)
                last.then_inc(rt_psum, 1)

            def into_hidden(f, e, j):
                x, b, s = ex[f], j % 2, e * J + j
                first = isinstance(e, int) and e == 0
                if j % 2 == 0:
                    n = e * PAIRS + j // 2
                    pe.wait_ge(x.whi, n * 2 + 2)
                    pe.wait_ge(x.wlo, n * 2 + 2)
                if not (first and j < 2):
                    if f == 0:
                        pe.wait_ge(x.up, s - 1)
                        pe.wait_ge(x.gated, s - 1)
                    else:
                        pe.wait_ge(x.act, s - 1)
                wh, wl = x.hi(j // 2), x.lo(j // 2)
                for part in range(x.parts):
                    for k in range(K):
                        last = mm3(pb[2 * part + b][:, :], x.hid_w(wh, part, k, b), x.hid_w(wl, part, k, b),
                                   xT_hi[:, k, :], xT_lo[:, k, :], k == 0, k == K - 1)
                last.then_inc(x.hid_psum, 1)

            def out_of_hidden(f, e, j):
                x, s = ex[f], e * J + j
                pe.wait_ge(x.ahi, s + 1)
                pe.wait_ge(x.alo, s + 1)
                if j == 0 and not (isinstance(e, int) and e == 0):
                    pe.wait_ge(x.o_read, e * T)
                wh, wl = x.out_w(x.hi(j // 2), j % 2), x.out_w(x.lo(j // 2), j % 2)
                for t in range(T):
                    at = slice(t * P, (t + 1) * P)
                    last = mm3(pb[4 + t][:, :], ah_b[j % 4][:, at], al_b[j % 4][:, at], wh, wl, j == 0, j == J - 1)
                    last.then_inc(x.down, 1)

            def experts(f):
                def before(e, j):
                    return (e, j - LAG) if j >= LAG else (e - 1, j - LAG + J)

                for j in range(J):
                    into_hidden(f, 0, j)
                    if j >= LAG:
                        out_of_hidden(f, 0, j - LAG)
                with pe.Fori(1, NE) as e:
                    for j in range(J):
                        into_hidden(f, e, j)
                        out_of_hidden(f, *before(e, j))
                for j in range(J - LAG, J):
                    out_of_hidden(f, NE - 1, j)

            def output_bias(f):
                x = ex[f]
                pe.wait_ge(comb_ready, f + 1)
                for t in range(T):
                    last = nc.tensor.transpose(pb[0][0:NE, t * P:(t + 1) * P], comb[:, t, :], ident[:, :])
                last.then_inc(combT_psum, 1)
                pe.wait_ge(combT_ready, f + 1)
                for t in range(T):
                    MM(pb[t][:, :], combT[:, t * P:(t + 1) * P], b_out[f][:, :], start=True, stop=True)\
                        .then_inc(bout_psum, 1)

            transpose_x(1)
            x_split(1)
            pe.wait_ge(x1_ready, T)
            route(0)
            pe.wait_ge(rt_logit, 1)
            pe.wait_ge(lapf_ready, T)
            experts(0)
            output_bias(0)

            transpose_x(2)
            x_split(2)
            pe.wait_ge(laplo_ready, T)

            def through(m, bank, stop):
                for t in range(T):
                    at = slice(t * P, (t + 1) * P)
                    for k in range(K):
                        last = mm3(pb[bank + t][:, :], xT_hi[:, k, at], xT_lo[:, k, at], cheb_at(m, k, 0),
                                   cheb_at(m, k, 1), k == 0, stop and k == K - 1)
                    if stop:
                        last.then_inc(term_psum if m == T else lin_psum, 1)

            def propagate(i, bank):
                pe.wait_ge(bhi_ready, T * i)
                pe.wait_ge(blo_ready, T * i)
                for t in range(T):
                    at = slice(t * P, (t + 1) * P)
                    for r in range(T):
                        last = mm3(pb[bank + t][:, :], lap_hi[:, r, at], lap_lo[:, r, at], bk_hi[:, r, :],
                                   bk_lo[:, r, :], False, r == T - 1)
                    last.then_inc(term_psum, 1)

            through(4, 0, True)
            for i in range(1, 5):
                bank = 4 * (i % 2)
                if i >= 2:
                    pe.wait_ge(term_ready, T * (i - 1))
                through(4 - i, bank, False)
                propagate(i, bank)
            pe.wait_ge(term_ready, 4 * T)
            through(5, 4, True)

            transpose_x(3)
            x_split(3)
            route(1)
            pe.wait_ge(rt_logit, 3)
            experts(1)
            output_bias(1)


_OUT = ("out", (512, 512))


def kernel(**inputs):
    import numpy as _np
    import concourse.bacc as _bacc
    from concourse import mybir as _mybir
    from concourse.bass_utils import run_bass_kernel_spmd as _run

    g = {k: _np.asarray(v) for k, v in inputs.items()}
    laid = {
        "x": g["x"], "src": g["src"], "dst": g["dst"], "edge_weight": g["edge_weight"],
        "attrT": g["edge_attr_16"].reshape(4, -1, 16).transpose(0, 2, 1),
        "Wq": g["L0_gnn_Wq"], "bq": g["L0_gnn_bq"], "Wk": g["L0_gnn_Wk"], "bk": g["L0_gnn_bk"],
        "Wv": g["L0_gnn_Wv"], "bv": g["L0_gnn_bv"], "Wo": g["L0_gnn_Wo"], "bo": g["L0_gnn_bo"],
        "We": g["L0_gnn_We"], "be": g["L0_gnn_be"],
        "router_w": g["L0_ffn_router_w"], "router_b": g["L0_ffn_router_b"],
        "gate_up": g["L0_ffn_gate_up_proj"], "gate_up_bias": g["L0_ffn_gate_up_proj_bias"],
        "down": g["L0_ffn_down_proj"], "down_bias": g["L0_ffn_down_proj_bias"],
        "gamma": g["L1_gnn_ln_gamma"], "beta": g["L1_gnn_ln_beta"],
        "cheb_lin": _np.concatenate([g["L1_gnn_cheb_W"].transpose(0, 2, 1), g["L1_gnn_lin_W"].T[None]]),
        "cheb_b": g["L1_gnn_cheb_b"], "lin_b": g["L1_gnn_lin_b"],
        "WrT": g["L1_ffn_Wr"].T, "br": g["L1_ffn_br"],
        "W1": g["L1_ffn_W1"], "b1": g["L1_ffn_b1"], "W2": g["L1_ffn_W2"], "b2": g["L1_ffn_b2"],
    }
    nc = _bacc.Bacc("TRN2", target_bir_lowering=False, num_devices=1)
    arrays, aps = {}, {}
    for name, v in laid.items():
        v = _np.ascontiguousarray(v)
        arrays[f"in_{name}"] = v
        aps[name] = nc.dram_tensor(f"in_{name}", v.shape, _mybir.dt.from_np(v.dtype), kind="ExternalInput").ap()
    out = nc.dram_tensor(_OUT[0], _OUT[1], _mybir.dt.float32, kind="ExternalOutput").ap()
    build_network(nc, aps, out)
    r = _run(nc, [arrays], core_ids=[0])
    return r.results[0][_OUT[0]]
```

```python
from contextlib import ExitStack

import concourse.bass as bass
from concourse import mybir
from concourse.alu_op_type import AluOpType as ALU

ACT = mybir.ActivationFunctionType
F32 = mybir.dt.float32
F16 = mybir.dt.float16
I32 = mybir.dt.int32
U32 = mybir.dt.uint32
AX_X = mybir.AxisListType.X

P = 128

X_SCALE = 16.0
W_SCALE = 256.0
XW_BACK = 1.0 / (X_SCALE * W_SCALE)
EDGE_SCALE = 4096.0
EB_SCALE = 64.0
LAP_SCALE = 64.0
B_SCALE = 64.0
Y_SCALE = 16.0
LN_EPS = 1e-5
QGELU = 1.702


class Chain:

    def __init__(self, eng, sem):
        self.eng, self.sem, self.base, self.k = eng, sem, 0, 0

    def link(self, ins):
        self.k += 1
        ins.then_inc(self.sem, 1)
        self.eng.wait_ge(self.sem, self.base + self.k)


def build_network(nc, a, out):
    N, D = a["x"].shape
    T = N // P
    K = D // P
    E_EDGES = a["src"].shape[0]
    C = E_EDGES // P
    ED, H = a["We"].shape
    HD = D // H
    NG = 32
    GN = N // NG
    GP = P // GN
    NE = a["router_b"].shape[0]
    I0 = a["down"].shape[1]
    I1 = a["W2"].shape[1]
    J = I0 // P
    CAP = (192, 256)
    HALF = 256
    W = 64
    assert I1 == I0 and D == 512 and N == 512 and T == 4 and C % 8 == 0 and GN * H == P

    ctx = ExitStack()
    with ctx:
        def sb(name, shape, dt):
            return ctx.enter_context(nc.sbuf_tensor(name, shape, dt))

        def sem(name):
            return ctx.enter_context(nc.semaphore(name))

        KB = 256
        r_stage = sb("r_stage", [P, 24 * KB], F32)
        r_split = sb("r_split", [P, 48 * KB], F32)
        r_gnn = sb("r_gnn", [P, 48 * KB], F32)
        r_work = sb("r_work", [P, 28 * KB], F32)
        r_mid = sb("r_mid", [P, 16 * KB], F32)
        x_sb = sb("x_sb", [P, T, D], F32)
        r_xT = sb("r_xT", [P, 8 * KB], F32)
        r_lap = sb("r_lap", [P, 8 * KB], F32)

        def view(region, start_kb, n, dt, pattern=None, **sizes):
            per = 2 if dt == F16 else 1
            ap = region[:, int(start_kb * KB):int(start_kb * KB) + n // per]
            if dt != F32:
                ap = ap.bitcast(dt)
            return ap.rearrange(pattern, **sizes) if pattern else ap

        xT_hi = view(r_xT, 0, K * N, F16, "p (k n) -> p k n", k=K)
        xT_lo = view(r_xT, 4, K * N, F16, "p (k n) -> p k n", k=K)
        adj = view(r_split, 40, T * N, F32, "p (t n) -> p t n", t=T)
        lap_hi = view(r_lap, 0, T * N, F16, "p (t n) -> p t n", t=T)
        lap_lo = view(r_lap, 4, T * N, F16, "p (t n) -> p t n", t=T)

        attrT = view(r_work, 0, 4096, F32)
        xn = view(r_work, 16, T * D, F32, "p (t d) -> p t d", t=T)
        score_m = [view(r_work, 4 * b, H * P, F32, "p (h j k) -> p h j k", h=H, j=GP) for b in range(2)]
        w_raw = [view(r_split, 8 * m, K * D, F32) for m in range(4)]
        qT = view(r_split, 32, K * N, F32, "p (k n) -> p k n", k=K)
        kT = view(r_split, 40, K * N, F32, "p (k n) -> p k n", k=K)
        qkvo_hi = [view(r_gnn, 8 * m, K * D, F16, "p (k n) -> p k n", k=K) for m in range(4)]
        qkvo_lo = [view(r_gnn, 8 * m + 4, K * D, F16, "p (k n) -> p k n", k=K) for m in range(4)]
        v_sb = view(r_mid, 0, T * D, F32, "p (t d) -> p t d", t=T)
        score = view(r_mid, 8, T * P, F32, "p (t k h) -> p t k h", t=T, k=GN)
        iota_i = view(r_mid, 10, N, F32).bitcast(I32)
        eb_f = view(r_mid, 12, C * H, F32, "p (c h) -> p c h", h=H)
        dl_hot = view(r_gnn, 32, C * GN, F16, "p (c g) -> p c g", g=GN)
        eb_hi = view(r_gnn, 36, C * H, F16, "p (c h) -> p c h", h=H)
        eb_lo = view(r_gnn, 38, C * H, F16, "p (c h) -> p c h", h=H)
        bv_bc = view(r_gnn, 40, D, F32)
        bo_bc = view(r_gnn, 42, D, F32)
        we_sb = view(r_gnn, 44, H, F32)
        be_bc = view(r_gnn, 45, H, F32)
        src_i = view(r_gnn, 46, C, F32).bitcast(I32)
        dst_i = view(r_gnn, 46.5, C, F32).bitcast(I32)
        w_f = view(r_gnn, 47, C, F32)
        src_r = view(r_mid, 8, P, F32)
        dst_r = view(r_mid, 8.5, P, F32)
        rel_r = view(r_mid, 9, P, F32)

        GC = 4
        src_hot = [view(r_work, 14 * b, GC * N, F16, "p (c n) -> p c n", c=GC) for b in range(2)]
        dst_hi = [view(r_work, 14 * b + 4, GC * N, F16, "p (c n) -> p c n", c=GC) for b in range(2)]
        dst_lo = [view(r_work, 14 * b + 8, GC * N, F16, "p (c n) -> p c n", c=GC) for b in range(2)]
        ebd = [view(r_work, 14 * b + 12, GC * 2 * P, F16, "p (c s q) -> p c s q", c=GC, s=2) for b in range(2)]

        prob = [view(r_work, 4 * b, H * P, F32, "p (h j k) -> p h j k", h=H, j=GP) for b in range(2)]
        probT = [view(r_work, 8 + 4 * b, H * P, F32, "p (h q) -> p h q", h=H) for b in range(2)]
        oT_hi = [view(r_work, 16 + 2 * b, K * P, F16, "p (k n) -> p k n", k=K) for b in range(2)]
        oT_lo = [view(r_work, 17 + 2 * b, K * P, F16, "p (k n) -> p k n", k=K) for b in range(2)]
        lap_f = [view(r_work, 2 * t, N, F32) for t in range(T)]

        xg_hi = [view(r_work, 12, K * CAP[f], F16, "p (k n) -> p k n", k=K) for f in range(2)]
        xg_lo = [view(r_work, 14, K * CAP[f], F16, "p (k n) -> p k n", k=K) for f in range(2)]
        pos_bc = view(r_work, 16, NE * N, F16, "p (e n) -> p e n", e=NE)
        to_node = view(r_work, 24, 2 * N, F16, "p (s n) -> p s n", s=2)
        to_slot = [view(r_work, 26, T * CAP[f], F16, "p (t n) -> p t n", t=T) for f in range(2)]
        sel = view(r_work, 24, NE * P, F16, "p (e q) -> p e q", e=NE)[0:NE, :, :]
        posT = view(r_work, 26, N, F16)[0:NE, :]
        xn_hi = view(r_mid, 8, T * D, F16, "p (t d) -> p t d", t=T)
        xn_lo = view(r_mid, 12, T * D, F16, "p (t d) -> p t d", t=T)

        cheb_raw = view(r_mid, 0, K * D, F32, "p (k n) -> p k n", k=K)
        cheb_all = r_gnn[:, :].bitcast(F16)
        bk = [view(r_mid, 8 * b, T * D, F32, "p (t d) -> p t d", t=T) for b in range(2)]
        bk_hi = view(r_work, 0, T * D, F16, "p (t d) -> p t d", t=T)
        bk_lo = view(r_work, 4, T * D, F16, "p (t d) -> p t d", t=T)
        xT_f = [view(r_work, 2 * k, N, F32) for k in range(K)]
        out_t = [view(r_work, 16 + 2 * t, D, F32) for t in range(T)]

        iota_n = sb("iota_n", [P, N], F16)
        ident = sb("ident", [P, P], F32)
        ones = sb("ones", [P, P], F32)
        diag = sb("diag", [P, T, P], F32)
        mask = sb("mask", [P, GP], F32)
        iota_e = sb("iota_e", [P, 8], F32)
        zeros = sb("zeros", [P, P], F16)
        span = sb("span", [C, 3], F32)
        base_i = view(r_lap, 3, C, F32)[0:1, :].bitcast(I32)
        flag_f = sb("flag_f", [1, 2], F32)
        flag_i = sb("flag_i", [1, 1], I32)
        dst_rel = view(r_lap, 2, C, F32)
        src_f = view(r_lap, 0, C, F32)
        dst_f = view(r_lap, 0.5, C, F32)
        dl_h = view(r_lap, 2.5, C, F16)
        w_hi = view(r_lap, 1, C, F32)
        w_lo = view(r_lap, 1.5, C, F32)
        w_h16 = view(r_lap, 2.75, C, F16)
        neg_half = sb("neg_half", [P, T], F32)
        stats = sb("stats", [P, T, 6], F32)
        mv = sb("mv", [P, T, 2], F32)
        var_eps = sb("var_eps", [P, T], F32)
        rstd = sb("rstd", [P, T], F32)
        hmax = sb("hmax", [P, T, H], F32)
        hsum = sb("hsum", [P, T, H], F32)
        deg = sb("deg", [P, T], F32)
        has = sb("has", [P, T], F32)
        ndinv = sb("ndinv", [P, T], F32)
        dinv = sb("dinv", [P, T], F32)
        cols = sb("cols", [P, 4, K], F32)
        rows = [view(r_mid, 0.5 * i, P, F32) for i in range(2)]
        cb_bc = sb("cb_bc", [P, D], F32)
        lb_bc = sb("lb_bc", [P, D], F32)
        rt_raw = [sb(f"rt_raw{f}", [P, K, NE], F32) for f in range(2)]
        rt_hi = [sb(f"rt_hi{f}", [P, K, NE], F16) for f in range(2)]
        rt_lo = [sb(f"rt_lo{f}", [P, K, NE], F16) for f in range(2)]
        rt_b = [sb(f"rt_b{f}", [P, NE], F32) for f in range(2)]
        b_in = [sb("b_in0", [P, NE, 2 * J], F32), sb("b_in1", [P, NE, J], F32)]
        b_sig = sb("b_sig", [P, NE, J], F32)
        b_out = [sb(f"b_out{f}", [NE, D], F32) for f in range(2)]
        logit = sb("logit", [P, T, NE], F32)
        rsum = sb("rsum", [P, T], F32)
        rmax = sb("rmax", [P, T], F32)
        top = sb("top", [P, T, 8], F32)
        top_i = sb("top_i", [P, T, 8], U32)
        top_f = sb("top_f", [P, T, 8], F32)
        tw = sb("tw", [P, T, 2], F32)
        pick = sb("pick", [P, 2, T, NE], F32)
        comb = sb("comb", [P, T, NE], F32)
        comb_s = sb("comb_s", [P, T, NE], F32)
        over_share = sb("over_share", [P, T, NE], F32)
        y_hi = cb_bc[:, :].bitcast(F16).rearrange("p (s d) -> p s d", s=2)
        y_lo = lb_bc[:, :].bitcast(F16).rearrange("p (s d) -> p s d", s=2)
        combT = cb_bc[0:NE, :]
        chosen = sb("chosen", [P, T, NE], F16)
        place = sb("place", [P, T, NE], F32)
        before_me = sb("before_me", [P, P], F16)
        ones_h = sb("ones_h", [P, P], F16)
        slot_i = sb("slot_i", [P, 2], I32)
        slot_id = sb("slot_id", [P, 2], F32)
        rank_e = sb("rank_e", [1, NE], F32)
        over_f = sb("over_f", [1, 2 * NE], F32)
        over_i = [sb(f"over_i{f}", [1, 2 * NE], I32) for f in range(2)]
        settled = sb("settled", [1, 32], F32)

        pb = [ctx.enter_context(nc.psum_tensor(f"pb{i}", [P, 512], F32)) for i in range(8)]

        rows_psum = sem("rows_psum")
        rows_read = sem("rows_read")
        x_in = sem("x_in")
        edges_in = sem("edges_in")
        edge_rows = sem("edge_rows")
        edge_cols = sem("edge_cols")
        base_ready = sem("base_ready")
        attr_in = sem("attr_in")
        wraw_in = [sem(f"wraw_in{m}") for m in range(4)]
        small_in = sem("small_in")
        tables = sem("tables")
        iota_step = sem("iota_step")
        dch = sem("dve_chain")
        ach = sem("act_chain")
        var_ready = sem("var_ready")
        rstd_ready = sem("rstd_ready")
        xn_ready = sem("xn_ready")
        eb_psum = sem("eb_psum")
        eb_read = sem("eb_read")
        xt_psum = sem("xt_psum")
        xf_ready = sem("xf_ready")
        xhi_ready = sem("xhi_ready")
        xlo_ready = sem("xlo_ready")
        qw_hi = sem("qw_hi")
        qw_lo = sem("qw_lo")
        qk_psum = sem("qk_psum")
        qk_ready = sem("qk_ready")
        v_psum = sem("v_psum")
        v_ready = sem("v_ready")
        score_psum = sem("score_psum")
        score_read = sem("score_read")
        hot_ready = sem("hot_ready")
        hot_used = sem("hot_used")
        scatter_psum = sem("scatter_psum")
        adj_ready = sem("adj_ready")
        bias_read = sem("bias_read")
        logits_ready = sem("logits_ready")
        exp_ready = sem("exp_ready")
        prob_ready = sem("prob_ready")
        probT_psum = sem("probT_psum")
        probT_ready = sem("probT_ready")
        o_psum = sem("o_psum")
        ohi_ready = sem("ohi_ready")
        olo_ready = sem("olo_ready")
        proj_psum = sem("proj_psum")
        x1_ready = sem("x1_ready")
        deg_ready = sem("deg_ready")
        dinv_pow = sem("dinv_pow")
        diag_ready = sem("diag_ready")
        dinv_psum = sem("dinv_psum")
        lapf_ready = sem("lapf_ready")
        laphi_ready = sem("laphi_ready")
        laplo_ready = sem("laplo_ready")
        rt_split = sem("rt_split")
        rt_split_lo = sem("rt_split_lo")
        rt_psum = sem("rt_psum")
        rt_logit = sem("rt_logit")
        rt_exp = sem("rt_exp")
        comb_ready = sem("comb_ready")
        place_psum = sem("place_psum")
        place_ready = sem("place_ready")
        over_ready = sem("over_ready")
        pass_done = sem("pass_done")
        turned_psum = sem("turned_psum")
        turned_ready = sem("turned_ready")
        bout_psum = sem("bout_psum")
        bout_added = sem("bout_added")
        spread_psum = sem("spread_psum")
        spread_act = sem("spread_act")
        spread_dve = sem("spread_dve")
        xnhi_ready = sem("xnhi_ready")
        xnlo_ready = sem("xnlo_ready")
        late_in = sem("late_in")
        cheb_in = sem("cheb_in")
        cheb_hi = sem("cheb_hi")
        cheb_lo = sem("cheb_lo")
        term_psum = sem("term_psum")
        term_ready = sem("term_ready")
        bhi_ready = sem("bhi_ready")
        blo_ready = sem("blo_ready")
        lin_psum = sem("lin_psum")
        out_done = sem("out_done")

        class Expert:

            def __init__(self, f, all):
                self.f, self.all = f, all
                self.cols = N if all else CAP[f]
                self.tiles = -(-self.cols // P)
                self.parts = 2 - f
                self.pair = (self.parts * K * 2 * P) + 2 * D
                g = f"f{f}_" + ("all_" if all else "")
                self.w_in = [sem(f"{g}w_in{b}") for b in range(2)]
                self.whi = sem(f"{g}whi_ready")
                self.wlo = sem(f"{g}wlo_ready")
                self.hid_psum = sem(f"{g}hid_psum")
                self.sig = sem(f"{g}sig_ready")
                self.up = sem(f"{g}up_ready")
                self.gated = sem(f"{g}gated_ready")
                self.act = sem(f"{g}act_ready")
                self.ahi = sem(f"{g}ahi_ready")
                self.alo = sem(f"{g}alo_ready")
                self.down = sem(f"{g}down_done")
                self.o_read = sem(f"{g}out_read")
                kb = 2 if all else 1
                n = self.cols
                self.sg_b = [view(r_work, kb * b, n, F32) for b in range(2)]
                self.up_b = [view(r_work, kb * (2 + b), n, F32) for b in range(2)]
                self.ga_b = [view(r_work, kb * (4 + b), n, F32) for b in range(2)]
                self.ac_b = [view(r_work, kb * (6 + b), n, F32) for b in range(2)]
                self.ah_b = [view(r_work, kb * (8 + b / 2), n, F16) for b in range(4)]
                self.al_b = [view(r_work, kb * (10 + b / 2), n, F16) for b in range(4)]
                if all:
                    self.share = sem(f"{g}share_step")
                    self.x_hi, self.x_lo = xT_hi, xT_lo
                else:
                    self.x_hi, self.x_lo = xg_hi[f], xg_lo[f]
                    self.slot_ready = sem(f"{g}slot_ready")
                    self.node_ready = sem(f"{g}node_ready")
                    self.xg_psum = sem(f"{g}xg_psum")
                    self.xghi = sem(f"{g}xghi_ready")
                    self.xglo = sem(f"{g}xglo_ready")
                    self.yhi = sem(f"{g}yhi_ready")
                    self.ylo = sem(f"{g}ylo_ready")
                    self.back_psum = sem(f"{g}back_psum")

            def hid_bank(self, part, b):
                if self.all:
                    return pb[2 * part + b][:, :]
                return pb[b][:, HALF * part:HALF * part + self.cols]

            def rows(self, t):
                return min(P, self.cols - P * t)

            def out_bank(self, t):
                return pb[(4 if self.all else 2) + t][0:self.rows(t), :]

            def stage(self, b):
                return view(r_stage, 12 * b, self.pair, F32)

            def hi(self, slot):
                return view(r_split, 12 * slot, self.pair, F16)

            def lo(self, slot):
                return view(r_split, 12 * slot + 6, self.pair, F16)

            def hid_w(self, ap, part, k, jo):
                o = part * K * 2 * P + k * 2 * P + jo * P
                return ap[:, o:o + P]

            def out_w(self, ap, jo):
                o = self.parts * K * 2 * P + jo * D
                return ap[:, o:o + D]

        ex = [Expert(f, False) for f in range(2)]
        ov = [Expert(f, True) for f in range(2)]
        PAIRS = J // 2
        AHEAD = 2
        LAG = 2

        block = ctx.enter_context(nc.Block())

        def bc(ap, pos, n):
            shape = list(ap.shape)
            u = ap.unsqueeze(pos)
            shape.insert(pos, n)
            return u.to_broadcast(shape)


        def at_expert(ap, e, col):
            return ap[:, bass.ds(e, 1), col:col + 1].rearrange("p e c -> p (e c)")

        def at_tile(ap, t, e):
            return ap[:, t:t + 1, bass.ds(e, 1)].rearrange("p t e -> p (t e)")

        def overflow(f, eng, prime, body, last=False):
            eng.wait_ge(over_ready, f + 1)
            some = eng.value_load(over_i[f][0:1, 0:1], min_val=0, max_val=1)
            with eng.If(some):
                prime()
                with eng.Fori(1, 2 * N // (CAP[f] + 1) + 1) as e:
                    here = eng.value_load(over_i[f][0:1, bass.ds(e - 1, 1)], min_val=0, max_val=1)
                    with eng.If(here):
                        w = eng.value_load(over_i[f][0:1, bass.ds(e + (NE - 1), 1)], min_val=0, max_val=NE - 1)
                        body(e, w)
            if not last:
                eng.wait_ge(pass_done, f + 1)

        def cheb_at(m, k, part):
            o = (m * 2 + part) * (K * D) + k * D
            return cheb_all[:, o:o + D]

        def cheb_part(m, k, part):
            return cheb_all[:, bass.ds(m * (2 * K * D) + (part * K * D + k * D), D)]

        @block.sync
        def _(sp):
            sp.dma_start(x_sb[:, :, :], a["x"].rearrange("(t p) d -> p t d", p=P)).then_inc(x_in, 16)
            for dst, name in ((src_i, "src"), (dst_i, "dst"), (w_f, "edge_weight")):
                sp.dma_start(dst, a[name].rearrange("(c p) -> c p", p=P)).then_inc(edges_in, 16)
            for g in range(4):
                sp.dma_start(attrT[32 * g:32 * g + ED, :], a["attrT"][g]).then_inc(attr_in, 16)
                sp.dma_start(we_sb[32 * g:32 * g + ED, :], a["We"]).then_inc(attr_in, 16)
            for m, name in enumerate(("Wq", "Wk", "Wv", "Wo")):
                sp.dma_start(w_raw[m].rearrange("p (k n) -> p k n", k=K),
                             a[name].rearrange("(k p) n -> p k n", p=P)).then_inc(wraw_in[m], 16)

            def load_pair(x, w, q):
                st, n = x.stage(q % 2), 2 * P
                if x.f == 0:
                    into = [a["gate_up"][:, :, i * I0:(i + 1) * I0] for i in range(2)]
                    down = a["down"]
                else:
                    into, down = [a["W1"]], a["W2"]
                for part, s in enumerate(into):
                    o = part * K * n
                    s = s.rearrange("e (k p) i -> p e k i", p=P)
                    sp.dma_start(st[:, o:o + K * n].rearrange("p (k i) -> p k i", k=K),
                                 s[:, bass.ds(w, 1), :, q * n:(q + 1) * n].rearrange("p e k i -> p (e k) i"))\
                        .then_inc(x.w_in[q % 2], 16)
                o = x.parts * K * n
                down = down.rearrange("e (j p) d -> p e j d", p=P)
                sp.dma_start(st[:, o:o + 2 * D].rearrange("p (j d) -> p j d", j=2),
                             down[:, bass.ds(w, 1), 2 * q:2 * q + 2, :].rearrange("p e j d -> p (e j) d"))\
                    .then_inc(x.w_in[q % 2], 16)

            def stage_free(x, n):
                sp.wait_ge(x.whi, 2 * (n - 1))
                sp.wait_ge(x.wlo, 2 * (n - 1))

            def rest(f):
                x = ov[f]

                def prime():
                    for b in range(2):
                        sp.sem_inc(x.w_in[b], 16 * (x.parts + 1) * (PAIRS // 2))

                def body(e, w):
                    sp.wait_ge(ex[f].whi, 2 * PAIRS * NE)
                    sp.wait_ge(ex[f].wlo, 2 * PAIRS * NE)
                    for q in range(PAIRS):
                        stage_free(x, e * PAIRS + q)
                        load_pair(x, w, q)

                overflow(f, sp, prime, body)

            for f in range(2):
                x = ex[f]
                if f == 1:
                    sp.wait_ge(ex[0].whi, 2 * PAIRS * NE)
                    sp.wait_ge(ex[0].wlo, 2 * PAIRS * NE)
                for q in range(PAIRS):
                    if q >= 2:
                        stage_free(x, q)
                    load_pair(x, 0, q)
                if f == 0:
                    sp.wait_ge(o_psum, T)
                    sp.wait_ge(prob_ready, T)

                def load_expert(e, matrix):
                    for q in range(PAIRS):
                        stage_free(x, e * PAIRS + q)
                        load_pair(x, e, q)
                        if matrix and q == 1:
                            if not isinstance(e, int):
                                sp.wait_ge(cheb_hi, (e - 1) * K)
                                sp.wait_ge(cheb_lo, (e - 1) * K)
                            m = a["cheb_lin"].rearrange("m (k p) n -> p m k n", p=P)
                            sp.dma_start(cheb_raw, m[:, bass.ds(e - 1, 1), :, :].rearrange("p m k n -> p (m k) n"))\
                                .then_inc(cheb_in, 16)

                load_expert(1, f == 0)
                with sp.Fori(2, NE - 1) as e:
                    load_expert(e, f == 0)
                load_expert(NE - 1, False)
                rest(f)
            for t in range(T):
                sp.wait_ge(ex[1].o_read, T * (NE - 1) + t + 1)
                sp.dma_start(out.rearrange("(t p) d -> p t d", p=P)[:, t, :], x_sb[:, t, :]).then_inc(out_done, 16)
            sp.wait_ge(out_done, 16 * T)

        @block.gpsimd
        def _(pool):
            nc.gpsimd.memset(ident[:, :], 0.0).then_inc(iota_step, 1)
            nc.gpsimd.memset(mask[:, :], 1.0).then_inc(iota_step, 1)
            nc.gpsimd.memset(zeros[:, :], 0.0).then_inc(tables, 1)
            nc.gpsimd.iota(iota_i, pattern=[[1, N]], base=0, channel_multiplier=0).then_inc(iota_step, 1)
            pool.wait_ge(iota_step, 3)
            nc.gpsimd.affine_select(out=ident[:, :], in_=ident[:, :], compare_op=ALU.not_equal, fill=1.0,
                                    base=0, pattern=[[-1, P]], channel_multiplier=1).then_inc(tables, 1)
            nc.gpsimd.affine_select(out=mask[:, :], in_=mask[:, :], compare_op=ALU.is_ge, fill=0.0,
                                    base=0, pattern=[[-GN, GP]], channel_multiplier=1).then_inc(iota_step, 1)
            pool.wait_ge(iota_step, 4)
            nc.gpsimd.affine_select(out=mask[:, :], in_=mask[:, :], compare_op=ALU.is_ge, fill=0.0,
                                    base=GN - 1, pattern=[[GN, GP]], channel_multiplier=-1).then_inc(tables, 1)
            nc.gpsimd.tensor_copy(iota_n[:, :], iota_i).then_inc(tables, 1)
            nc.gpsimd.tensor_copy(iota_e[:, :], iota_i[:, 0:8]).then_inc(tables, 1)
            nc.gpsimd.memset(neg_half[:, :], -0.5).then_inc(tables, 1)
            nc.gpsimd.memset(ones[:, :], 1.0).then_inc(tables, 1)
            nc.gpsimd.memset(ones_h[:, :], 1.0).then_inc(tables, 1)
            nc.gpsimd.iota(slot_i[:, :], pattern=[[P, 2]], base=0, channel_multiplier=1).then_inc(iota_step, 1)
            pool.wait_ge(iota_step, 5)
            nc.gpsimd.tensor_copy(slot_id[:, :], slot_i[:, :]).then_inc(tables, 1)

            def inv_sqrt(n):
                pool.wait_ge(var_ready, n + 1)
                nc.gpsimd.tensor_tensor(rstd[:, :], var_eps[:, :], neg_half[:, :], ALU.pow).then_inc(rstd_ready, 1)

            pool.wait_ge(tables, 9)
            inv_sqrt(0)
            pool.wait_ge(deg_ready, 1)
            nc.gpsimd.tensor_tensor(dinv[:, :], deg[:, :], neg_half[:, :], ALU.pow).then_inc(dinv_pow, 1)
            for n in range(1, 5):
                inv_sqrt(n)

        @block.scalar
        def _(act):
            ch = Chain(act, ach)
            rows1 = [("b1", 0, NE * J), ("bq", NE * J, K), ("bk", NE * J + K, K),
                     ("gamma", NE * J + 2 * K, K), ("beta", NE * J + 3 * K, K)]
            act.dma_start(rows[0][:, :], a["gate_up_bias"].rearrange("e (j p) -> (e j) p", p=P)).then_inc(small_in, 16)
            for name, r, n in rows1:
                s = a[name].rearrange("e (j p) -> (e j) p" if name == "b1" else "(j p) -> j p", p=P)
                act.dma_start(rows[1][r:r + n, :], s).then_inc(small_in, 16)
            for dst, name in ((bv_bc, "bv"), (bo_bc, "bo"), (be_bc, "be"), (rt_b[0][:, :], "router_b"), (rt_b[1][:, :], "br")):
                act.dma_start(dst, a[name].partition_broadcast(P)).then_inc(small_in, 16)
            for f, name in enumerate(("router_w", "WrT")):
                act.dma_start(rt_raw[f][:, :, :], a[name].rearrange("(k p) e -> p k e", p=P)).then_inc(small_in, 16)
            for f, name in enumerate(("down_bias", "b2")):
                act.dma_start(b_out[f][:, :], a[name]).then_inc(small_in, 16)

            def x_hi(n):
                for k in range(K):
                    act.wait_ge(xt_psum, K * n + k + 1)
                    nc.scalar.activation(xT_hi[:, k, :], pb[4 + k][:, :], ACT.Copy, scale=X_SCALE)\
                        .then_inc(xhi_ready, 1)

            def node_hi(f):
                act.wait_ge(xn_ready, T * (2 if f == 0 else 5))
                for t in range(T):
                    nc.scalar.activation(xn_hi[:, t, :], xn[:, t, :], ACT.Copy, scale=X_SCALE)\
                        .then_inc(xnhi_ready, 1)

            def weight_hi(x, e, q, half, slot_free=None):
                if half == 0:
                    act.wait_ge(x.w_in[q % 2], (e * (PAIRS // 2) + q // 2 + 1) * (16 * (x.parts + 1)))
                    if slot_free is not None:
                        act.wait_ge(x.down, slot_free * x.tiles)
                o, w = half * x.pair // 2, x.pair // 2
                nc.scalar.activation(x.hi(q % PAIRS)[:, o:o + w], x.stage(q % 2)[:, o:o + w], ACT.Copy,
                                     scale=W_SCALE).then_inc(x.whi, 1)

            for m in range(3):
                act.wait_ge(wraw_in[m], 16)
                nc.scalar.activation(qkvo_hi[m], w_raw[m].rearrange("p (k n) -> p k n", k=K), ACT.Copy,
                                     scale=W_SCALE).then_inc(qw_hi, 1)
                if m == 0:
                    x_hi(0)
            act.wait_ge(rows_read, 1)
            for i in range(2 * K):
                act.wait_ge(qk_psum, i + 1)
                dst, c = (qT, i) if i < K else (kT, i - K)
                nc.scalar.activation(dst[:, c, :], pb[i][:, :], ACT.Identity, bias=cols[:, i // K, c:c + 1],
                                     scale=XW_BACK).then_inc(qk_ready, 1)
            act.wait_ge(wraw_in[3], 16)
            nc.scalar.activation(qkvo_hi[3], w_raw[3].rearrange("p (k n) -> p k n", k=K), ACT.Copy,
                                 scale=W_SCALE).then_inc(qw_hi, 1)
            act.wait_ge(small_in, 16 * 15)
            for f in range(2):
                nc.scalar.activation(rt_hi[f][:, :, :], rt_raw[f][:, :, :], ACT.Copy, scale=W_SCALE)\
                    .then_inc(rt_split, 1)
            act.wait_ge(qw_lo, 4)
            for q in range(AHEAD):
                for half in range(2):
                    weight_hi(ex[0], 0, q, half)

            act.wait_ge(scatter_psum, 1)
            act.wait_ge(score_psum, T)
            for t in range(T):
                nc.scalar.activation(adj[:, t, :], pb[t][:, :], ACT.Copy, scale=1.0 / EDGE_SCALE,
                                     accum_out=deg[:, t:t + 1]).then_inc(adj_ready, 1)
            act.wait_ge(logits_ready, 1)
            nc.scalar.activation(score, score, ACT.Exp).then_inc(exp_ready, 1)

            def prob_t(t):
                act.wait_ge(probT_psum, t + 1)
                if t >= 2:
                    act.wait_ge(o_psum, t - 1)
                b0 = 6 if t % 2 == 0 else 4
                for i in range(2):
                    nc.scalar.activation(probT[t % 2][:, 4 * i:4 * i + 4, :],
                                         pb[b0 + i][:, :].rearrange("p (h q) -> p h q", h=4), ACT.Copy)\
                        .then_inc(probT_ready, 1)

            def head_out(t):
                act.wait_ge(o_psum, t + 1)
                if t >= 2:
                    act.wait_ge(proj_psum, t - 1)
                nc.scalar.activation(oT_hi[t % 2], pb[t % 2][:, :].rearrange("p (k n) -> p k n", k=K), ACT.Copy,
                                     scale=X_SCALE).then_inc(ohi_ready, 1)

            for t in range(T + 1):
                if t < T:
                    prob_t(t)
                if t >= 1:
                    head_out(t - 1)

            x_hi(1)
            node_hi(0)

            act.wait_ge(rt_logit, 2)
            nc.scalar.activation(tw[:, :, 1], rsum[:, :], ACT.Exp).then_inc(rt_exp, 1)
            for t in range(T):
                act.wait_ge(lapf_ready, t + 1)
                nc.scalar.activation(lap_hi[:, t, :], lap_f[t], ACT.Copy).then_inc(laphi_ready, 1)

            def expert_step(x, e, w, j, prepare, matrix=False, slot_wait=True):
                b, s = j % 2, e * J + j
                first = isinstance(e, int) and e == 0
                act.wait_ge(x.hid_psum, s + 1)
                if x.f == 0:
                    if not (first and j < 2):
                        act.wait_ge(x.act, s - 1)
                    nc.scalar.activation(x.sg_b[b], x.hid_bank(0, b), ACT.Sigmoid, bias=at_expert(b_sig, w, j),
                                         scale=QGELU * XW_BACK).then_inc(x.sig, 1)
                    nc.scalar.activation(x.up_b[b], x.hid_bank(1, b), ACT.Identity,
                                         bias=at_expert(b_in[0], w, J + j),
                                         scale=XW_BACK * X_SCALE * XW_BACK).then_inc(x.up, 1)
                else:
                    if not (first and j < 2):
                        act.wait_ge(x.alo, s - 1)
                    nc.scalar.activation(x.ac_b[b], x.hid_bank(0, b), ACT.Gelu, bias=at_expert(b_in[1], w, j),
                                         scale=XW_BACK).then_inc(x.act, 1)
                if prepare:
                    q = j // 2 + AHEAD
                    weight_hi(x, e, q, j % 2, s - j % 2 - 2 if slot_wait and not (first and q < PAIRS) else None)
                if matrix and 2 <= j < 2 + K:
                    if j == 2:
                        act.wait_ge(cheb_in, e * 16)
                    nc.scalar.activation(cheb_part(e - 1, j - 2, 0), cheb_raw[:, j - 2, :], ACT.Copy,
                                         scale=W_SCALE).then_inc(cheb_hi, 1)
                if not x.all and j == J - 1 and not (isinstance(e, int) and e == NE - 1):
                    gathered_hi(x, e + 1)
                act.wait_ge(x.act, s + 1)
                if not (first and j < 4):
                    act.wait_ge(x.down, (s - 3) * x.tiles)
                nc.scalar.activation(x.ah_b[j % 4], x.ac_b[b], ACT.Copy,
                                     scale=1.0 if x.f == 0 else X_SCALE).then_inc(x.ahi, 1)
                if not x.all and j == 1 and not first:
                    output_hi(x, e - 1)

            def gathered_hi(x, e):
                for i in range(2):
                    act.wait_ge(x.xg_psum, e * 4 + (i + 1))
                    nc.scalar.activation(x.x_hi[:, 2 * i:2 * i + 2, :],
                                         pb[4 + i][:, :].rearrange("p (k n) -> p k n", k=2)[:, :, 0:x.cols],
                                         ACT.Copy).then_inc(x.xghi, 1)

            def output_hi(x, e):
                for t in range(x.tiles):
                    r = x.rows(t)
                    act.wait_ge(x.down, e * (J * x.tiles) + ((J - 1) * x.tiles + t + 1))
                    nc.scalar.activation(y_hi[0:r, t, :], x.out_bank(t), ACT.Copy, scale=Y_SCALE * XW_BACK)\
                        .then_inc(x.yhi, 1)

            def spread_read(f, half):
                act.wait_ge(spread_psum, 2 * f + half + 1)
                for i in range(2):
                    nc.scalar.activation(pos_bc[:, 4 * half + i, :], pb[4 + i][:, :], ACT.Copy)\
                        .then_inc(spread_act, 1)

            def experts(f):
                x = ex[f]
                gathered_hi(x, 0)
                for j in range(J):
                    expert_step(x, 0, 0, j, True)
                    if j in (3, 5):
                        spread_read(f, (j - 3) // 2)
                with act.Fori(1, NE - 1) as e:
                    for j in range(J):
                        expert_step(x, e, e, j, True, f == 0)
                for j in range(J):
                    expert_step(x, NE - 1, NE - 1, j, j // 2 + AHEAD < PAIRS)
                output_hi(x, NE - 1)

            def rest(f):
                x = ov[f]

                def prime():
                    act.sem_inc(x.whi, 2 * PAIRS)
                    act.sem_inc(x.ahi, J)
                    if f == 0:
                        act.sem_inc(x.sig, J)
                        act.sem_inc(x.up, J)
                    else:
                        act.sem_inc(x.act, J)

                def body(e, w):
                    act.wait_ge(ex[f].o_read, T * NE)
                    act.wait_ge(x.down, e * (J * T))
                    for q in range(AHEAD):
                        for half in range(2):
                            weight_hi(x, e, q, half)
                    for j in range(J):
                        expert_step(x, e, w, j, j // 2 + AHEAD < PAIRS, slot_wait=False)

                overflow(f, act, prime, body)

            experts(0)
            rest(0)
            act.wait_ge(ex[0].o_read, T * NE)
            act.dma_start(cb_bc[:, :], a["cheb_b"].partition_broadcast(P)).then_inc(late_in, 16)
            act.dma_start(lb_bc[:, :], a["lin_b"].partition_broadcast(P)).then_inc(late_in, 16)

            for k in range(K):
                act.wait_ge(xt_psum, 2 * K + k + 1)
                nc.scalar.activation(xT_f[k], pb[4 + k][:, :], ACT.Identity, bias=cols[:, 3, k:k + 1],
                                     scale=cols[:, 2, k:k + 1]).then_inc(xf_ready, 1)
                act.wait_ge(xf_ready, k + 1)
                nc.scalar.activation(xT_hi[:, k, :], xT_f[k], ACT.Copy).then_inc(xhi_ready, 1)
            act.wait_ge(ex[0].down, NE * J * ex[0].tiles)
            for q in range(AHEAD):
                for half in range(2):
                    weight_hi(ex[1], 0, q, half)
            for i in range(4):
                for t in range(T):
                    act.wait_ge(term_ready, T * i + t + 1)
                    if i >= 1:
                        act.wait_ge(term_psum, T * (i + 1))
                    nc.scalar.activation(bk_hi[:, t, :], bk[i % 2][:, t, :], ACT.Copy,
                                         scale=B_SCALE if i < 3 else B_SCALE / 2).then_inc(bhi_ready, 1)
            x_hi(3)
            node_hi(1)
            act.wait_ge(rt_logit, 4)
            nc.scalar.activation(logit[:, :, :], logit[:, :, :], ACT.Exp).then_inc(rt_exp, 1)
            experts(1)
            rest(1)

        @block.vector
        def _(dve):
            ch = Chain(dve, dch)
            V = nc.vector

            def layernorm(n, dst):
                src = xn if n == 3 else x_sb
                for t in range(T):
                    ins = V.bn_stats(stats[:, t, :], src[:, t, :])
                    ch.link(ins)
                for t in range(T):
                    ch.link(V.bn_aggr(mv[:, t, :], stats[:, t, :]))
                V.tensor_scalar(var_eps[:, :], mv[:, :, 1], LN_EPS, None, ALU.add).then_inc(var_ready, 1)
                dve.wait_ge(rstd_ready, n + 1)
                for t in range(T):
                    V.tensor_scalar(dst[:, t, :], src[:, t, :], mv[:, t, 0:1], rstd[:, t:t + 1], ALU.subtract,
                                    ALU.mult).then_inc(xn_ready, 1)

            def x_lo(n):
                for k in range(K):
                    dve.wait_ge(xhi_ready, K * n + k + 1)
                    V.scalar_tensor_tensor(xT_lo[:, k, :], pb[4 + k][:, :], X_SCALE, xT_hi[:, k, :], ALU.mult,
                                           ALU.subtract).then_inc(xlo_ready, 1)

            def node_lo(f):
                for t in range(T):
                    dve.wait_ge(xnhi_ready, T * f + t + 1)
                    V.scalar_tensor_tensor(xn_lo[:, t, :], xn[:, t, :], X_SCALE, xn_hi[:, t, :], ALU.mult,
                                           ALU.subtract).then_inc(xnlo_ready, 1)

            def weight_lo(x, e, q, half):
                dve.wait_ge(x.whi, (e * PAIRS + q) * 2 + half + 1)
                o, w = half * x.pair // 2, x.pair // 2
                V.scalar_tensor_tensor(x.lo(q % PAIRS)[:, o:o + w], x.stage(q % 2)[:, o:o + w], W_SCALE,
                                       x.hi(q % PAIRS)[:, o:o + w], ALU.mult, ALU.subtract).then_inc(x.wlo, 1)

            dve.wait_ge(x_in, 16)
            layernorm(0, xn)
            dve.wait_ge(edges_in, 48)
            dve.wait_ge(tables, 9)
            V.tensor_scalar(rank_e[:, :], iota_e[0:1, 0:NE], -1.0, float(NE), ALU.mult, ALU.add)
            V.tensor_scalar(before_me[:, :], iota_n[:, 0:P], slot_id[:, 0:1], None, ALU.is_gt)
            V.tensor_copy(src_r, src_i)
            ch.link(V.tensor_copy(dst_r, dst_i))
            V.tensor_reduce(span[:, 1:2], dst_r, AX_X, ALU.max)
            ch.link(V.tensor_reduce(span[:, 0:1], dst_r, AX_X, ALU.min))
            ch.link(V.tensor_scalar(span[:, 0:1], span[:, 0:1], float(N - W), None, ALU.min))
            V.tensor_tensor(span[:, 2:3], span[:, 1:2], span[:, 0:1], ALU.subtract)
            V.tensor_scalar(rel_r, dst_r, span[:, 0:1], None, ALU.subtract).then_inc(edge_rows, 1)
            dve.wait_ge(edge_cols, 1)
            V.tensor_copy(src_f[:, :], pb[5][:, 0:C])
            ch.link(V.tensor_copy(dst_f[:, :], pb[5][:, P:P + C]))
            V.tensor_copy(dst_rel[:, :], pb[5][:, 2 * P:2 * P + C])
            ch.link(V.tensor_scalar(w_lo[:, :], pb[5][:, 3 * P:3 * P + C], EDGE_SCALE, None, ALU.mult))
            V.tensor_copy(base_i[:, :], pb[6][0:1, 0:C])
            ch.link(V.tensor_reduce(flag_f[:, 0:1], pb[6][0:1, P:P + C], AX_X, ALU.max))
            ch.link(V.tensor_scalar(flag_f[:, 1:2], flag_f[:, 0:1], float(W), None, ALU.is_lt))
            V.tensor_copy(flag_i[:, :], flag_f[:, 1:2]).then_inc(base_ready, 1)
            ch.link(V.tensor_copy(w_h16[:, :], w_lo[:, :]))
            ch.link(V.tensor_copy(w_hi[:, :], w_h16[:, :]))
            ch.link(V.tensor_tensor(w_lo[:, :], w_lo[:, :], w_hi[:, :], ALU.subtract))
            ch.link(V.tensor_copy(dst_i, dst_f[:, :]))
            ch.link(V.tensor_scalar(dst_i, dst_i, GN - 1, None, ALU.bitwise_and))
            ch.link(V.tensor_copy(dl_h[:, :], dst_i))
            ch.link(V.tensor_tensor(dl_hot, bc(iota_n[:, 0:GN], 1, C), bc(dl_h[:, :], 2, GN), ALU.is_equal))
            dve.wait_ge(small_in, 16 * 15)
            dve.wait_ge(rows_psum, 2)
            n0, n1 = 2 * NE * J, NE * J
            cols0 = pb[4][:, 0:n0].rearrange("p (e j) -> p e j", e=NE)
            V.tensor_scalar(b_sig[:, :, :], cols0[:, :, 0:J], QGELU, None, ALU.mult)
            V.tensor_scalar(b_in[0][:, :, 0:J], cols0[:, :, 0:J], 1.0 / XW_BACK, None, ALU.mult)
            V.tensor_scalar(b_in[0][:, :, J:2 * J], cols0[:, :, J:2 * J], 1.0, X_SCALE * XW_BACK, ALU.add, ALU.mult)
            V.tensor_copy(b_in[1][:, :, :], pb[4][:, n0:n0 + n1].rearrange("p (e j) -> p e j", e=NE))
            V.tensor_copy(cols[:, 0:2, :], pb[4][:, n0 + n1:n0 + n1 + 2 * K].rearrange("p (v k) -> p v k", v=2))
            V.tensor_scalar(cols[:, 2:4, :], pb[4][:, n0 + n1 + 2 * K:n0 + n1 + 4 * K]
                            .rearrange("p (v k) -> p v k", v=2), X_SCALE, None, ALU.mult).then_inc(rows_read, 1)
            for g in range(4):
                dve.wait_ge(eb_psum, g + 1)
                V.tensor_tensor(eb_f[:, C // 4 * g:C // 4 * (g + 1), :],
                                pb[g][:, 0:C // 4 * H].rearrange("p (c h) -> p c h", h=H), bc(be_bc, 1, C // 4),
                                ALU.add).then_inc(eb_read, 1)
            dve.wait_ge(eb_read, 4)
            ch.link(V.tensor_scalar(eb_hi, eb_f, EB_SCALE, None, ALU.mult))
            ch.link(V.scalar_tensor_tensor(eb_lo, eb_f, EB_SCALE, eb_hi, ALU.mult, ALU.subtract))
            x_lo(0)

            def qkvo_lo_part(m):
                dve.wait_ge(qw_hi, m + 1)
                V.scalar_tensor_tensor(qkvo_lo[m].rearrange("p k n -> p (k n)"), w_raw[m], W_SCALE,
                                       qkvo_hi[m].rearrange("p k n -> p (k n)"), ALU.mult, ALU.subtract)\
                    .then_inc(qw_lo, 1)

            for m in range(3):
                qkvo_lo_part(m)
            for t in range(T):
                dve.wait_ge(v_psum, t + 1)
                V.scalar_tensor_tensor(v_sb[:, t, :], pb[t][:, :], XW_BACK, bv_bc, ALU.mult, ALU.add)\
                    .then_inc(v_ready, 1)
            for t in range(T):
                dve.wait_ge(score_psum, t + 1)
                for i in range(2):
                    ins = V.tensor_tensor(score_m[t % 2][:, i:H:2, :, :],
                                          pb[4 + 2 * (t % 2) + i][:, :].rearrange("p (h j k) -> p h j k", h=4, j=GP),
                                          bc(bc(mask[:, :], 1, 4), 3, GN), ALU.mult)
                    ins.then_inc(score_read, 1)
                dve.wait_ge(score_read, 2 * t + 2)
                ch.link(V.tensor_reduce(score[:, t, :, :].rearrange("p k h -> p h k"),
                                        score_m[t % 2].rearrange("p h j k -> p h k j"), AX_X, ALU.add))
            ch.link(V.tensor_tensor(x_sb[:, :, :], x_sb[:, :, :], bc(bo_bc, 1, T), ALU.add))
            qkvo_lo_part(3)
            for f in range(2):
                dve.wait_ge(rt_split, f + 1)
                V.scalar_tensor_tensor(rt_lo[f][:, :, :].rearrange("p k e -> p (k e)"),
                                       rt_raw[f][:, :, :].rearrange("p k e -> p (k e)"), W_SCALE,
                                       rt_hi[f][:, :, :].rearrange("p k e -> p (k e)"), ALU.mult, ALU.subtract)\
                    .then_inc(rt_split_lo, 1)

            def one_hots(i, b, free, windowed):
                if free:
                    dve.wait_ge(hot_used, i * 2 + (b - 1))
                n = W if windowed else N
                dst = dst_rel if windowed else dst_f
                for c in range(GC):
                    at = bass.ds(i * (2 * GC) + (b * GC + c), 1)
                    V.tensor_scalar(src_hot[b][:, c, :], iota_n[:, :], src_f[:, at], None, ALU.is_equal)
                    V.tensor_scalar(dst_hi[b][:, c, 0:n], iota_n[:, 0:n], dst[:, at], w_hi[:, at], ALU.is_equal,
                                    ALU.mult)
                    V.tensor_scalar(dst_lo[b][:, c, 0:n], iota_n[:, 0:n], dst[:, at], w_lo[:, at], ALU.is_equal,
                                    ALU.mult)
                at = bass.ds(i * (2 * GC) + b * GC, GC)
                for s, eb in enumerate((eb_hi, eb_lo)):
                    last = V.tensor_tensor(ebd[b][:, :, s, :].rearrange("p c (g h) -> p c g h", h=H),
                                           bc(dl_hot[:, at, :], 3, H), bc(eb[:, at, :], 2, GN), ALU.mult)
                last.then_inc(hot_ready, 1)

            def all_one_hots(windowed):
                one_hots(0, 0, False, windowed)
                one_hots(0, 1, False, windowed)
                with dve.Fori(1, C // (2 * GC)) as i:
                    one_hots(i, 0, True, windowed)
                    one_hots(i, 1, True, windowed)

            dve.wait_ge(score_psum, T)
            dve.wait_ge(base_ready, 1)
            narrow = dve.value_load(flag_i[0:1, 0:1], min_val=0, max_val=1)
            with dve.If(narrow):
                all_one_hots(True)
            with dve.Else():
                all_one_hots(False)
            for q in range(AHEAD):
                for half in range(2):
                    weight_lo(ex[0], 0, q, half)

            dve.wait_ge(scatter_psum, 1)
            flat = score.rearrange("p t k h -> p t (k h)")
            ch.link(V.tensor_scalar(score, score, float(HD) ** -0.5, None, ALU.mult))
            for s in range(2):
                for i in range(2):
                    ins = V.scalar_tensor_tensor(
                        flat[:, 2 * i:2 * i + 2, :],
                        pb[4 + i][:, :].rearrange("p (t s q) -> p t s q", t=2, s=2)[:, :, s, :],
                        1.0 / EB_SCALE, flat[:, 2 * i:2 * i + 2, :], ALU.mult, ALU.add)
                    ch.link(ins)
            by_head = score.rearrange("p t k h -> p t h k")
            ch.link(V.tensor_reduce(hmax[:, :, :], by_head, AX_X, ALU.max))
            V.tensor_tensor(score, score, bc(hmax[:, :, :], 2, GN), ALU.subtract).then_inc(logits_ready, 1)
            dve.wait_ge(exp_ready, 1)
            ch.link(V.tensor_reduce(hsum[:, :, :], by_head, AX_X, ALU.add))
            ch.link(V.reciprocal(hsum[:, :, :], hsum[:, :, :]))
            ch.link(V.tensor_tensor(score, score, bc(hsum[:, :, :], 2, GN), ALU.mult))

            def spread(t):
                if t >= 2:
                    dve.wait_ge(probT_psum, t - 1)
                V.tensor_tensor(prob[t % 2], bc(score[:, t, :, :].rearrange("p k h -> p h k"), 2, GP),
                                bc(bc(mask[:, :], 1, H), 3, GN), ALU.mult).then_inc(prob_ready, 1)

            def head_lo(t):
                dve.wait_ge(ohi_ready, t + 1)
                V.scalar_tensor_tensor(oT_lo[t % 2].rearrange("p k n -> p (k n)"), pb[t % 2][:, :], X_SCALE,
                                       oT_hi[t % 2].rearrange("p k n -> p (k n)"), ALU.mult, ALU.subtract)\
                    .then_inc(olo_ready, 1)

            def project(t):
                dve.wait_ge(proj_psum, t + 1)
                ins = V.scalar_tensor_tensor(x_sb[:, t, :], pb[2 + t % 2][:, :], XW_BACK, x_sb[:, t, :], ALU.mult,
                                             ALU.add)
                ins.then_inc(x1_ready, 1)

            dve.wait_ge(adj_ready, T)
            ch.link(V.tensor_scalar(has[:, :], deg[:, :], 0.0, None, ALU.is_gt))
            ch.link(V.tensor_tensor(deg[:, :], deg[:, :], has[:, :], ALU.mult))
            ch.link(V.scalar_tensor_tensor(deg[:, :], has[:, :], -1.0, deg[:, :], ALU.mult, ALU.add))
            V.tensor_scalar(deg[:, :], deg[:, :], 1.0, None, ALU.add).then_inc(deg_ready, 1)

            for t in range(T + 2):
                if t < T:
                    spread(t)
                if 1 <= t <= T:
                    head_lo(t - 1)
                if t >= 2:
                    project(t - 2)
            dve.wait_ge(dinv_pow, 1)
            ch.link(V.tensor_tensor(dinv[:, :], dinv[:, :], has[:, :], ALU.mult))
            V.tensor_scalar(ndinv[:, :], dinv[:, :], -2.0 * LAP_SCALE, None, ALU.mult)
            for t in range(T):
                V.tensor_scalar(diag[:, t, :], ident[:, :], dinv[:, t:t + 1], None, ALU.mult).then_inc(diag_ready, 1)

            dve.wait_ge(x1_ready, T)
            layernorm(1, xn)
            x_lo(1)
            node_lo(0)

            def choose(f):
                vals = logit
                for t in range(T):
                    ch.link(V.max(top[:, t, :], vals[:, t, :]))
                for t in range(T):
                    ch.link(V.max_index(top_i[:, t, :], top[:, t, :], vals[:, t, :]))
                ch.link(V.tensor_copy(top_f[:, :, :], top_i[:, :, :]))
                if f == 0:
                    V.tensor_tensor(rsum[:, :], top[:, :, 1], top[:, :, 0], ALU.subtract).then_inc(rt_logit, 1)
                    dve.wait_ge(rt_exp, 1)
                    ch.link(V.tensor_scalar(rsum[:, :], tw[:, :, 1], 1.0, None, ALU.add))
                    ch.link(V.reciprocal(tw[:, :, 0], rsum[:, :]))
                    ch.link(V.tensor_tensor(tw[:, :, 1], tw[:, :, 1], tw[:, :, 0], ALU.mult))
                else:
                    ch.link(V.tensor_copy(tw[:, :, :], top[:, :, 0:2]))
                for t in range(T):
                    for r in range(2):
                        ch.link(V.tensor_scalar(pick[:, r, t, :], iota_e[:, 0:NE], top_f[:, t, r:r + 1],
                                                tw[:, t, r:r + 1], ALU.is_equal, ALU.mult))
                ch.link(V.tensor_tensor(comb[:, :, :], pick[:, 0, :, :], pick[:, 1, :, :], ALU.add))
                ch.link(V.tensor_scalar(chosen[:, :, :], comb[:, :, :], 0.0, None, ALU.not_equal))
                V.tensor_scalar(comb_s[:, :, :], comb[:, :, :], 1.0 / Y_SCALE, None, ALU.mult).then_inc(comb_ready, 1)

            def places(f):
                dve.wait_ge(place_psum, f + 1)
                counts = pb[3][:, 0:T * NE].rearrange("p (t e) -> p t e", t=T)
                ch.link(V.scalar_tensor_tensor(place[:, :, :], counts, 1.0, chosen[:, :, :], ALU.add, ALU.mult))
                ch.link(V.tensor_scalar(place[:, :, :], place[:, :, :], 1.0, None, ALU.subtract))
                to_slots(ex[f], 0)
                ch.link(V.tensor_scalar(over_f[:, 0:NE], pb[3][0:1, T * NE:(T + 1) * NE], float(CAP[f]), None,
                                        ALU.is_gt))
                ch.link(V.tensor_tensor(over_f[:, 0:NE], over_f[:, 0:NE], rank_e[:, :], ALU.mult))
                ch.link(V.max(over_f[:, NE:2 * NE], over_f[:, 0:NE]))
                ch.link(V.tensor_scalar(over_f[:, 0:NE], over_f[:, NE:2 * NE], 1.0, None, ALU.min))
                ch.link(V.scalar_tensor_tensor(over_f[:, NE:2 * NE], over_f[:, NE:2 * NE], -float(NE), over_f[:, 0:NE],
                                               ALU.add, ALU.mult))
                ch.link(V.tensor_scalar(over_f[:, NE:2 * NE], over_f[:, NE:2 * NE], -1.0, None, ALU.mult))
                V.tensor_copy(over_i[f][:, :], over_f[:, :]).then_inc(over_ready, 1)

            def to_slots(x, e):
                for t in range(T):
                    ins = V.tensor_scalar(to_slot[x.f][:, t, :], iota_n[:, 0:x.cols], at_tile(place, t, e), None,
                                          ALU.is_equal)
                ins.then_inc(x.slot_ready, 1)

            def to_nodes(x, e):
                for t in range(x.tiles):
                    r = x.rows(t)
                    ins = V.tensor_scalar(to_node[0:r, t, :],
                                          pos_bc[0:r, bass.ds(e, 1), :].rearrange("p e n -> p (e n)"),
                                          slot_id[0:r, t:t + 1], None, ALU.is_equal)
                ins.then_inc(x.node_ready, 1)

            def gathered_lo(x, e):
                for i in range(2):
                    dve.wait_ge(x.xg_psum, e * 4 + (i + 3))
                    V.tensor_copy(x.x_lo[:, 2 * i:2 * i + 2, :],
                                  pb[6 + i][:, :].rearrange("p (k n) -> p k n", k=2)[:, :, 0:x.cols])\
                        .then_inc(x.xglo, 1)

            def output_lo(x, e):
                for t in range(x.tiles):
                    r = x.rows(t)
                    dve.wait_ge(x.yhi, e * x.tiles + (t + 1))
                    V.scalar_tensor_tensor(y_lo[0:r, t, :], x.out_bank(t), Y_SCALE * XW_BACK, y_hi[0:r, t, :],
                                           ALU.mult, ALU.subtract).then_inc(x.ylo, 1)

            def bring_back(x, e):
                for t in range(T):
                    dve.wait_ge(x.back_psum, e * T + (t + 1))
                    V.scalar_tensor_tensor(x_sb[:, t, :], pb[4 + t][:, :], at_tile(comb_s, t, e), x_sb[:, t, :],
                                           ALU.mult, ALU.add).then_inc(x.o_read, 1)

            def turned(f):
                dve.wait_ge(turned_psum, f + 1)
                V.tensor_copy(posT, pb[4][0:NE, :])
                V.tensor_copy(sel, bc(ident[0:NE, 0:NE], 2, P))
                V.tensor_copy(combT, pb[5][0:NE, :]).then_inc(turned_ready, 1)

            def add_biases(f):
                for t in range(T):
                    dve.wait_ge(bout_psum, T * f + t + 1)
                    V.tensor_tensor(x_sb[:, t, :], x_sb[:, t, :], pb[4 + t][:, :], ALU.add).then_inc(bout_added, 1)

            def spread_read(f, half):
                dve.wait_ge(spread_psum, 2 * f + half + 1)
                for i in range(2, 4):
                    V.tensor_copy(pos_bc[:, 4 * half + i, :], pb[4 + i][:, :]).then_inc(spread_dve, 1)

            def logits(f):
                dve.wait_ge(rt_psum, f + 1)
                V.scalar_tensor_tensor(logit[:, :, :], pb[2][:, 0:T * NE].rearrange("p (t e) -> p t e", t=T), XW_BACK,
                                       bc(rt_b[f][:, :], 1, T), ALU.mult, ALU.add).then_inc(rt_logit, 1)
                dve.wait_ge(rt_logit, 1 if f == 0 else 3)

            logits(0)
            choose(0)
            for t in range(T):
                dve.wait_ge(dinv_psum, T)
                V.scalar_tensor_tensor(lap_f[t], adj[:, t, :], ndinv[:, t:t + 1], pb[1][:, :], ALU.mult, ALU.mult)\
                    .then_inc(lapf_ready, 1)
            places(0)
            for t in range(T):
                dve.wait_ge(laphi_ready, t + 1)
                V.tensor_tensor(lap_lo[:, t, :], lap_f[t], lap_hi[:, t, :], ALU.subtract).then_inc(laplo_ready, 1)

            def expert_step(x, e, w, j, prepare, matrix=False):
                b, s = j % 2, e * J + j
                first, final = (isinstance(e, int) and e == n for n in (0, NE - 1))
                if not x.all and j == 2 and not first:
                    to_nodes(x, e - 1)
                if not x.all and j == 6 and not final:
                    to_slots(x, e + 1)
                if x.f == 0:
                    dve.wait_ge(x.sig, s + 1)
                    dve.wait_ge(x.up, s + 1)
                    V.scalar_tensor_tensor(x.ga_b[b], x.hid_bank(0, b), at_expert(b_in[0], w, j), x.sg_b[b], ALU.add,
                                           ALU.mult).then_inc(x.gated, 1)
                    dve.wait_ge(x.gated, s + 1)
                    V.tensor_tensor(x.ac_b[b], x.ga_b[b], x.up_b[b], ALU.mult).then_inc(x.act, 1)
                if prepare:
                    weight_lo(x, e, j // 2 + AHEAD, j % 2)
                if matrix and 2 <= j < 2 + K:
                    dve.wait_ge(cheb_hi, (e - 1) * K + (j - 1))
                    V.scalar_tensor_tensor(cheb_part(e - 1, j - 2, 1), cheb_raw[:, j - 2, :], W_SCALE,
                                           cheb_part(e - 1, j - 2, 0), ALU.mult, ALU.subtract).then_inc(cheb_lo, 1)
                if not x.all and j == J - 1 and not final:
                    gathered_lo(x, e + 1)
                dve.wait_ge(x.ahi, s + 1)
                if x.f == 0:
                    V.tensor_tensor(x.al_b[j % 4], x.ac_b[b], x.ah_b[j % 4], ALU.subtract).then_inc(x.alo, 1)
                else:
                    V.scalar_tensor_tensor(x.al_b[j % 4], x.ac_b[b], X_SCALE, x.ah_b[j % 4], ALU.mult, ALU.subtract)\
                        .then_inc(x.alo, 1)
                if not x.all and j == 1 and not first:
                    output_lo(x, e - 1)
                if not x.all and j == 4 and not first:
                    bring_back(x, e - 1)

            def experts(f):
                x = ex[f]
                gathered_lo(x, 0)
                for j in range(J):
                    expert_step(x, 0, 0, j, True)
                    if j == 1:
                        turned(f)
                    if j == 2:
                        add_biases(f)
                    if j in (3, 5):
                        spread_read(f, (j - 3) // 2)
                        if j == 3:
                            dve.wait_ge(bout_added, T * (f + 1))
                dve.wait_ge(spread_act, 4 * (f + 1))
                with dve.Fori(1, NE - 1) as e:
                    for j in range(J):
                        expert_step(x, e, e, j, True, f == 0)
                for j in range(J):
                    expert_step(x, NE - 1, NE - 1, j, j // 2 + AHEAD < PAIRS)
                output_lo(x, NE - 1)
                to_nodes(x, NE - 1)
                bring_back(x, NE - 1)
                dve.wait_ge(x.o_read, T * NE)

            def rest(f):
                x = ov[f]

                def prime():
                    dve.sem_inc(x.share, 2)
                    dve.sem_inc(x.wlo, 2 * PAIRS)
                    dve.sem_inc(x.alo, J)
                    dve.sem_inc(x.o_read, T)
                    if f == 0:
                        dve.sem_inc(x.gated, J)
                        dve.sem_inc(x.act, J)

                def body(e, w):
                    V.tensor_scalar(over_share[:, :, :], place[:, :, :], CAP[f] - 0.5, XW_BACK, ALU.is_gt, ALU.mult)\
                        .then_inc(x.share, 1)
                    dve.wait_ge(x.share, e * 2 + 1)
                    V.tensor_tensor(over_share[:, :, :], over_share[:, :, :], comb[:, :, :], ALU.mult)\
                        .then_inc(x.share, 1)
                    dve.wait_ge(x.share, e * 2 + 2)
                    for q in range(AHEAD):
                        for half in range(2):
                            weight_lo(x, e, q, half)
                    for j in range(J):
                        expert_step(x, e, w, j, j // 2 + AHEAD < PAIRS)
                    for t in range(T):
                        dve.wait_ge(x.down, e * (J * T) + ((J - 1) * T + t + 1))
                        V.scalar_tensor_tensor(x_sb[:, t, :], x.out_bank(t), at_tile(over_share, t, w),
                                               x_sb[:, t, :], ALU.mult, ALU.add).then_inc(x.o_read, 1)

                    dve.wait_ge(x.o_read, e * T + T)
                    V.tensor_copy(settled[:, bass.ds(e + 16 * f, 1)], rank_e[:, 0:1])

                overflow(f, dve, prime, body, last=True)
                V.memset(settled[:, 16 * f:16 * f + 1], 0.0).then_inc(pass_done, 1)

            experts(0)
            rest(0)

            layernorm(2, xn)
            dve.wait_ge(xn_ready, 3 * T)
            layernorm(3, xn)
            for k in range(K):
                dve.wait_ge(xhi_ready, 2 * K + k + 1)
                V.tensor_tensor(xT_lo[:, k, :], xT_f[k], xT_hi[:, k, :], ALU.subtract).then_inc(xlo_ready, 1)
            for q in range(AHEAD):
                for half in range(2):
                    weight_lo(ex[1], 0, q, half)

            def term(i, t):
                dve.wait_ge(term_psum, T * i + t + 1)
                p = pb[4 * (i % 2) + t][:, :]
                if i < 2:
                    ins = V.tensor_scalar(bk[i][:, t, :], p, XW_BACK, None, ALU.mult)
                else:
                    ins = V.scalar_tensor_tensor(bk[i % 2][:, t, :], p, XW_BACK, bk[i % 2][:, t, :], ALU.mult,
                                                 ALU.subtract)
                ins.then_inc(term_ready, 1)

            def term_lo(i, t):
                dve.wait_ge(bhi_ready, T * i + t + 1)
                V.scalar_tensor_tensor(bk_lo[:, t, :], bk[i % 2][:, t, :], B_SCALE if i < 3 else B_SCALE / 2,
                                       bk_hi[:, t, :], ALU.mult, ALU.subtract).then_inc(blo_ready, 1)

            for i in range(4):
                for t in range(T):
                    term(i, t)
                    if t >= 1:
                        term_lo(i, t - 1)
                term_lo(i, T - 1)
            for t in range(T):
                term(4, t)
            dve.wait_ge(late_in, 32)
            for t in range(T):
                dve.wait_ge(term_ready, 4 * T + t + 1)
                ch.link(V.tensor_tensor(out_t[t], bk[0][:, t, :], cb_bc[:, :], ALU.add))
                ch.link(V.scalar_tensor_tensor(out_t[t], out_t[t], 0.01, out_t[t], ALU.mult, ALU.max))
                ch.link(V.tensor_tensor(x_sb[:, t, :], x_sb[:, t, :], out_t[t], ALU.add))
                ch.link(V.tensor_tensor(x_sb[:, t, :], x_sb[:, t, :], lb_bc[:, :], ALU.add))
            for t in range(T):
                dve.wait_ge(lin_psum, t + 1)
                ch.link(V.scalar_tensor_tensor(x_sb[:, t, :], pb[4 + t][:, :], XW_BACK, x_sb[:, t, :], ALU.mult,
                                               ALU.add))

            layernorm(4, xn)
            x_lo(3)
            node_lo(1)
            logits(1)
            for t in range(T):
                ch.link(V.tensor_reduce(rmax[:, t:t + 1], logit[:, t, :], AX_X, ALU.max))
            V.tensor_tensor(logit[:, :, :], logit[:, :, :], bc(rmax[:, :], 2, NE), ALU.subtract).then_inc(rt_logit, 1)
            dve.wait_ge(rt_exp, 2)
            ch.link(V.tensor_reduce(rsum[:, :], logit[:, :, :], AX_X, ALU.add))
            ch.link(V.reciprocal(rsum[:, :], rsum[:, :]))
            ch.link(V.tensor_tensor(logit[:, :, :], logit[:, :, :], bc(rsum[:, :], 2, NE), ALU.mult))
            choose(1)
            places(1)
            experts(1)
            rest(1)

        @block.tensor
        def _(pe):
            MM = nc.tensor.matmul

            def mm3(o, sh, sl, mh, ml, start, stop):
                MM(o, sh, mh, start=start, stop=False)
                MM(o, sh, ml, start=False, stop=False)
                return MM(o, sl, mh, start=False, stop=stop)

            def transpose_x(n):
                for k in range(K):
                    for t in range(T):
                        pe.wait_ge(xn_ready, T * (n if n < 2 else n + 1) + t + 1)
                        last = nc.tensor.transpose(pb[4 + k][:, t * P:(t + 1) * P], xn[:, t, k * P:(k + 1) * P],
                                                   ident[:, :])
                    last.then_inc(xt_psum, 1)

            def x_split(n):
                pe.wait_ge(xhi_ready, K * (n + 1))
                pe.wait_ge(xlo_ready, K * (n + 1))

            pe.wait_ge(tables, 9)
            pe.wait_ge(small_in, 16 * 15)
            nr = NE * J + 4 * K
            nc.tensor.transpose(pb[4][:, 0:P], rows[0][:, :], ident[:, :]).then_inc(rows_psum, 1)
            nc.tensor.transpose(pb[4][:, P:P + nr], rows[1][0:nr, :], ident[0:nr, 0:nr]).then_inc(rows_psum, 1)

            pe.wait_ge(edge_rows, 1)
            for n, r in enumerate((src_r, dst_r, rel_r, w_f)):
                nc.tensor.transpose(pb[5][:, n * P:n * P + C], r, ident[:, :])
            nc.tensor.transpose(pb[6][0:1, 0:C], span[:, 0:1], ident[:, :])
            nc.tensor.transpose(pb[6][0:1, P:P + C], span[:, 2:3], ident[:, :]).then_inc(edge_cols, 1)

            pe.wait_ge(attr_in, 16 * 8)
            for g in range(4):
                for c in range(C // 4):
                    last = MM(pb[g][:, c * H:(c + 1) * H], attrT[32 * g:32 * g + ED, c * P:(c + 1) * P],
                              we_sb[32 * g:32 * g + ED, :], start=True, stop=True)
                last.then_inc(eb_psum, 1)

            pe.wait_ge(rows_read, 1)
            pe.wait_ge(base_ready, 1)
            transpose_x(0)
            x_split(0)
            pe.wait_ge(eb_read, 4)
            for m in range(2):
                pe.wait_ge(qw_hi, m + 1)
                pe.wait_ge(qw_lo, m + 1)
                for c in range(K):
                    for k in range(K):
                        at = slice(c * P, (c + 1) * P)
                        last = mm3(pb[4 * m + c][:, :], qkvo_hi[m][:, k, at], qkvo_lo[m][:, k, at],
                                   xT_hi[:, k, :], xT_lo[:, k, :], k == 0, k == K - 1)
                    last.then_inc(qk_psum, 1)
            pe.wait_ge(qw_hi, 3)
            pe.wait_ge(qw_lo, 3)
            for t in range(T):
                pe.wait_ge(qk_ready, t + 1)
                at = slice(t * P, (t + 1) * P)
                for k in range(K):
                    last = mm3(pb[t][:, :], xT_hi[:, k, at], xT_lo[:, k, at], qkvo_hi[2][:, k, :],
                               qkvo_lo[2][:, k, :], k == 0, k == K - 1)
                last.then_inc(v_psum, 1)
            pe.wait_ge(qk_ready, 2 * K)
            for t in range(T):
                if t >= 2:
                    pe.wait_ge(score_read, 2 * (t - 1))
                at = slice(t * P, (t + 1) * P)
                for h in range(H):
                    r = slice(HD * (h % 2), HD * (h % 2) + HD)
                    o = pb[4 + 2 * (t % 2) + h % 2][:, (h // 2) * P:(h // 2 + 1) * P]
                    last = MM(o, qT[r, h // 2, at], kT[r, h // 2, at], start=True, stop=True)
                last.then_inc(score_psum, 1)

            def scatter(i, b, windowed, firsts):
                pe.wait_ge(hot_ready, i * 2 + (b + 1))
                for c in range(GC):
                    if windowed:
                        cols, n = bass.ds(firsts[b * GC + c], W), W
                    else:
                        cols, n = slice(0, N), N
                    for t in range(T):
                        w = src_hot[b][:, c, t * P:(t + 1) * P]
                        MM(pb[t][:, cols], w, dst_hi[b][:, c, 0:n], start=False, stop=False, skip_group_check=True)
                        MM(pb[t][:, cols], w, dst_lo[b][:, c, 0:n], start=False, stop=False, skip_group_check=True)
                        last = MM(pb[4 + t // 2][:, 256 * (t % 2):256 * (t % 2) + 256], w,
                                  ebd[b][:, c, :, :].rearrange("p s q -> p (s q)"), start=False, stop=False,
                                  skip_group_check=True)
                last.then_inc(hot_used, 1)

            def all_scatter(windowed):
                with pe.Fori(0, C // (2 * GC)) as i:
                    firsts = None
                    if windowed:
                        firsts = nc.values_load_multi_w_load_instructions(
                            base_i[0:1, bass.ds(i * (2 * GC), 2 * GC)], engines=[mybir.EngineType.PE], min_val=0,
                            max_val=N - W, skip_runtime_bounds_check_because="a minimum with N - W made them")[1]
                    for b in range(2):
                        scatter(i, b, windowed, firsts)

            pe.wait_ge(v_ready, T)
            pe.wait_ge(score_read, 2 * T)
            for t in range(T + 2):
                MM(pb[t][:, :], zeros[:, :], iota_n[:, :], start=True, stop=False, skip_group_check=True)
            narrow = pe.value_load(flag_i[0:1, 0:1], min_val=0, max_val=1)
            with pe.If(narrow):
                all_scatter(True)
            with pe.Else():
                all_scatter(False)
            for t in range(T + 2):
                last = MM(pb[t][:, :], zeros[:, :], iota_n[:, :], start=False, stop=True, skip_group_check=True)
            last.then_inc(scatter_psum, 1)

            def transpose_prob(t):
                pe.wait_ge(prob_ready, t + 1)
                if t >= 2:
                    pe.wait_ge(probT_ready, 2 * (t - 1))
                for h in range(H):
                    o = pb[(6 if t % 2 == 0 else 4) + h // 4][:, (h % 4) * P:(h % 4 + 1) * P]
                    last = nc.tensor.transpose(o, prob[t % 2][:, h, :, :].rearrange("p j k -> p (j k)"), ident[:, :])
                last.then_inc(probT_psum, 1)

            def attend(t):
                pe.wait_ge(probT_ready, 2 * (t + 1))
                if t < 2:
                    pe.wait_ge(adj_ready, T)
                else:
                    pe.wait_ge(ohi_ready, t - 1)
                    pe.wait_ge(olo_ready, t - 1)
                for h in range(H):
                    o = pb[t % 2][HD * (h % 2):HD * (h % 2) + HD, (h // 2) * P:(h // 2 + 1) * P]
                    last = MM(o, v_sb[:, t, h * HD:(h + 1) * HD], probT[t % 2][:, h, :], start=True, stop=True)
                last.then_inc(o_psum, 1)

            def project(t):
                pe.wait_ge(ohi_ready, t + 1)
                pe.wait_ge(olo_ready, t + 1)
                if t >= 2:
                    pe.wait_ge(x1_ready, t - 1)
                for k in range(K):
                    last = mm3(pb[2 + t % 2][:, :], oT_hi[t % 2][:, k, :], oT_lo[t % 2][:, k, :], qkvo_hi[3][:, k, :],
                               qkvo_lo[3][:, k, :], k == 0, k == K - 1)
                last.then_inc(proj_psum, 1)

            pe.wait_ge(qw_lo, 4)
            for t in range(T + 2):
                if t < T:
                    transpose_prob(t)
                if 1 <= t <= T:
                    attend(t - 1)
                if t >= 2:
                    project(t - 2)

            for t in range(T):
                pe.wait_ge(diag_ready, t + 1)
                MM(pb[1][:, t * P:(t + 1) * P], ones[:, :], diag[:, t, :], start=True, stop=True)\
                    .then_inc(dinv_psum, 1)

            def route(f):
                pe.wait_ge(rt_split_lo, 2)
                for t in range(T):
                    at = slice(t * P, (t + 1) * P)
                    for k in range(K):
                        last = mm3(pb[2][:, t * NE:(t + 1) * NE], xT_hi[:, k, at], xT_lo[:, k, at], rt_hi[f][:, k, :],
                                   rt_lo[f][:, k, :], k == 0, k == K - 1)
                last.then_inc(rt_psum, 1)

            def positions(f):
                pe.wait_ge(comb_ready, f + 1)
                for t in range(T):
                    o = pb[3][:, t * NE:(t + 1) * NE]
                    MM(o, before_me[:, :], chosen[:, t, :], start=True, stop=t == 0)
                    for s in range(t):
                        MM(o, ones_h[:, :], chosen[:, s, :], start=False, stop=s == t - 1)
                for t in range(T):
                    last = MM(pb[3][0:1, T * NE:(T + 1) * NE], ones_h[:, 0:1], chosen[:, t, :], start=t == 0,
                              stop=t == T - 1)
                last.then_inc(place_psum, 1)

            def gather(x, e):
                pe.wait_ge(x.slot_ready, e + 1)
                for part, src in enumerate((xn_hi, xn_lo)):
                    for k in range(K):
                        for t in range(T):
                            o = HALF * (k % 2)
                            last = MM(pb[4 + 2 * part + k // 2][:, o:o + x.cols], src[:, t, k * P:(k + 1) * P],
                                      to_slot[x.f][:, t, :], start=t == 0, stop=t == T - 1)
                        if k % 2 == 1:
                            last.then_inc(x.xg_psum, 1)

            def bring_back(x, e):
                pe.wait_ge(x.node_ready, e + 1)
                pe.wait_ge(x.yhi, (e + 1) * x.tiles)
                pe.wait_ge(x.ylo, (e + 1) * x.tiles)
                for t in range(T):
                    for s in range(x.tiles):
                        r = x.rows(s)
                        for y in (y_hi, y_lo):
                            last = MM(pb[4 + t][:, :], to_node[0:r, s, t * P:(t + 1) * P], y[0:r, s, :],
                                      start=s == 0 and y is y_hi, stop=s == x.tiles - 1 and y is y_lo)
                    last.then_inc(x.back_psum, 1)

            def into_hidden(x, e, j):
                b, s = j % 2, e * J + j
                first = isinstance(e, int) and e == 0
                if j % 2 == 0:
                    n = e * PAIRS + j // 2
                    pe.wait_ge(x.whi, n * 2 + 2)
                    pe.wait_ge(x.wlo, n * 2 + 2)
                if not (first and j < 2):
                    if x.f == 0:
                        pe.wait_ge(x.up, s - 1)
                        pe.wait_ge(x.gated, s - 1)
                    else:
                        pe.wait_ge(x.act, s - 1)
                if not x.all and j == 0:
                    pe.wait_ge(x.xghi, 2 * e + 2)
                    pe.wait_ge(x.xglo, 2 * e + 2)
                wh, wl = x.hi(j // 2), x.lo(j // 2)
                for part in range(x.parts):
                    for k in range(K):
                        last = mm3(x.hid_bank(part, b), x.hid_w(wh, part, k, b), x.hid_w(wl, part, k, b),
                                   x.x_hi[:, k, :], x.x_lo[:, k, :], k == 0, k == K - 1)
                last.then_inc(x.hid_psum, 1)

            def out_of_hidden(x, e, j):
                s = e * J + j
                pe.wait_ge(x.ahi, s + 1)
                pe.wait_ge(x.alo, s + 1)
                if j == 0 and not (isinstance(e, int) and e == 0):
                    if x.all:
                        pe.wait_ge(x.o_read, e * T)
                    else:
                        pe.wait_ge(x.yhi, e * x.tiles)
                        pe.wait_ge(x.ylo, e * x.tiles)
                wh, wl = x.out_w(x.hi(j // 2), j % 2), x.out_w(x.lo(j // 2), j % 2)
                for t in range(x.tiles):
                    at = slice(t * P, t * P + x.rows(t))
                    last = mm3(x.out_bank(t), x.ah_b[j % 4][:, at], x.al_b[j % 4][:, at], wh, wl, j == 0, j == J - 1)
                    last.then_inc(x.down, 1)

            def turn(f):
                for bank, src in ((4, place), (5, comb)):
                    for t in range(T):
                        last = nc.tensor.transpose(pb[bank][0:NE, t * P:(t + 1) * P], src[:, t, :], ident[:, :])
                last.then_inc(turned_psum, 1)

            def biases(f):
                pe.wait_ge(turned_ready, f + 1)
                for t in range(T):
                    MM(pb[4 + t][:, :], combT[:, t * P:(t + 1) * P], b_out[f][:, :], start=True, stop=True)\
                        .then_inc(bout_psum, 1)

            def spread(f, half):
                if half == 0:
                    pe.wait_ge(bout_added, T * (f + 1))
                else:
                    pe.wait_ge(spread_act, 4 * f + 2)
                    pe.wait_ge(spread_dve, 4 * f + 2)
                for i in range(4):
                    last = MM(pb[4 + i][:, :], sel[:, 4 * half + i, :], posT, start=True, stop=True)
                last.then_inc(spread_psum, 1)

            def experts(f):
                x = ex[f]

                def step(e, j):
                    into_hidden(x, e, j)
                    if isinstance(e, int) and e == 0:
                        if j == 1:
                            turn(f)
                        if j == 2:
                            biases(f)
                        if j in (3, 5):
                            spread(f, (j - 3) // 2)
                    elif j == 3:
                        bring_back(x, e - 1)
                    if j == J - 1 and not (isinstance(e, int) and e == NE - 1):
                        if isinstance(e, int):
                            pe.wait_ge(spread_act, 4 * (f + 1))
                            pe.wait_ge(spread_dve, 4 * (f + 1))
                        else:
                            pe.wait_ge(x.o_read, e * T)
                        gather(x, e + 1)
                    if j == 1 and not (isinstance(e, int) and e == 0):
                        out_of_hidden(x, e - 1, J - 1)
                    if j >= LAG:
                        out_of_hidden(x, e, j - LAG)
                    if j == J - 1:
                        out_of_hidden(x, e, j - 1)

                pe.wait_ge(xnhi_ready, T * (f + 1))
                pe.wait_ge(xnlo_ready, T * (f + 1))
                gather(x, 0)
                for j in range(J):
                    step(0, j)
                with pe.Fori(1, NE - 1) as e:
                    for j in range(J):
                        step(e, j)
                for j in range(J):
                    step(NE - 1, j)
                out_of_hidden(x, NE - 1, J - 1)
                pe.wait_ge(x.o_read, (NE - 1) * T)
                bring_back(x, NE - 1)

            def rest(f):
                x = ov[f]

                def prime():
                    pe.sem_inc(x.hid_psum, J)
                    pe.sem_inc(x.down, J * T)

                def body(e, w):
                    pe.wait_ge(ex[f].o_read, T * NE)
                    for j in range(J):
                        into_hidden(x, e, j)
                        if j >= LAG:
                            out_of_hidden(x, e, j - LAG)
                    for j in range(J - LAG, J):
                        out_of_hidden(x, e, j)

                overflow(f, pe, prime, body)

            transpose_x(1)
            x_split(1)
            pe.wait_ge(x1_ready, T)
            route(0)
            positions(0)
            pe.wait_ge(lapf_ready, T)
            experts(0)
            rest(0)

            transpose_x(2)
            x_split(2)
            pe.wait_ge(laplo_ready, T)

            def through(m, bank, stop):
                for t in range(T):
                    at = slice(t * P, (t + 1) * P)
                    for k in range(K):
                        last = mm3(pb[bank + t][:, :], xT_hi[:, k, at], xT_lo[:, k, at], cheb_at(m, k, 0),
                                   cheb_at(m, k, 1), k == 0, stop and k == K - 1)
                    if stop:
                        last.then_inc(term_psum if m == T else lin_psum, 1)

            def propagate(i, bank):
                pe.wait_ge(bhi_ready, T * i)
                pe.wait_ge(blo_ready, T * i)
                for t in range(T):
                    at = slice(t * P, (t + 1) * P)
                    for r in range(T):
                        last = mm3(pb[bank + t][:, :], lap_hi[:, r, at], lap_lo[:, r, at], bk_hi[:, r, :],
                                   bk_lo[:, r, :], False, r == T - 1)
                    last.then_inc(term_psum, 1)

            through(4, 0, True)
            for i in range(1, 5):
                bank = 4 * (i % 2)
                if i >= 2:
                    pe.wait_ge(term_ready, T * (i - 1))
                through(4 - i, bank, False)
                propagate(i, bank)
            pe.wait_ge(term_ready, 4 * T)
            through(5, 4, True)

            transpose_x(3)
            x_split(3)
            route(1)
            positions(1)
            experts(1)
            rest(1)


_OUT = ("out", (512, 512))


def kernel(**inputs):
    import numpy as _np
    import concourse.bacc as _bacc
    from concourse import mybir as _mybir
    from concourse.bass_utils import run_bass_kernel_spmd as _run

    g = {k: _np.asarray(v) for k, v in inputs.items()}
    laid = {
        "x": g["x"], "src": g["src"], "dst": g["dst"], "edge_weight": g["edge_weight"],
        "attrT": g["edge_attr_16"].reshape(4, -1, 16).transpose(0, 2, 1),
        "Wq": g["L0_gnn_Wq"], "bq": g["L0_gnn_bq"], "Wk": g["L0_gnn_Wk"], "bk": g["L0_gnn_bk"],
        "Wv": g["L0_gnn_Wv"], "bv": g["L0_gnn_bv"], "Wo": g["L0_gnn_Wo"], "bo": g["L0_gnn_bo"],
        "We": g["L0_gnn_We"], "be": g["L0_gnn_be"],
        "router_w": g["L0_ffn_router_w"], "router_b": g["L0_ffn_router_b"],
        "gate_up": g["L0_ffn_gate_up_proj"], "gate_up_bias": g["L0_ffn_gate_up_proj_bias"],
        "down": g["L0_ffn_down_proj"], "down_bias": g["L0_ffn_down_proj_bias"],
        "gamma": g["L1_gnn_ln_gamma"], "beta": g["L1_gnn_ln_beta"],
        "cheb_lin": _np.concatenate([g["L1_gnn_cheb_W"].transpose(0, 2, 1), g["L1_gnn_lin_W"].T[None]]),
        "cheb_b": g["L1_gnn_cheb_b"], "lin_b": g["L1_gnn_lin_b"],
        "WrT": g["L1_ffn_Wr"].T, "br": g["L1_ffn_br"],
        "W1": g["L1_ffn_W1"], "b1": g["L1_ffn_b1"], "W2": g["L1_ffn_W2"], "b2": g["L1_ffn_b2"],
    }
    nc = _bacc.Bacc("TRN2", target_bir_lowering=False, num_devices=1)
    arrays, aps = {}, {}
    for name, v in laid.items():
        v = _np.ascontiguousarray(v)
        arrays[f"in_{name}"] = v
        aps[name] = nc.dram_tensor(f"in_{name}", v.shape, _mybir.dt.from_np(v.dtype), kind="ExternalInput").ap()
    out = nc.dram_tensor(_OUT[0], _OUT[1], _mybir.dt.float32, kind="ExternalOutput").ap()
    build_network(nc, aps, out)
    r = _run(nc, [arrays], core_ids=[0])
    return r.results[0][_OUT[0]]
```

```python
from contextlib import ExitStack

import concourse.bass as bass
from concourse import mybir
from concourse.alu_op_type import AluOpType as ALU

ACT = mybir.ActivationFunctionType
F32 = mybir.dt.float32
F16 = mybir.dt.float16
I32 = mybir.dt.int32
U32 = mybir.dt.uint32
AX_X = mybir.AxisListType.X

P = 128

X_SCALE = 16.0
W_SCALE = 256.0
XW_BACK = 1.0 / (X_SCALE * W_SCALE)
EDGE_SCALE = 4096.0
EB_SCALE = 64.0
LAP_SCALE = 64.0
B_SCALE = 64.0
Y_SCALE = 16.0
LN_EPS = 1e-5
QGELU = 1.702


class Chain:

    def __init__(self, eng, sem):
        self.eng, self.sem, self.base, self.k = eng, sem, 0, 0

    def add(self, ins):
        self.k += 1
        ins.then_inc(self.sem, 1)

    def link(self, ins):
        self.k += 1
        ins.then_inc(self.sem, 1)
        self.eng.wait_ge(self.sem, self.base + self.k)


def build_network(nc, a, out):
    N, D = a["x"].shape
    T = N // P
    K = D // P
    C = a["src"].shape[0] // P
    H, ED = a["WeT"].shape
    HD = D // H
    NG = 32
    GN = N // NG
    GP = P // GN
    NE = a["router_b"].shape[0]
    I0 = a["down"].shape[1]
    I1 = a["W2"].shape[1]
    J = I0 // P
    CAP = (192, 256)
    HALF = 256
    W = 64
    assert I1 == I0 and D == 512 and N == 512 and T == 4 and C % 8 == 0 and GN * H == P

    ctx = ExitStack()
    with ctx:
        def sb(name, shape, dt):
            return ctx.enter_context(nc.sbuf_tensor(name, shape, dt))

        def sem(name):
            return ctx.enter_context(nc.semaphore(name))

        KB = 256
        r_stage = sb("r_stage", [P, 24 * KB], F32)
        r_split = sb("r_split", [P, 48 * KB], F32)
        r_gnn = sb("r_gnn", [P, 48 * KB], F32)
        r_work = sb("r_work", [P, 28 * KB], F32)
        r_mid = sb("r_mid", [P, 16 * KB], F32)
        x_sb = sb("x_sb", [P, T, D], F32)
        r_xT = sb("r_xT", [P, 8 * KB], F32)
        r_lap = sb("r_lap", [P, 8 * KB], F32)

        diag = sb("diag", [P, T, P], F32)

        def view(region, start_kb, n, dt, pattern=None, **sizes):
            per = 2 if dt == F16 else 1
            ap = region[:, int(start_kb * KB):int(start_kb * KB) + n // per]
            if dt != F32:
                ap = ap.bitcast(dt)
            return ap.rearrange(pattern, **sizes) if pattern else ap

        xT_hi = view(r_xT, 0, K * N, F16, "p (k n) -> p k n", k=K)
        xT_lo = view(r_xT, 4, K * N, F16, "p (k n) -> p k n", k=K)
        adj = view(r_split, 40, T * N, F32, "p (t n) -> p t n", t=T)
        lap_hi = view(r_lap, 0, T * N, F16, "p (t n) -> p t n", t=T)
        lap_lo = view(r_lap, 4, T * N, F16, "p (t n) -> p t n", t=T)

        attr = view(r_work, 0, C * ED, F32, "p (c d) -> p c d", d=ED)
        EC = 8
        attr_w = [view(r_work, kb, EC * H * ED, F32, "p (c h d) -> p c h d", h=H, d=ED) for kb in (8, 12, 24, 16, 20)]
        AB = len(attr_w)
        xn = view(r_work, 16, T * D, F32, "p (t d) -> p t d", t=T)
        score_m = [view(r_work, 4 * b, H * P, F32, "p (h j k) -> p h j k", h=H, j=GP) for b in range(2)]
        w_raw = [view(r_split, 8 * m, K * D, F32) for m in range(4)]
        qT = view(r_split, 32, K * N, F32, "p (k n) -> p k n", k=K)
        kT = view(r_split, 40, K * N, F32, "p (k n) -> p k n", k=K)
        qkvo_hi = [view(r_gnn, 8 * m, K * D, F16, "p (k n) -> p k n", k=K) for m in range(4)]
        qkvo_lo = [view(r_gnn, 8 * m + 4, K * D, F16, "p (k n) -> p k n", k=K) for m in range(4)]
        v_sb = view(r_mid, 0, T * D, F32, "p (t d) -> p t d", t=T)
        score = view(r_mid, 8, T * P, F32, "p (t k h) -> p t k h", t=T, k=GN)
        iota_i = view(r_mid, 10, N, F32).bitcast(I32)
        eb_f = view(r_mid, 12, C * H, F32, "p (c h) -> p c h", h=H)
        dl_hot = view(r_gnn, 32, C * GN, F16, "p (c g) -> p c g", g=GN)
        eb_hi = view(r_gnn, 36, C * H, F16, "p (c h) -> p c h", h=H)
        eb_lo = view(r_gnn, 38, C * H, F16, "p (c h) -> p c h", h=H)
        bv_bc = view(r_gnn, 40, D, F32)
        bo_bc = view(r_gnn, 42, D, F32)
        we_bc = view(r_gnn, 44, H * ED, F32, "p (h d) -> p h d", h=H)
        be_bc = view(r_gnn, 45, H, F32)
        src_i = view(r_gnn, 46, C, F32).bitcast(I32)
        dst_i = view(r_gnn, 46.5, C, F32).bitcast(I32)
        w_f = view(r_gnn, 47, C, F32)
        src_r = view(r_mid, 8, P, F32)
        dst_r = view(r_mid, 8.5, P, F32)
        rel_r = view(r_mid, 9, P, F32)

        GC = 4
        AC = 2
        src_hot = [view(r_work, 14 * b, GC * N, F16, "p (c n) -> p c n", c=GC) for b in range(2)]
        dst_hi = [view(r_work, 14 * b + 4, GC * N, F16, "p (c n) -> p c n", c=GC) for b in range(2)]
        dst_lo = [view(r_work, 14 * b + 8, GC * N, F16, "p (c n) -> p c n", c=GC) for b in range(2)]
        ebd = [view(r_work, 14 * b + 12, GC * 2 * P, F16, "p (c s q) -> p c s q", c=GC, s=2) for b in range(2)]

        src_off = diag[:, :, :].rearrange("p t q -> p (t q)").bitcast(F16).rearrange("p (i n) -> p i n", i=2)
        src_neg = view(r_lap, 3.5, C, F32)
        rel_h = view(r_lap, 4, C, F16)
        w_l16 = view(r_lap, 4.25, C, F16)
        rel_hot = [view(r_lap, 4.5 + 0.5 * b, GC * W, F16, "p (c w) -> p c w", c=GC) for b in range(2)]

        prob = [view(r_work, 4 * b, H * P, F32, "p (h j k) -> p h j k", h=H, j=GP) for b in range(2)]
        probT = [view(r_work, 8 + 4 * b, H * P, F32, "p (h q) -> p h q", h=H) for b in range(2)]
        oT_hi = [view(r_work, 16 + 2 * b, K * P, F16, "p (k n) -> p k n", k=K) for b in range(2)]
        oT_lo = [view(r_work, 17 + 2 * b, K * P, F16, "p (k n) -> p k n", k=K) for b in range(2)]
        lap_f = [view(r_work, 2 * t, N, F32) for t in range(T)]

        xg_hi = [view(r_work, 12, K * CAP[f], F16, "p (k n) -> p k n", k=K) for f in range(2)]
        xg_lo = [view(r_work, 14, K * CAP[f], F16, "p (k n) -> p k n", k=K) for f in range(2)]
        pos_bc = view(r_work, 16, NE * N, F16, "p (e n) -> p e n", e=NE)
        to_node = view(r_work, 24, 2 * N, F16, "p (s n) -> p s n", s=2)
        to_slot = [view(r_work, 26, T * CAP[f], F16, "p (t n) -> p t n", t=T) for f in range(2)]
        sel = view(r_work, 24, NE * P, F16, "p (e q) -> p e q", e=NE)[0:NE, :, :]
        posT = view(r_work, 26, N, F16)[0:NE, :]
        xn_hi = view(r_mid, 8, T * D, F16, "p (t d) -> p t d", t=T)
        xn_lo = view(r_mid, 12, T * D, F16, "p (t d) -> p t d", t=T)

        cheb_raw = view(r_mid, 0, K * D, F32, "p (k n) -> p k n", k=K)
        cheb_all = r_gnn[:, :].bitcast(F16)
        bk = [view(r_mid, 8 * b, T * D, F32, "p (t d) -> p t d", t=T) for b in range(2)]
        bk_hi = view(r_work, 0, T * D, F16, "p (t d) -> p t d", t=T)
        bk_lo = view(r_work, 4, T * D, F16, "p (t d) -> p t d", t=T)
        xT_f = [view(r_work, 2 * k, N, F32) for k in range(K)]
        out_t = [view(r_work, 16 + 2 * t, D, F32) for t in range(T)]

        iota_n = sb("iota_n", [P, N], F16)
        ident = sb("ident", [P, P], F32)
        ones = sb("ones", [P, P], F32)
        mask = sb("mask", [P, GP], F32)
        iota_e = sb("iota_e", [P, 8], F32)
        zeros = sb("zeros", [P, P], F16)
        span = sb("span", [C, 3], F32)
        base_i = view(r_lap, 3, C, F32)[0:1, :].bitcast(I32)
        flag_f = sb("flag_f", [1, 2], F32)
        flag_i = sb("flag_i", [1, 1], I32)
        src_f = view(r_lap, 0, C, F32)
        dst_f = view(r_lap, 0.5, C, F32)
        dl_h = view(r_lap, 2.5, C, F16)
        w_hi = view(r_lap, 1, C, F32)
        w_lo = view(r_lap, 1.5, C, F32)
        w_h16 = view(r_lap, 2.75, C, F16)
        neg_half = sb("neg_half", [P, T], F32)
        stats = sb("stats", [P, T, 6], F32)
        mv = sb("mv", [P, T, 2], F32)
        var_eps = sb("var_eps", [P, T], F32)
        rstd = sb("rstd", [P, T], F32)
        rstd1 = sb("rstd1", [P, T], F32)
        hmax = sb("hmax", [P, T, H], F32)
        hsum = sb("hsum", [P, T, H], F32)
        deg = sb("deg", [P, T], F32)
        has = sb("has", [P, T], F32)
        ndinv = sb("ndinv", [P, T], F32)
        dinv = sb("dinv", [P, T], F32)
        cols = sb("cols", [P, 4, K], F32)
        rows = [view(r_mid, 0.5 * i, P, F32) for i in range(2)]
        cb_bc = sb("cb_bc", [P, D], F32)
        lb_bc = sb("lb_bc", [P, D], F32)
        rt_raw = [sb(f"rt_raw{f}", [P, K, NE], F32) for f in range(2)]
        rt_hi = [sb(f"rt_hi{f}", [P, K, NE], F16) for f in range(2)]
        rt_lo = [sb(f"rt_lo{f}", [P, K, NE], F16) for f in range(2)]
        rt_b = [sb(f"rt_b{f}", [P, NE], F32) for f in range(2)]
        b_in = [sb("b_in0", [P, NE, 2 * J], F32), sb("b_in1", [P, NE, J], F32)]
        b_sig = sb("b_sig", [P, NE, J], F32)
        b_out = [sb(f"b_out{f}", [NE, D], F32) for f in range(2)]
        logit = sb("logit", [P, T, NE], F32)
        rsum = sb("rsum", [P, T], F32)
        rmax = sb("rmax", [P, T], F32)
        top = sb("top", [P, T, 8], F32)
        top_i = sb("top_i", [P, T, 8], U32)
        top_f = sb("top_f", [P, T, 8], F32)
        tw = sb("tw", [P, T, 2], F32)
        pick = sb("pick", [P, 2, T, NE], F32)
        comb = sb("comb", [P, T, NE], F32)
        comb_s = sb("comb_s", [P, T, NE], F32)
        over_share = sb("over_share", [P, T, NE], F32)
        y_hi = cb_bc[:, :].bitcast(F16).rearrange("p (s d) -> p s d", s=2)
        y_lo = lb_bc[:, :].bitcast(F16).rearrange("p (s d) -> p s d", s=2)
        combT = cb_bc[0:NE, :]
        chosen = sb("chosen", [P, T, NE], F16)
        place = sb("place", [P, T, NE], F32)
        before_me = sb("before_me", [P, P], F16)
        ones_h = sb("ones_h", [P, P], F16)
        slot_i = sb("slot_i", [P, 2], I32)
        slot_id = sb("slot_id", [P, 2], F32)
        rank_e = sb("rank_e", [1, NE], F32)
        over_f = sb("over_f", [1, 2 * NE], F32)
        over_i = [sb(f"over_i{f}", [1, 2 * NE], I32) for f in range(2)]
        settled = sb("settled", [1, 32], F32)

        pb = [ctx.enter_context(nc.psum_tensor(f"pb{i}", [P, 512], F32)) for i in range(8)]

        rows_psum = sem("rows_psum")
        rows_read = sem("rows_read")
        x_in = sem("x_in")
        edges_in = sem("edges_in")
        edge_rows = sem("edge_rows")
        edge_cols = sem("edge_cols")
        base_ready = sem("base_ready")
        attr_in = sem("attr_in")
        wraw_in = [sem(f"wraw_in{m}") for m in range(4)]
        small_in = sem("small_in")
        tables = sem("tables")
        iota_step = sem("iota_step")
        dch = sem("dve_chain")
        ach = sem("act_chain")
        var_ready = sem("var_ready")
        rstd_ready = sem("rstd_ready")
        xn_ready = sem("xn_ready")
        attr_mul = sem("attr_mul")
        eb_sum = sem("eb_sum")
        edge_bias = sem("edge_bias")
        xt_psum = sem("xt_psum")
        xf_ready = sem("xf_ready")
        xhi_ready = sem("xhi_ready")
        xlo_ready = sem("xlo_ready")
        qw_hi = sem("qw_hi")
        qw_lo = sem("qw_lo")
        qk_psum = sem("qk_psum")
        qk_ready = sem("qk_ready")
        v_psum = sem("v_psum")
        v_ready = sem("v_ready")
        score_psum = sem("score_psum")
        score_read = sem("score_read")
        hot_ready = sem("hot_ready")
        hot_used = sem("hot_used")
        off_ready = sem("off_ready")
        hot_act = sem("hot_act")
        rel_ready = sem("rel_ready")
        scatter_psum = sem("scatter_psum")
        adj_ready = sem("adj_ready")
        logits_ready = sem("logits_ready")
        exp_ready = sem("exp_ready")
        prob_ready = sem("prob_ready")
        probT_psum = sem("probT_psum")
        probT_ready = sem("probT_ready")
        o_psum = sem("o_psum")
        ohi_ready = sem("ohi_ready")
        olo_ready = sem("olo_ready")
        proj_psum = sem("proj_psum")
        x1_ready = sem("x1_ready")
        deg_ready = sem("deg_ready")
        dinv_pow = sem("dinv_pow")
        diag_ready = sem("diag_ready")
        dinv_psum = sem("dinv_psum")
        lapf_ready = sem("lapf_ready")
        laphi_ready = sem("laphi_ready")
        laplo_ready = sem("laplo_ready")
        rt_split = sem("rt_split")
        rt_split_lo = sem("rt_split_lo")
        rt_psum = sem("rt_psum")
        rt_logit = sem("rt_logit")
        rt_exp = sem("rt_exp")
        comb_ready = sem("comb_ready")
        place_psum = sem("place_psum")
        over_ready = sem("over_ready")
        pass_done = sem("pass_done")
        turned_psum = sem("turned_psum")
        turned_ready = sem("turned_ready")
        bout_psum = sem("bout_psum")
        bout_added = sem("bout_added")
        spread_psum = sem("spread_psum")
        spread_act = sem("spread_act")
        spread_dve = sem("spread_dve")
        xnhi_ready = sem("xnhi_ready")
        xnlo_ready = sem("xnlo_ready")
        late_in = sem("late_in")
        cheb_in = sem("cheb_in")
        cheb_hi = sem("cheb_hi")
        cheb_lo = sem("cheb_lo")
        term_psum = sem("term_psum")
        term_ready = sem("term_ready")
        bhi_ready = sem("bhi_ready")
        blo_ready = sem("blo_ready")
        lin_psum = sem("lin_psum")
        out_done = sem("out_done")

        class Expert:

            def __init__(self, f, all):
                self.f, self.all = f, all
                self.cols = N if all else CAP[f]
                self.tiles = -(-self.cols // P)
                self.parts = 2 - f
                self.pair = (self.parts * K * 2 * P) + 2 * D
                g = f"f{f}_" + ("all_" if all else "")
                self.w_in = [sem(f"{g}w_in{b}") for b in range(2)]
                self.whi = sem(f"{g}whi_ready")
                self.wlo = sem(f"{g}wlo_ready")
                self.hid_psum = sem(f"{g}hid_psum")
                if f == 0:
                    self.sig = sem(f"{g}sig_ready")
                    self.up = sem(f"{g}up_ready")
                    self.gated = sem(f"{g}gated_ready")
                self.act = sem(f"{g}act_ready")
                self.ahi = sem(f"{g}ahi_ready")
                self.alo = sem(f"{g}alo_ready")
                self.down = sem(f"{g}down_done")
                self.o_read = sem(f"{g}out_read")
                kb = 2 if all else 1
                n = self.cols
                self.sg_b = [view(r_work, kb * b, n, F32) for b in range(2)]
                self.up_b = [view(r_work, kb * (2 + b), n, F32) for b in range(2)]
                self.ga_b = [view(r_work, kb * (4 + b), n, F32) for b in range(2)]
                self.ac_b = [view(r_work, kb * (6 + b), n, F32) for b in range(2)]
                self.ah_b = [view(r_work, kb * (8 + b / 2), n, F16) for b in range(4)]
                self.al_b = [view(r_work, kb * (10 + b / 2), n, F16) for b in range(4)]
                if all:
                    self.share = sem(f"{g}share_step")
                    self.x_hi, self.x_lo = xT_hi, xT_lo
                else:
                    self.x_hi, self.x_lo = xg_hi[f], xg_lo[f]
                    self.slot_ready = sem(f"{g}slot_ready")
                    self.node_ready = sem(f"{g}node_ready")
                    self.xg_psum = sem(f"{g}xg_psum")
                    self.xghi = sem(f"{g}xghi_ready")
                    self.xglo = sem(f"{g}xglo_ready")
                    self.yhi = sem(f"{g}yhi_ready")
                    self.ylo = sem(f"{g}ylo_ready")
                    self.back_psum = sem(f"{g}back_psum")

            def hid_bank(self, part, b):
                if self.all:
                    return pb[2 * part + b][:, :]
                return pb[b][:, HALF * part:HALF * part + self.cols]

            def rows(self, t):
                return min(P, self.cols - P * t)

            def out_bank(self, t):
                return pb[(4 if self.all else 2) + t][0:self.rows(t), :]

            def stage(self, b):
                return view(r_stage, 12 * b, self.pair, F32)

            def hi(self, slot):
                return view(r_split, 12 * slot, self.pair, F16)

            def lo(self, slot):
                return view(r_split, 12 * slot + 6, self.pair, F16)

            def hid_w(self, ap, part, k, jo):
                o = part * K * 2 * P + k * 2 * P + jo * P
                return ap[:, o:o + P]

            def out_w(self, ap, jo):
                o = self.parts * K * 2 * P + jo * D
                return ap[:, o:o + D]

        ex = [Expert(f, False) for f in range(2)]
        ov = [Expert(f, True) for f in range(2)]
        PAIRS = J // 2
        AHEAD = 2
        LAG = 2

        block = ctx.enter_context(nc.Block())

        def bc(ap, pos, n):
            shape = list(ap.shape)
            u = ap.unsqueeze(pos)
            shape.insert(pos, n)
            return u.to_broadcast(shape)


        def at_expert(ap, e, col):
            return ap[:, bass.ds(e, 1), col:col + 1].rearrange("p e c -> p (e c)")

        def at_tile(ap, t, e):
            return ap[:, t:t + 1, bass.ds(e, 1)].rearrange("p t e -> p (t e)")

        def overflow(f, eng, body, last=False):
            eng.wait_ge(over_ready, f + 1)
            some = eng.value_load(over_i[f][0:1, 0:1], min_val=0, max_val=1)
            with eng.If(some):
                with eng.Fori(1, 2 * N // (CAP[f] + 1) + 1) as e:
                    here = eng.value_load(over_i[f][0:1, bass.ds(e - 1, 1)], min_val=0, max_val=1)
                    with eng.If(here):
                        w = eng.value_load(over_i[f][0:1, bass.ds(e + (NE - 1), 1)], min_val=0, max_val=NE - 1)
                        body(e, w)
            if not last:
                eng.wait_ge(pass_done, f + 1)

        def cheb_at(m, k, part):
            o = (m * 2 + part) * (K * D) + k * D
            return cheb_all[:, o:o + D]

        def cheb_part(m, k, part):
            return cheb_all[:, bass.ds(m * (2 * K * D) + (part * K * D + k * D), D)]

        @block.sync
        def _(sp):
            sp.dma_start(x_sb[:, :, :], a["x"].rearrange("(t p) d -> p t d", p=P)).then_inc(x_in, 16)
            for dst, name in ((src_i, "src"), (dst_i, "dst"), (w_f, "edge_weight")):
                sp.dma_start(dst, a[name].rearrange("(c p) -> c p", p=P)).then_inc(edges_in, 16)
            for m, name in enumerate(("Wq", "Wk", "Wv", "Wo")):
                sp.dma_start(w_raw[m].rearrange("p (k n) -> p k n", k=K),
                             a[name].rearrange("(k p) n -> p k n", p=P)).then_inc(wraw_in[m], 16)
                if m == 0:
                    sp.dma_start(attr, a["attr"]).then_inc(attr_in, 16)
                    sp.dma_start(we_bc.rearrange("p h d -> p (h d)"),
                                 a["WeT"].rearrange("h d -> (h d)").partition_broadcast(P)).then_inc(attr_in, 16)

            def load_pair(x, w, q):
                st, n = x.stage(q % 2), 2 * P
                if x.f == 0:
                    into = [a["gate_up"][:, :, i * I0:(i + 1) * I0] for i in range(2)]
                    down = a["down"]
                else:
                    into, down = [a["W1"]], a["W2"]
                for part, s in enumerate(into):
                    o = part * K * n
                    s = s.rearrange("e (k p) i -> p e k i", p=P)
                    sp.dma_start(st[:, o:o + K * n].rearrange("p (k i) -> p k i", k=K),
                                 s[:, bass.ds(w, 1), :, q * n:(q + 1) * n].rearrange("p e k i -> p (e k) i"))\
                        .then_inc(x.w_in[q % 2], 16)
                o = x.parts * K * n
                down = down.rearrange("e (j p) d -> p e j d", p=P)
                sp.dma_start(st[:, o:o + 2 * D].rearrange("p (j d) -> p j d", j=2),
                             down[:, bass.ds(w, 1), 2 * q:2 * q + 2, :].rearrange("p e j d -> p (e j) d"))\
                    .then_inc(x.w_in[q % 2], 16)

            def stage_free(x, n):
                sp.wait_ge(x.whi, 2 * (n - 1))
                sp.wait_ge(x.wlo, 2 * (n - 1))

            def prime(f):
                x = ov[f]
                for b in range(2):
                    sp.sem_inc(x.w_in[b], 16 * (x.parts + 1) * (PAIRS // 2))

            def rest(f):
                x = ov[f]

                def body(e, w):
                    sp.wait_ge(ex[f].whi, 2 * PAIRS * NE)
                    sp.wait_ge(ex[f].wlo, 2 * PAIRS * NE)
                    for q in range(PAIRS):
                        stage_free(x, e * PAIRS + q)
                        load_pair(x, w, q)

                overflow(f, sp, body)

            for f in range(2):
                x = ex[f]
                prime(f)
                if f == 1:
                    sp.wait_ge(ex[0].whi, 2 * PAIRS * NE)
                    sp.wait_ge(ex[0].wlo, 2 * PAIRS * NE)
                for q in range(PAIRS):
                    if q >= 2:
                        stage_free(x, q)
                    load_pair(x, 0, q)
                if f == 0:
                    sp.wait_ge(o_psum, T)
                    sp.wait_ge(prob_ready, T)

                def load_expert(e, matrix):
                    for q in range(PAIRS):
                        stage_free(x, e * PAIRS + q)
                        load_pair(x, e, q)
                        if matrix and q == 1:
                            if not isinstance(e, int):
                                sp.wait_ge(cheb_hi, (e - 1) * K)
                                sp.wait_ge(cheb_lo, (e - 1) * K)
                            m = a["cheb_lin"].rearrange("m (k p) n -> p m k n", p=P)
                            sp.dma_start(cheb_raw, m[:, bass.ds(e - 1, 1), :, :].rearrange("p m k n -> p (m k) n"))\
                                .then_inc(cheb_in, 16)

                load_expert(1, f == 0)
                with sp.Fori(2, NE - 1) as e:
                    load_expert(e, f == 0)
                load_expert(NE - 1, False)
                rest(f)
            for t in range(T):
                sp.wait_ge(ex[1].o_read, T * (NE - 1) + t + 1)
                sp.dma_start(out.rearrange("(t p) d -> p t d", p=P)[:, t, :], x_sb[:, t, :]).then_inc(out_done, 16)
            sp.wait_ge(out_done, 16 * T)

        @block.gpsimd
        def _(pool):
            nc.gpsimd.memset(ident[:, :], 0.0).then_inc(iota_step, 1)
            nc.gpsimd.memset(mask[:, :], 1.0).then_inc(iota_step, 1)
            nc.gpsimd.memset(zeros[:, :], 0.0).then_inc(tables, 1)
            nc.gpsimd.iota(iota_i, pattern=[[1, N]], base=0, channel_multiplier=0).then_inc(iota_step, 1)
            pool.wait_ge(iota_step, 3)
            nc.gpsimd.affine_select(out=ident[:, :], in_=ident[:, :], compare_op=ALU.not_equal, fill=1.0,
                                    base=0, pattern=[[-1, P]], channel_multiplier=1).then_inc(tables, 1)
            nc.gpsimd.affine_select(out=mask[:, :], in_=mask[:, :], compare_op=ALU.is_ge, fill=0.0,
                                    base=0, pattern=[[-GN, GP]], channel_multiplier=1).then_inc(iota_step, 1)
            pool.wait_ge(iota_step, 4)
            nc.gpsimd.affine_select(out=mask[:, :], in_=mask[:, :], compare_op=ALU.is_ge, fill=0.0,
                                    base=GN - 1, pattern=[[GN, GP]], channel_multiplier=-1).then_inc(tables, 1)
            nc.gpsimd.tensor_copy(iota_n[:, :], iota_i).then_inc(tables, 1)
            nc.gpsimd.tensor_copy(iota_e[:, :], iota_i[:, 0:8]).then_inc(tables, 1)
            nc.gpsimd.memset(neg_half[:, :], -0.5).then_inc(tables, 1)
            nc.gpsimd.memset(ones[:, :], 1.0).then_inc(tables, 1)
            nc.gpsimd.memset(ones_h[:, :], 1.0).then_inc(tables, 1)
            nc.gpsimd.iota(slot_i[:, :], pattern=[[P, 2]], base=0, channel_multiplier=1).then_inc(iota_step, 1)
            pool.wait_ge(iota_step, 5)
            nc.gpsimd.tensor_copy(slot_id[:, :], slot_i[:, :]).then_inc(tables, 1)

            def inv_sqrt(n):
                pool.wait_ge(var_ready, n + 1)
                nc.gpsimd.tensor_tensor(rstd[:, :], var_eps[:, :], neg_half[:, :], ALU.pow).then_inc(rstd_ready, 1)

            pool.wait_ge(tables, 9)
            inv_sqrt(0)
            pool.wait_ge(attr_in, 32)
            for i in range(C // EC):
                if i == 3:
                    pool.wait_ge(xhi_ready, K)
                if i >= AB:
                    pool.wait_ge(eb_sum, i - AB + 1)
                nc.gpsimd.tensor_tensor(attr_w[i % AB], bc(attr[:, EC * i:EC * (i + 1), :], 2, H), bc(we_bc, 1, EC),
                                        ALU.mult).then_inc(attr_mul, 1)
            pool.wait_ge(deg_ready, 1)
            nc.gpsimd.tensor_tensor(dinv[:, :], deg[:, :], neg_half[:, :], ALU.pow).then_inc(dinv_pow, 1)
            for n in range(1, 5):
                inv_sqrt(n)

        @block.scalar
        def _(act):
            ch = Chain(act, ach)
            rows1 = [("b1", 0, NE * J), ("bq", NE * J, K), ("bk", NE * J + K, K),
                     ("gamma", NE * J + 2 * K, K), ("beta", NE * J + 3 * K, K)]
            act.dma_start(rows[0][:, :], a["gate_up_bias"].rearrange("e (j p) -> (e j) p", p=P)).then_inc(small_in, 16)
            for name, r, n in rows1:
                s = a[name].rearrange("e (j p) -> (e j) p" if name == "b1" else "(j p) -> j p", p=P)
                act.dma_start(rows[1][r:r + n, :], s).then_inc(small_in, 16)
            for dst, name in ((bv_bc, "bv"), (bo_bc, "bo"), (be_bc, "be"), (rt_b[0][:, :], "router_b"), (rt_b[1][:, :], "br")):
                act.dma_start(dst, a[name].partition_broadcast(P)).then_inc(small_in, 16)
            for f, name in enumerate(("router_w", "WrT")):
                act.dma_start(rt_raw[f][:, :, :], a[name].rearrange("(k p) e -> p k e", p=P)).then_inc(small_in, 16)
            for f, name in enumerate(("down_bias", "b2")):
                act.dma_start(b_out[f][:, :], a[name]).then_inc(small_in, 16)

            def x_hi(n):
                for k in range(K):
                    act.wait_ge(xt_psum, K * n + k + 1)
                    nc.scalar.activation(xT_hi[:, k, :], pb[4 + k][:, :], ACT.Copy, scale=X_SCALE)\
                        .then_inc(xhi_ready, 1)

            def node_hi(f):
                act.wait_ge(xn_ready, T * (2 if f == 0 else 4))
                for t in range(T):
                    nc.scalar.activation(xn_hi[:, t, :], xn[:, t, :], ACT.Copy, scale=X_SCALE)\
                        .then_inc(xnhi_ready, 1)

            def weight_hi(x, e, q, half, slot_free=None):
                if half == 0:
                    act.wait_ge(x.w_in[q % 2], (e * (PAIRS // 2) + q // 2 + 1) * (16 * (x.parts + 1)))
                    if slot_free is not None:
                        act.wait_ge(x.down, slot_free * x.tiles)
                o, w = half * x.pair // 2, x.pair // 2
                nc.scalar.activation(x.hi(q % PAIRS)[:, o:o + w], x.stage(q % 2)[:, o:o + w], ACT.Copy,
                                     scale=W_SCALE).then_inc(x.whi, 1)

            x_hi(0)
            for m in range(4):
                act.wait_ge(wraw_in[m], 16)
                nc.scalar.activation(qkvo_hi[m], w_raw[m].rearrange("p (k n) -> p k n", k=K), ACT.Copy,
                                     scale=W_SCALE).then_inc(qw_hi, 1)
            act.wait_ge(small_in, 16 * 15)
            for f in range(2):
                nc.scalar.activation(rt_hi[f][:, :, :], rt_raw[f][:, :, :], ACT.Copy, scale=W_SCALE)\
                    .then_inc(rt_split, 1)
            act.wait_ge(rows_read, 1)
            for i in range(2 * K):
                act.wait_ge(qk_psum, i + 1)
                dst, c = (qT, i) if i < K else (kT, i - K)
                nc.scalar.activation(dst[:, c, :], pb[(4 + i) % 8][:, :], ACT.Identity, bias=cols[:, i // K, c:c + 1],
                                     scale=XW_BACK).then_inc(qk_ready, 1)
            act.wait_ge(qw_lo, 4)
            for q in range(AHEAD):
                for half in range(2):
                    weight_hi(ex[0], 0, q, half)

            def sources(i, b, free):
                if free:
                    act.wait_ge(hot_used, i * 2 + (b - 1))
                if free or b > 0:
                    act.wait_ge(hot_act, i * (2 * AC) + b * AC)
                for c in range(AC):
                    one = bass.ds(i * (2 * GC) + (b * GC + c), 1)
                    nc.scalar.activation(src_off[:, c, :], iota_n[:, :], ACT.Abs, bias=src_neg[:, one])\
                        .then_inc(off_ready, 1)
                for c in range(AC):
                    act.wait_ge(off_ready, i * (2 * AC) + (b * AC + c + 1))
                    nc.scalar.activation(src_hot[b][:, c, :], src_off[:, c, :], ACT.Relu, bias=ones[:, 0:1],
                                         scale=-1.0).then_inc(hot_act, 1)

            act.wait_ge(base_ready, 1)
            act.wait_ge(edge_bias, 1)
            for b in range(2):
                sources(0, b, False)
            with act.Fori(1, C // (2 * GC)) as i:
                for b in range(2):
                    sources(i, b, True)

            act.wait_ge(scatter_psum, 1)
            act.wait_ge(score_psum, T)
            for t in range(T):
                nc.scalar.activation(adj[:, t, :], pb[t][:, :], ACT.Copy, scale=1.0 / EDGE_SCALE,
                                     accum_out=deg[:, t:t + 1]).then_inc(adj_ready, 1)
            act.wait_ge(logits_ready, 1)
            nc.scalar.activation(score, score, ACT.Exp).then_inc(exp_ready, 1)

            def prob_t(t):
                act.wait_ge(probT_psum, t + 1)
                if t >= 2:
                    act.wait_ge(o_psum, t - 1)
                b0 = 6 if t % 2 == 0 else 4
                for i in range(2):
                    nc.scalar.activation(probT[t % 2][:, 4 * i:4 * i + 4, :],
                                         pb[b0 + i][:, :].rearrange("p (h q) -> p h q", h=4), ACT.Copy)\
                        .then_inc(probT_ready, 1)

            def head_out(t):
                act.wait_ge(o_psum, t + 1)
                if t >= 2:
                    act.wait_ge(proj_psum, t - 1)
                nc.scalar.activation(oT_hi[t % 2], pb[t % 2][:, :].rearrange("p (k n) -> p k n", k=K), ACT.Copy,
                                     scale=X_SCALE).then_inc(ohi_ready, 1)

            for t in range(T + 1):
                if t < T:
                    prob_t(t)
                if t >= 1:
                    head_out(t - 1)

            x_hi(1)
            node_hi(0)

            act.wait_ge(rt_logit, 2)
            nc.scalar.activation(tw[:, :, 1], rsum[:, :], ACT.Exp).then_inc(rt_exp, 1)
            for t in range(T):
                act.wait_ge(lapf_ready, t + 1)
                nc.scalar.activation(lap_hi[:, t, :], lap_f[t], ACT.Copy).then_inc(laphi_ready, 1)

            def expert_step(x, e, w, j, prepare, matrix=False, slot_wait=True):
                b, s = j % 2, e * J + j
                first = isinstance(e, int) and e == 0
                act.wait_ge(x.hid_psum, s + 1)
                if x.f == 0:
                    if not (first and j < 2):
                        act.wait_ge(x.act, s - 1)
                    nc.scalar.activation(x.sg_b[b], x.hid_bank(0, b), ACT.Sigmoid, bias=at_expert(b_sig, w, j),
                                         scale=QGELU * XW_BACK).then_inc(x.sig, 1)
                    nc.scalar.activation(x.up_b[b], x.hid_bank(1, b), ACT.Identity,
                                         bias=at_expert(b_in[0], w, J + j),
                                         scale=XW_BACK * X_SCALE * XW_BACK).then_inc(x.up, 1)
                else:
                    if not (first and j < 2):
                        act.wait_ge(x.alo, s - 1)
                    nc.scalar.activation(x.ac_b[b], x.hid_bank(0, b), ACT.Gelu, bias=at_expert(b_in[1], w, j),
                                         scale=XW_BACK).then_inc(x.act, 1)
                if not x.all and j == 0 and not first:
                    output_hi(x, e - 1)
                if prepare:
                    q = j // 2 + AHEAD
                    weight_hi(x, e, q, j % 2, s - j % 2 - 2 if slot_wait and not (first and q < PAIRS) else None)
                if matrix and 2 <= j < 2 + K:
                    if j == 2:
                        act.wait_ge(cheb_in, e * 16)
                    nc.scalar.activation(cheb_part(e - 1, j - 2, 0), cheb_raw[:, j - 2, :], ACT.Copy,
                                         scale=W_SCALE).then_inc(cheb_hi, 1)
                if not x.all and j == J - 1 and not (isinstance(e, int) and e == NE - 1):
                    gathered_hi(x, e + 1)
                act.wait_ge(x.act, s + 1)
                if not (first and j < 4):
                    act.wait_ge(x.down, (s - 3) * x.tiles)
                nc.scalar.activation(x.ah_b[j % 4], x.ac_b[b], ACT.Copy,
                                     scale=1.0 if x.f == 0 else X_SCALE).then_inc(x.ahi, 1)

            def gathered_hi(x, e):
                for i in range(2):
                    act.wait_ge(x.xg_psum, e * 4 + (i + 1))
                    nc.scalar.activation(x.x_hi[:, 2 * i:2 * i + 2, :],
                                         pb[4 + i][:, :].rearrange("p (k n) -> p k n", k=2)[:, :, 0:x.cols],
                                         ACT.Copy).then_inc(x.xghi, 1)

            def output_hi(x, e):
                for t in range(x.tiles):
                    r = x.rows(t)
                    act.wait_ge(x.down, e * (J * x.tiles) + ((J - 1) * x.tiles + t + 1))
                    nc.scalar.activation(y_hi[0:r, t, :], x.out_bank(t), ACT.Copy, scale=Y_SCALE * XW_BACK)\
                        .then_inc(x.yhi, 1)

            def spread_read(f, half):
                act.wait_ge(spread_psum, 2 * f + half + 1)
                for i in range(2):
                    nc.scalar.activation(pos_bc[:, 4 * half + i, :], pb[4 + i][:, :], ACT.Copy)\
                        .then_inc(spread_act, 1)

            def experts(f):
                x = ex[f]
                gathered_hi(x, 0)
                if f == 0:
                    act.wait_ge(laplo_ready, T)
                for j in range(J):
                    expert_step(x, 0, 0, j, True)
                    if j in (2, 4):
                        spread_read(f, (j - 2) // 2)
                with act.Fori(1, NE - 1) as e:
                    for j in range(J):
                        expert_step(x, e, e, j, True, f == 0)
                for j in range(J):
                    expert_step(x, NE - 1, NE - 1, j, j // 2 + AHEAD < PAIRS)
                output_hi(x, NE - 1)

            def prime(f):
                x = ov[f]
                act.sem_inc(x.whi, 2 * PAIRS)
                act.sem_inc(x.ahi, J)
                if f == 0:
                    act.sem_inc(x.sig, J)
                    act.sem_inc(x.up, J)
                else:
                    act.sem_inc(x.act, J)

            def rest(f):
                x = ov[f]

                def body(e, w):
                    act.wait_ge(ex[f].down, NE * J * ex[f].tiles)
                    act.wait_ge(x.down, e * (J * T))
                    for q in range(AHEAD):
                        for half in range(2):
                            weight_hi(x, e, q, half)
                    for j in range(J):
                        expert_step(x, e, w, j, j // 2 + AHEAD < PAIRS, slot_wait=False)

                overflow(f, act, body)

            prime(0)
            experts(0)
            rest(0)
            act.wait_ge(ex[0].o_read, T * NE)
            act.dma_start(cb_bc[:, :], a["cheb_b"].partition_broadcast(P)).then_inc(late_in, 16)
            act.dma_start(lb_bc[:, :], a["lin_b"].partition_broadcast(P)).then_inc(late_in, 16)

            for k in range(K):
                act.wait_ge(xt_psum, 2 * K + k + 1)
                nc.scalar.activation(xT_f[k], pb[4 + k][:, :], ACT.Identity, bias=cols[:, 3, k:k + 1],
                                     scale=cols[:, 2, k:k + 1]).then_inc(xf_ready, 1)
                act.wait_ge(xf_ready, k + 1)
                nc.scalar.activation(xT_hi[:, k, :], xT_f[k], ACT.Copy).then_inc(xhi_ready, 1)
            act.wait_ge(ex[0].down, NE * J * ex[0].tiles)
            for q in range(AHEAD):
                for half in range(2):
                    weight_hi(ex[1], 0, q, half)
            for i in range(4):
                for t in range(T):
                    act.wait_ge(term_ready, T * i + t + 1)
                    if i >= 1:
                        act.wait_ge(term_psum, T * (i + 1))
                    nc.scalar.activation(bk_hi[:, t, :], bk[i % 2][:, t, :], ACT.Copy,
                                         scale=B_SCALE if i < 3 else B_SCALE / 2).then_inc(bhi_ready, 1)
            x_hi(3)
            node_hi(1)
            act.wait_ge(rt_logit, 4)
            nc.scalar.activation(logit[:, :, :], logit[:, :, :], ACT.Exp).then_inc(rt_exp, 1)
            prime(1)
            experts(1)
            rest(1)

        @block.vector
        def _(dve):
            ch = Chain(dve, dch)
            V = nc.vector

            def layernorm(n, dst, again=False):
                for t in range(T - 1):
                    ch.add(V.bn_stats(stats[:, t, :], x_sb[:, t, :]))
                ch.link(V.bn_stats(stats[:, T - 1, :], x_sb[:, T - 1, :]))
                for t in range(T - 1):
                    ch.add(V.bn_aggr(mv[:, t, :], stats[:, t, :]))
                ch.link(V.bn_aggr(mv[:, T - 1, :], stats[:, T - 1, :]))
                V.tensor_scalar(var_eps[:, :], mv[:, :, 1], LN_EPS, None, ALU.add).then_inc(var_ready, 1)
                dve.wait_ge(rstd_ready, n + 1)
                if again:
                    ch.link(V.tensor_copy(rstd1[:, :], rstd[:, :]))
                    ch.link(V.tensor_tensor(var_eps[:, :], mv[:, :, 1], rstd1[:, :], ALU.mult))
                    ch.link(V.tensor_tensor(var_eps[:, :], var_eps[:, :], rstd1[:, :], ALU.mult))
                    V.tensor_scalar(var_eps[:, :], var_eps[:, :], LN_EPS, None, ALU.add).then_inc(var_ready, 1)
                    dve.wait_ge(rstd_ready, n + 2)
                    ch.link(V.tensor_tensor(rstd[:, :], rstd[:, :], rstd1[:, :], ALU.mult))
                for t in range(T):
                    V.tensor_scalar(dst[:, t, :], x_sb[:, t, :], mv[:, t, 0:1], rstd[:, t:t + 1], ALU.subtract,
                                    ALU.mult).then_inc(xn_ready, 1)

            def x_lo(n):
                for k in range(K):
                    dve.wait_ge(xhi_ready, K * n + k + 1)
                    V.scalar_tensor_tensor(xT_lo[:, k, :], pb[4 + k][:, :], X_SCALE, xT_hi[:, k, :], ALU.mult,
                                           ALU.subtract).then_inc(xlo_ready, 1)

            def node_lo(f):
                for t in range(T):
                    dve.wait_ge(xnhi_ready, T * f + t + 1)
                    V.scalar_tensor_tensor(xn_lo[:, t, :], xn[:, t, :], X_SCALE, xn_hi[:, t, :], ALU.mult,
                                           ALU.subtract).then_inc(xnlo_ready, 1)

            def weight_lo(x, e, q, half):
                dve.wait_ge(x.whi, (e * PAIRS + q) * 2 + half + 1)
                o, w = half * x.pair // 2, x.pair // 2
                V.scalar_tensor_tensor(x.lo(q % PAIRS)[:, o:o + w], x.stage(q % 2)[:, o:o + w], W_SCALE,
                                       x.hi(q % PAIRS)[:, o:o + w], ALU.mult, ALU.subtract).then_inc(x.wlo, 1)

            dve.wait_ge(x_in, 16)
            layernorm(0, xn)
            dve.wait_ge(edges_in, 48)
            dve.wait_ge(tables, 9)
            V.tensor_scalar(rank_e[:, :], iota_e[0:1, 0:NE], -1.0, float(NE), ALU.mult, ALU.add)
            V.tensor_scalar(before_me[:, :], iota_n[:, 0:P], slot_id[:, 0:1], None, ALU.is_gt)
            V.tensor_copy(src_r, src_i)
            ch.link(V.tensor_copy(dst_r, dst_i))
            V.tensor_reduce(span[:, 1:2], dst_r, AX_X, ALU.max)
            ch.link(V.tensor_reduce(span[:, 0:1], dst_r, AX_X, ALU.min))
            ch.link(V.tensor_scalar(span[:, 0:1], span[:, 0:1], float(N - W), None, ALU.min))
            V.tensor_tensor(span[:, 2:3], span[:, 1:2], span[:, 0:1], ALU.subtract)
            V.tensor_scalar(rel_r, dst_r, span[:, 0:1], None, ALU.subtract).then_inc(edge_rows, 1)
            x_lo(0)

            def qkvo_lo_part(m):
                dve.wait_ge(qw_hi, m + 1)
                V.scalar_tensor_tensor(qkvo_lo[m].rearrange("p k n -> p (k n)"), w_raw[m], W_SCALE,
                                       qkvo_hi[m].rearrange("p k n -> p (k n)"), ALU.mult, ALU.subtract)\
                    .then_inc(qw_lo, 1)

            qkvo_lo_part(0)
            dve.wait_ge(edge_cols, 1)
            V.tensor_copy(src_f[:, :], pb[0][:, 0:C])
            ch.link(V.tensor_copy(dst_f[:, :], pb[0][:, P:P + C]))
            V.tensor_copy(rel_h[:, :], pb[0][:, 2 * P:2 * P + C])
            V.tensor_scalar(src_neg[:, :], pb[0][:, 0:C], -1.0, None, ALU.mult)
            ch.link(V.tensor_scalar(w_lo[:, :], pb[0][:, 3 * P:3 * P + C], EDGE_SCALE, None, ALU.mult))
            V.tensor_copy(base_i[:, :], pb[1][0:1, 0:C])
            ch.link(V.tensor_reduce(flag_f[:, 0:1], pb[1][0:1, P:P + C], AX_X, ALU.max))
            ch.link(V.tensor_scalar(flag_f[:, 1:2], flag_f[:, 0:1], float(W), None, ALU.is_lt))
            V.tensor_copy(flag_i[:, :], flag_f[:, 1:2]).then_inc(base_ready, 1)
            ch.link(V.tensor_copy(w_h16[:, :], w_lo[:, :]))
            ch.link(V.tensor_copy(w_hi[:, :], w_h16[:, :]))
            ch.link(V.tensor_tensor(w_lo[:, :], w_lo[:, :], w_hi[:, :], ALU.subtract))
            V.tensor_copy(w_l16[:, :], w_lo[:, :])
            ch.link(V.tensor_copy(dst_i, dst_f[:, :]))
            ch.link(V.tensor_scalar(dst_i, dst_i, GN - 1, None, ALU.bitwise_and))
            ch.link(V.tensor_copy(dl_h[:, :], dst_i))
            ch.link(V.tensor_tensor(dl_hot, bc(iota_n[:, 0:GN], 1, C), bc(dl_h[:, :], 2, GN), ALU.is_equal))
            qkvo_lo_part(1)
            EARLY = 4

            def edge_bias_sum(i):
                dve.wait_ge(attr_mul, i + 1)
                V.tensor_reduce(eb_f[:, EC * i:EC * (i + 1), :].rearrange("p c h -> p (c h)"),
                                attr_w[i % AB].rearrange("p c h d -> p (c h) d"), AX_X, ALU.add).then_inc(eb_sum, 1)

            for i in range(EARLY):
                edge_bias_sum(i)
            dve.wait_ge(small_in, 16 * 15)
            dve.wait_ge(rows_psum, 2)
            n0, n1 = 2 * NE * J, NE * J
            cols0 = pb[2][:, 0:n0].rearrange("p (e j) -> p e j", e=NE)
            V.tensor_scalar(b_sig[:, :, :], cols0[:, :, 0:J], QGELU, None, ALU.mult)
            V.tensor_scalar(b_in[0][:, :, 0:J], cols0[:, :, 0:J], 1.0 / XW_BACK, None, ALU.mult)
            V.tensor_scalar(b_in[0][:, :, J:2 * J], cols0[:, :, J:2 * J], 1.0, X_SCALE * XW_BACK, ALU.add, ALU.mult)
            V.tensor_copy(b_in[1][:, :, :], pb[2][:, n0:n0 + n1].rearrange("p (e j) -> p e j", e=NE))
            V.tensor_copy(cols[:, 0:2, :], pb[2][:, n0 + n1:n0 + n1 + 2 * K].rearrange("p (v k) -> p v k", v=2))
            V.tensor_scalar(cols[:, 2:4, :], pb[2][:, n0 + n1 + 2 * K:n0 + n1 + 4 * K]
                            .rearrange("p (v k) -> p v k", v=2), X_SCALE, None, ALU.mult).then_inc(rows_read, 1)
            qkvo_lo_part(2)
            for i in range(EARLY, C // EC):
                if i == 6:
                    ch.link(V.tensor_tensor(x_sb[:, :, :], x_sb[:, :, :], bc(bo_bc, 1, T), ALU.add))
                if i == 8:
                    qkvo_lo_part(3)
                if i == 12:
                    for f in range(2):
                        dve.wait_ge(rt_split, f + 1)
                        V.scalar_tensor_tensor(rt_lo[f][:, :, :].rearrange("p k e -> p (k e)"),
                                               rt_raw[f][:, :, :].rearrange("p k e -> p (k e)"), W_SCALE,
                                               rt_hi[f][:, :, :].rearrange("p k e -> p (k e)"), ALU.mult,
                                               ALU.subtract).then_inc(rt_split_lo, 1)
                edge_bias_sum(i)
            dve.wait_ge(eb_sum, C // EC)
            ch.link(V.tensor_tensor(eb_f, eb_f, bc(be_bc, 1, C), ALU.add))
            ch.link(V.tensor_scalar(eb_hi, eb_f, EB_SCALE, None, ALU.mult))
            ch.link(V.scalar_tensor_tensor(eb_lo, eb_f, EB_SCALE, eb_hi, ALU.mult, ALU.subtract))
            for t in range(T):
                dve.wait_ge(v_psum, t + 1)
                V.scalar_tensor_tensor(v_sb[:, t, :], pb[t][:, :], XW_BACK, bv_bc, ALU.mult, ALU.add)\
                    .then_inc(v_ready, 1)
            for t in range(T):
                dve.wait_ge(score_psum, t + 1)
                for i in range(2):
                    ins = V.tensor_tensor(score_m[t % 2][:, i:H:2, :, :],
                                          pb[4 + 2 * (t % 2) + i][:, :].rearrange("p (h j k) -> p h j k", h=4, j=GP),
                                          bc(bc(mask[:, :], 1, 4), 3, GN), ALU.mult)
                    ins.then_inc(score_read, 1)
                dve.wait_ge(score_read, 2 * t + 2)
                ch.link(V.tensor_reduce(score[:, t, :, :].rearrange("p k h -> p h k"),
                                        score_m[t % 2].rearrange("p h j k -> p h k j"), AX_X, ALU.add))
            V.memset(settled[:, 31:32], 0.0).then_inc(edge_bias, 1)

            def one_hots(i, b, free, windowed):
                if free:
                    dve.wait_ge(hot_used, i * 2 + (b - 1))
                at = bass.ds(i * (2 * GC) + b * GC, GC)
                if windowed:
                    V.tensor_tensor(rel_hot[b], bc(iota_n[:, 0:W], 1, GC), bc(rel_h[:, at], 2, W), ALU.is_equal)\
                        .then_inc(rel_ready, 1)
                for c in range(AC, GC):
                    one = bass.ds(i * (2 * GC) + (b * GC + c), 1)
                    V.tensor_scalar(src_hot[b][:, c, :], iota_n[:, :], src_f[:, one], None, ALU.is_equal)
                if windowed:
                    dve.wait_ge(rel_ready, i * 2 + (b + 1))
                    for dst, w in ((dst_hi, w_h16), (dst_lo, w_l16)):
                        V.tensor_tensor(dst[b][:, :, 0:W], rel_hot[b], bc(w[:, at], 2, W), ALU.mult)
                else:
                    for c in range(GC):
                        one = bass.ds(i * (2 * GC) + (b * GC + c), 1)
                        for dst, w in ((dst_hi, w_hi), (dst_lo, w_lo)):
                            V.tensor_scalar(dst[b][:, c, :], iota_n[:, :], dst_f[:, one], w[:, one], ALU.is_equal,
                                            ALU.mult)
                for s, eb in enumerate((eb_hi, eb_lo)):
                    last = V.tensor_tensor(ebd[b][:, :, s, :].rearrange("p c (g h) -> p c g h", h=H),
                                           bc(dl_hot[:, at, :], 3, H), bc(eb[:, at, :], 2, GN), ALU.mult)
                last.then_inc(hot_ready, 1)

            def all_one_hots(windowed):
                one_hots(0, 0, False, windowed)
                one_hots(0, 1, False, windowed)
                with dve.Fori(1, C // (2 * GC)) as i:
                    one_hots(i, 0, True, windowed)
                    one_hots(i, 1, True, windowed)

            dve.wait_ge(score_psum, T)
            dve.wait_ge(base_ready, 1)
            narrow = dve.value_load(flag_i[0:1, 0:1], min_val=0, max_val=1)
            with dve.If(narrow):
                all_one_hots(True)
            with dve.Else():
                all_one_hots(False)
            dve.wait_ge(scatter_psum, 1)
            flat = score.rearrange("p t k h -> p t (k h)")
            ch.link(V.tensor_scalar(score, score, float(HD) ** -0.5, None, ALU.mult))
            for s in range(2):
                for i in range(2):
                    ins = V.scalar_tensor_tensor(
                        flat[:, 2 * i:2 * i + 2, :],
                        pb[4 + i][:, :].rearrange("p (t s q) -> p t s q", t=2, s=2)[:, :, s, :],
                        1.0 / EB_SCALE, flat[:, 2 * i:2 * i + 2, :], ALU.mult, ALU.add)
                    ch.link(ins)
            by_head = score.rearrange("p t k h -> p t h k")
            ch.link(V.tensor_reduce(hmax[:, :, :], by_head, AX_X, ALU.max))
            V.tensor_tensor(score, score, bc(hmax[:, :, :], 2, GN), ALU.subtract).then_inc(logits_ready, 1)
            dve.wait_ge(exp_ready, 1)
            ch.link(V.tensor_reduce(hsum[:, :, :], by_head, AX_X, ALU.add))
            ch.link(V.reciprocal(hsum[:, :, :], hsum[:, :, :]))
            ch.link(V.tensor_tensor(score, score, bc(hsum[:, :, :], 2, GN), ALU.mult))

            def spread(t):
                if t >= 2:
                    dve.wait_ge(probT_psum, t - 1)
                V.tensor_tensor(prob[t % 2], bc(score[:, t, :, :].rearrange("p k h -> p h k"), 2, GP),
                                bc(bc(mask[:, :], 1, H), 3, GN), ALU.mult).then_inc(prob_ready, 1)

            def head_lo(t):
                dve.wait_ge(ohi_ready, t + 1)
                V.scalar_tensor_tensor(oT_lo[t % 2].rearrange("p k n -> p (k n)"), pb[t % 2][:, :], X_SCALE,
                                       oT_hi[t % 2].rearrange("p k n -> p (k n)"), ALU.mult, ALU.subtract)\
                    .then_inc(olo_ready, 1)

            def project(t):
                dve.wait_ge(proj_psum, t + 1)
                ins = V.scalar_tensor_tensor(x_sb[:, t, :], pb[2 + t % 2][:, :], XW_BACK, x_sb[:, t, :], ALU.mult,
                                             ALU.add)
                ins.then_inc(x1_ready, 1)

            dve.wait_ge(adj_ready, T)
            ch.link(V.tensor_scalar(has[:, :], deg[:, :], 0.0, None, ALU.is_gt))
            ch.link(V.tensor_tensor(deg[:, :], deg[:, :], has[:, :], ALU.mult))
            ch.link(V.scalar_tensor_tensor(deg[:, :], has[:, :], -1.0, deg[:, :], ALU.mult, ALU.add))
            V.tensor_scalar(deg[:, :], deg[:, :], 1.0, None, ALU.add).then_inc(deg_ready, 1)

            for t in range(T + 2):
                if t < T:
                    spread(t)
                if 1 <= t <= T:
                    head_lo(t - 1)
                if t < 2 * AHEAD:
                    weight_lo(ex[0], 0, t // 2, t % 2)
                if t >= 2:
                    project(t - 2)
            dve.wait_ge(dinv_pow, 1)
            ch.link(V.tensor_tensor(dinv[:, :], dinv[:, :], has[:, :], ALU.mult))
            V.tensor_scalar(ndinv[:, :], dinv[:, :], -2.0 * LAP_SCALE, None, ALU.mult)
            for t in range(T):
                V.tensor_scalar(diag[:, t, :], ident[:, :], dinv[:, t:t + 1], None, ALU.mult).then_inc(diag_ready, 1)

            dve.wait_ge(x1_ready, T)
            layernorm(1, xn)
            x_lo(1)
            node_lo(0)

            def choose(f):
                vals = logit
                for t in range(T):
                    (ch.add if t < T - 1 else ch.link)(V.max(top[:, t, :], vals[:, t, :]))
                for t in range(T):
                    (ch.add if t < T - 1 else ch.link)(V.max_index(top_i[:, t, :], top[:, t, :], vals[:, t, :]))
                ch.link(V.tensor_copy(top_f[:, :, :], top_i[:, :, :]))
                if f == 0:
                    V.tensor_tensor(rsum[:, :], top[:, :, 1], top[:, :, 0], ALU.subtract).then_inc(rt_logit, 1)
                    dve.wait_ge(rt_exp, 1)
                    ch.link(V.tensor_scalar(rsum[:, :], tw[:, :, 1], 1.0, None, ALU.add))
                    ch.link(V.reciprocal(tw[:, :, 0], rsum[:, :]))
                    ch.link(V.tensor_tensor(tw[:, :, 1], tw[:, :, 1], tw[:, :, 0], ALU.mult))
                else:
                    ch.link(V.tensor_copy(tw[:, :, :], top[:, :, 0:2]))
                ch.link(V.tensor_tensor(pick[:, :, :, :], bc(bc(iota_e[:, 0:NE], 1, T), 1, 2),
                                        bc(top_f[:, :, 0:2].rearrange("p t r -> p r t"), 3, NE), ALU.is_equal))
                ch.link(V.tensor_tensor(pick[:, :, :, :], pick[:, :, :, :],
                                        bc(tw[:, :, :].rearrange("p t r -> p r t"), 3, NE), ALU.mult))
                ch.link(V.tensor_tensor(comb[:, :, :], pick[:, 0, :, :], pick[:, 1, :, :], ALU.add))
                ch.link(V.tensor_scalar(chosen[:, :, :], comb[:, :, :], 0.0, None, ALU.not_equal))
                V.tensor_scalar(comb_s[:, :, :], comb[:, :, :], 1.0 / Y_SCALE, None, ALU.mult).then_inc(comb_ready, 1)

            def places(f):
                dve.wait_ge(place_psum, f + 1)
                counts = pb[3][:, 0:T * NE].rearrange("p (t e) -> p t e", t=T)
                ch.link(V.scalar_tensor_tensor(place[:, :, :], counts, 1.0, chosen[:, :, :], ALU.add, ALU.mult))
                ch.link(V.tensor_scalar(place[:, :, :], place[:, :, :], 1.0, None, ALU.subtract))
                to_slots(ex[f], 0)

            def beyond_slots(f):
                ch.link(V.tensor_scalar(over_f[:, 0:NE], pb[3][0:1, T * NE:(T + 1) * NE], float(CAP[f]), None,
                                        ALU.is_gt))
                ch.link(V.tensor_tensor(over_f[:, 0:NE], over_f[:, 0:NE], rank_e[:, :], ALU.mult))
                ch.link(V.max(over_f[:, NE:2 * NE], over_f[:, 0:NE]))
                ch.link(V.tensor_scalar(over_f[:, 0:NE], over_f[:, NE:2 * NE], 1.0, None, ALU.min))
                ch.link(V.scalar_tensor_tensor(over_f[:, NE:2 * NE], over_f[:, NE:2 * NE], -float(NE), over_f[:, 0:NE],
                                               ALU.add, ALU.mult))
                ch.link(V.tensor_scalar(over_f[:, NE:2 * NE], over_f[:, NE:2 * NE], -1.0, None, ALU.mult))
                V.tensor_copy(over_i[f][:, :], over_f[:, :]).then_inc(over_ready, 1)

            def to_slots(x, e):
                for t in range(T):
                    ins = V.tensor_scalar(to_slot[x.f][:, t, :], iota_n[:, 0:x.cols], at_tile(place, t, e), None,
                                          ALU.is_equal)
                ins.then_inc(x.slot_ready, 1)

            def to_nodes(x, e):
                for t in range(x.tiles):
                    r = x.rows(t)
                    ins = V.tensor_scalar(to_node[0:r, t, :],
                                          pos_bc[0:r, bass.ds(e, 1), :].rearrange("p e n -> p (e n)"),
                                          slot_id[0:r, t:t + 1], None, ALU.is_equal)
                ins.then_inc(x.node_ready, 1)

            def gathered_lo(x, e):
                for i in range(2):
                    dve.wait_ge(x.xg_psum, e * 4 + (i + 3))
                    V.tensor_copy(x.x_lo[:, 2 * i:2 * i + 2, :],
                                  pb[6 + i][:, :].rearrange("p (k n) -> p k n", k=2)[:, :, 0:x.cols])\
                        .then_inc(x.xglo, 1)

            def output_lo(x, e):
                for t in range(x.tiles):
                    r = x.rows(t)
                    dve.wait_ge(x.yhi, e * x.tiles + (t + 1))
                    V.scalar_tensor_tensor(y_lo[0:r, t, :], x.out_bank(t), Y_SCALE * XW_BACK, y_hi[0:r, t, :],
                                           ALU.mult, ALU.subtract).then_inc(x.ylo, 1)

            def bring_back(x, e):
                for t in range(T):
                    dve.wait_ge(x.back_psum, e * T + (t + 1))
                    V.scalar_tensor_tensor(x_sb[:, t, :], pb[4 + t][:, :], at_tile(comb_s, t, e), x_sb[:, t, :],
                                           ALU.mult, ALU.add).then_inc(x.o_read, 1)

            def turned(f):
                dve.wait_ge(turned_psum, f + 1)
                V.tensor_copy(posT, pb[4][0:NE, :])
                V.tensor_copy(sel, bc(ident[0:NE, 0:NE], 2, P))
                V.tensor_copy(combT, pb[5][0:NE, :]).then_inc(turned_ready, 1)

            def add_biases(f):
                for t in range(T):
                    dve.wait_ge(bout_psum, T * f + t + 1)
                    V.tensor_tensor(x_sb[:, t, :], x_sb[:, t, :], pb[4 + t][:, :], ALU.add).then_inc(bout_added, 1)

            def spread_read(f, half):
                dve.wait_ge(spread_psum, 2 * f + half + 1)
                for i in range(2, 4):
                    V.tensor_copy(pos_bc[:, 4 * half + i, :], pb[4 + i][:, :]).then_inc(spread_dve, 1)

            def logits(f):
                dve.wait_ge(rt_psum, f + 1)
                V.scalar_tensor_tensor(logit[:, :, :], pb[2][:, 0:T * NE].rearrange("p (t e) -> p t e", t=T), XW_BACK,
                                       bc(rt_b[f][:, :], 1, T), ALU.mult, ALU.add).then_inc(rt_logit, 1)
                dve.wait_ge(rt_logit, 1 if f == 0 else 3)

            logits(0)
            choose(0)
            places(0)
            for t in range(T):
                dve.wait_ge(dinv_psum, T)
                V.scalar_tensor_tensor(lap_f[t], adj[:, t, :], ndinv[:, t:t + 1], pb[1][:, :], ALU.mult, ALU.mult)\
                    .then_inc(lapf_ready, 1)

            def laplacian_lo():
                for t in range(T):
                    dve.wait_ge(laphi_ready, t + 1)
                    V.tensor_tensor(lap_lo[:, t, :], lap_f[t], lap_hi[:, t, :], ALU.subtract)\
                        .then_inc(laplo_ready, 1)

            def expert_step(x, e, w, j, prepare, matrix=False):
                b, s = j % 2, e * J + j
                first, final = (isinstance(e, int) and e == n for n in (0, NE - 1))
                if not x.all and j == 1 and not first:
                    to_nodes(x, e - 1)
                if not x.all and j == 5 and not final:
                    to_slots(x, e + 1)
                if x.f == 0:
                    dve.wait_ge(x.sig, s + 1)
                    dve.wait_ge(x.up, s + 1)
                    V.scalar_tensor_tensor(x.ga_b[b], x.hid_bank(0, b), at_expert(b_in[0], w, j), x.sg_b[b], ALU.add,
                                           ALU.mult).then_inc(x.gated, 1)
                    dve.wait_ge(x.gated, s + 1)
                    V.tensor_tensor(x.ac_b[b], x.ga_b[b], x.up_b[b], ALU.mult).then_inc(x.act, 1)
                if not x.all and j == 0 and not first:
                    output_lo(x, e - 1)
                if not x.all and j == J - 1 and not final:
                    gathered_lo(x, e + 1)
                if prepare:
                    weight_lo(x, e, j // 2 + AHEAD, j % 2)
                if matrix and 2 <= j < 2 + K:
                    dve.wait_ge(cheb_hi, (e - 1) * K + (j - 1))
                    V.scalar_tensor_tensor(cheb_part(e - 1, j - 2, 1), cheb_raw[:, j - 2, :], W_SCALE,
                                           cheb_part(e - 1, j - 2, 0), ALU.mult, ALU.subtract).then_inc(cheb_lo, 1)
                dve.wait_ge(x.ahi, s + 1)
                if x.f == 0:
                    V.tensor_tensor(x.al_b[j % 4], x.ac_b[b], x.ah_b[j % 4], ALU.subtract).then_inc(x.alo, 1)
                else:
                    V.scalar_tensor_tensor(x.al_b[j % 4], x.ac_b[b], X_SCALE, x.ah_b[j % 4], ALU.mult, ALU.subtract)\
                        .then_inc(x.alo, 1)
                if not x.all and j == 3 and not first:
                    bring_back(x, e - 1)

            def experts(f):
                x = ex[f]
                gathered_lo(x, 0)
                beyond_slots(f)
                if f == 0:
                    laplacian_lo()
                for j in range(J):
                    expert_step(x, 0, 0, j, True)
                    if j == 0:
                        turned(f)
                    if j == 1:
                        add_biases(f)
                    if j in (2, 4):
                        spread_read(f, (j - 2) // 2)
                        if j == 2:
                            dve.wait_ge(bout_added, T * (f + 1))
                dve.wait_ge(spread_act, 4 * (f + 1))
                with dve.Fori(1, NE - 1) as e:
                    for j in range(J):
                        expert_step(x, e, e, j, True, f == 0)
                for j in range(J):
                    expert_step(x, NE - 1, NE - 1, j, j // 2 + AHEAD < PAIRS)
                output_lo(x, NE - 1)
                to_nodes(x, NE - 1)
                bring_back(x, NE - 1)
                dve.wait_ge(x.o_read, T * NE)

            def prime(f):
                x = ov[f]
                dve.sem_inc(x.share, 2)
                dve.sem_inc(x.wlo, 2 * PAIRS)
                dve.sem_inc(x.alo, J)
                dve.sem_inc(x.o_read, T)
                if f == 0:
                    dve.sem_inc(x.gated, J)
                    dve.sem_inc(x.act, J)

            def rest(f):
                x = ov[f]

                def body(e, w):
                    for q in range(AHEAD):
                        for half in range(2):
                            weight_lo(x, e, q, half)
                    V.tensor_scalar(over_share[:, :, :], place[:, :, :], CAP[f] - 0.5, XW_BACK, ALU.is_gt, ALU.mult)\
                        .then_inc(x.share, 1)
                    dve.wait_ge(x.share, e * 2 + 1)
                    V.tensor_tensor(over_share[:, :, :], over_share[:, :, :], comb[:, :, :], ALU.mult)\
                        .then_inc(x.share, 1)
                    dve.wait_ge(x.share, e * 2 + 2)
                    for j in range(J):
                        expert_step(x, e, w, j, j // 2 + AHEAD < PAIRS)
                    for t in range(T):
                        dve.wait_ge(x.down, e * (J * T) + ((J - 1) * T + t + 1))
                        V.scalar_tensor_tensor(x_sb[:, t, :], x.out_bank(t), at_tile(over_share, t, w),
                                               x_sb[:, t, :], ALU.mult, ALU.add).then_inc(x.o_read, 1)

                    dve.wait_ge(x.o_read, e * T + T)
                    V.tensor_copy(settled[:, bass.ds(e + 16 * f, 1)], rank_e[:, 0:1])

                overflow(f, dve, body, last=True)
                V.memset(settled[:, 16 * f:16 * f + 1], 0.0).then_inc(pass_done, 1)

            prime(0)
            experts(0)
            rest(0)

            layernorm(2, xn, again=True)
            for k in range(K):
                dve.wait_ge(xhi_ready, 2 * K + k + 1)
                V.tensor_tensor(xT_lo[:, k, :], xT_f[k], xT_hi[:, k, :], ALU.subtract).then_inc(xlo_ready, 1)
            for q in range(AHEAD):
                for half in range(2):
                    weight_lo(ex[1], 0, q, half)

            def term(i, t):
                dve.wait_ge(term_psum, T * i + t + 1)
                p = pb[4 * (i % 2) + t][:, :]
                if i < 2:
                    ins = V.tensor_scalar(bk[i][:, t, :], p, XW_BACK, None, ALU.mult)
                else:
                    ins = V.scalar_tensor_tensor(bk[i % 2][:, t, :], p, XW_BACK, bk[i % 2][:, t, :], ALU.mult,
                                                 ALU.subtract)
                ins.then_inc(term_ready, 1)

            def term_lo(i, t):
                dve.wait_ge(bhi_ready, T * i + t + 1)
                V.scalar_tensor_tensor(bk_lo[:, t, :], bk[i % 2][:, t, :], B_SCALE if i < 3 else B_SCALE / 2,
                                       bk_hi[:, t, :], ALU.mult, ALU.subtract).then_inc(blo_ready, 1)

            for i in range(4):
                for t in range(T):
                    term(i, t)
                    if t >= 1:
                        term_lo(i, t - 1)
                term_lo(i, T - 1)
                if i == 0:
                    dve.wait_ge(late_in, 32)
                    ch.link(V.tensor_tensor(x_sb[:, :, :], x_sb[:, :, :], bc(lb_bc[:, :], 1, T), ALU.add))
                if i == 2:
                    dve.wait_ge(blo_ready, 3 * T)
                    ch.link(V.tensor_tensor(bk[0], bk[0], bc(cb_bc[:, :], 1, T), ALU.subtract))
            for t in range(T):
                term(4, t)
                dve.wait_ge(term_ready, 4 * T + t + 1)
                ch.link(V.scalar_tensor_tensor(out_t[t], bk[0][:, t, :], 0.01, bk[0][:, t, :], ALU.mult, ALU.max))
                (ch.add if t < T - 1 else ch.link)(V.tensor_tensor(x_sb[:, t, :], x_sb[:, t, :], out_t[t], ALU.add))
            for t in range(T):
                dve.wait_ge(lin_psum, t + 1)
                (ch.add if t < T - 1 else ch.link)(V.scalar_tensor_tensor(
                    x_sb[:, t, :], pb[4 + t][:, :], XW_BACK, x_sb[:, t, :], ALU.mult, ALU.add))

            layernorm(4, xn)
            x_lo(3)
            node_lo(1)
            logits(1)
            for t in range(T):
                ch.link(V.tensor_reduce(rmax[:, t:t + 1], logit[:, t, :], AX_X, ALU.max))
            V.tensor_tensor(logit[:, :, :], logit[:, :, :], bc(rmax[:, :], 2, NE), ALU.subtract).then_inc(rt_logit, 1)
            dve.wait_ge(rt_exp, 2)
            ch.link(V.tensor_reduce(rsum[:, :], logit[:, :, :], AX_X, ALU.add))
            ch.link(V.reciprocal(rsum[:, :], rsum[:, :]))
            ch.link(V.tensor_tensor(logit[:, :, :], logit[:, :, :], bc(rsum[:, :], 2, NE), ALU.mult))
            choose(1)
            places(1)
            prime(1)
            experts(1)
            rest(1)

        @block.tensor
        def _(pe):
            MM = nc.tensor.matmul

            def mm3(o, sh, sl, mh, ml, start, stop):
                MM(o, sh, mh, start=start, stop=False)
                MM(o, sh, ml, start=False, stop=False)
                return MM(o, sl, mh, start=False, stop=stop)

            def transpose_x(n):
                for k in range(K):
                    for t in range(T):
                        pe.wait_ge(xn_ready, T * n + t + 1)
                        last = nc.tensor.transpose(pb[4 + k][:, t * P:(t + 1) * P], xn[:, t, k * P:(k + 1) * P],
                                                   ident[:, :])
                    last.then_inc(xt_psum, 1)

            def x_split(n):
                pe.wait_ge(xhi_ready, K * (n + 1))
                pe.wait_ge(xlo_ready, K * (n + 1))

            pe.wait_ge(tables, 9)
            transpose_x(0)

            pe.wait_ge(edge_rows, 1)
            for n, r in enumerate((src_r, dst_r, rel_r, w_f)):
                nc.tensor.transpose(pb[0][:, n * P:n * P + C], r, ident[:, :])
            nc.tensor.transpose(pb[1][0:1, 0:C], span[:, 0:1], ident[:, :])
            nc.tensor.transpose(pb[1][0:1, P:P + C], span[:, 2:3], ident[:, :]).then_inc(edge_cols, 1)

            x_split(0)
            for m in range(2):
                pe.wait_ge(qw_hi, m + 1)
                pe.wait_ge(qw_lo, m + 1)
                if m == 1:
                    pe.wait_ge(small_in, 16 * 15)
                    nr = NE * J + 4 * K
                    nc.tensor.transpose(pb[2][:, 0:P], rows[0][:, :], ident[:, :]).then_inc(rows_psum, 1)
                    nc.tensor.transpose(pb[2][:, P:P + nr], rows[1][0:nr, :], ident[0:nr, 0:nr]).then_inc(rows_psum, 1)
                    pe.wait_ge(rows_read, 1)
                    pe.wait_ge(base_ready, 1)
                for c in range(K):
                    for k in range(K):
                        at = slice(c * P, (c + 1) * P)
                        last = mm3(pb[4 * (1 - m) + c][:, :], qkvo_hi[m][:, k, at], qkvo_lo[m][:, k, at],
                                   xT_hi[:, k, :], xT_lo[:, k, :], k == 0, k == K - 1)
                    last.then_inc(qk_psum, 1)
            pe.wait_ge(qw_hi, 3)
            pe.wait_ge(qw_lo, 3)
            for t in range(T):
                pe.wait_ge(qk_ready, K + t + 1)
                at = slice(t * P, (t + 1) * P)
                for k in range(K):
                    last = mm3(pb[t][:, :], xT_hi[:, k, at], xT_lo[:, k, at], qkvo_hi[2][:, k, :],
                               qkvo_lo[2][:, k, :], k == 0, k == K - 1)
                last.then_inc(v_psum, 1)
            pe.wait_ge(qk_ready, 2 * K)
            for t in range(T):
                if t >= 2:
                    pe.wait_ge(score_read, 2 * (t - 1))
                at = slice(t * P, (t + 1) * P)
                for h in range(H):
                    r = slice(HD * (h % 2), HD * (h % 2) + HD)
                    o = pb[4 + 2 * (t % 2) + h % 2][:, (h // 2) * P:(h // 2 + 1) * P]
                    last = MM(o, qT[r, h // 2, at], kT[r, h // 2, at], start=True, stop=True)
                last.then_inc(score_psum, 1)

            def scatter(i, b, windowed, firsts):
                pe.wait_ge(hot_ready, i * 2 + (b + 1))
                pe.wait_ge(hot_act, i * (2 * AC) + (b + 1) * AC)
                for c in range(GC):
                    if windowed:
                        cols, n = bass.ds(firsts[b * GC + c], W), W
                    else:
                        cols, n = slice(0, N), N
                    for t in range(T):
                        w = src_hot[b][:, c, t * P:(t + 1) * P]
                        MM(pb[t][:, cols], w, dst_hi[b][:, c, 0:n], start=False, stop=False, skip_group_check=True)
                        MM(pb[t][:, cols], w, dst_lo[b][:, c, 0:n], start=False, stop=False, skip_group_check=True)
                        last = MM(pb[4 + t // 2][:, 256 * (t % 2):256 * (t % 2) + 256], w,
                                  ebd[b][:, c, :, :].rearrange("p s q -> p (s q)"), start=False, stop=False,
                                  skip_group_check=True)
                last.then_inc(hot_used, 1)

            def all_scatter(windowed):
                with pe.Fori(0, C // (2 * GC)) as i:
                    firsts = None
                    if windowed:
                        firsts = nc.values_load_multi_w_load_instructions(
                            base_i[0:1, bass.ds(i * (2 * GC), 2 * GC)], engines=[mybir.EngineType.PE], min_val=0,
                            max_val=N - W, skip_runtime_bounds_check_because="a minimum with N - W made them")[1]
                    for b in range(2):
                        scatter(i, b, windowed, firsts)

            pe.wait_ge(v_ready, T)
            pe.wait_ge(score_read, 2 * T)
            for t in range(T + 2):
                MM(pb[t][:, :], zeros[:, :], iota_n[:, :], start=True, stop=False, skip_group_check=True)
            narrow = pe.value_load(flag_i[0:1, 0:1], min_val=0, max_val=1)
            with pe.If(narrow):
                all_scatter(True)
            with pe.Else():
                all_scatter(False)
            for t in range(T + 2):
                last = MM(pb[t][:, :], zeros[:, :], iota_n[:, :], start=False, stop=True, skip_group_check=True)
            last.then_inc(scatter_psum, 1)

            def transpose_prob(t):
                pe.wait_ge(prob_ready, t + 1)
                if t >= 2:
                    pe.wait_ge(probT_ready, 2 * (t - 1))
                for h in range(H):
                    o = pb[(6 if t % 2 == 0 else 4) + h // 4][:, (h % 4) * P:(h % 4 + 1) * P]
                    last = nc.tensor.transpose(o, prob[t % 2][:, h, :, :].rearrange("p j k -> p (j k)"), ident[:, :])
                last.then_inc(probT_psum, 1)

            def attend(t):
                pe.wait_ge(probT_ready, 2 * (t + 1))
                if t < 2:
                    pe.wait_ge(adj_ready, T)
                else:
                    pe.wait_ge(ohi_ready, t - 1)
                    pe.wait_ge(olo_ready, t - 1)
                for h in range(H):
                    o = pb[t % 2][HD * (h % 2):HD * (h % 2) + HD, (h // 2) * P:(h // 2 + 1) * P]
                    last = MM(o, v_sb[:, t, h * HD:(h + 1) * HD], probT[t % 2][:, h, :], start=True, stop=True)
                last.then_inc(o_psum, 1)

            def project(t):
                pe.wait_ge(ohi_ready, t + 1)
                pe.wait_ge(olo_ready, t + 1)
                if t >= 2:
                    pe.wait_ge(x1_ready, t - 1)
                for k in range(K):
                    last = mm3(pb[2 + t % 2][:, :], oT_hi[t % 2][:, k, :], oT_lo[t % 2][:, k, :], qkvo_hi[3][:, k, :],
                               qkvo_lo[3][:, k, :], k == 0, k == K - 1)
                last.then_inc(proj_psum, 1)

            pe.wait_ge(qw_lo, 4)
            for t in range(T + 2):
                if t < T:
                    transpose_prob(t)
                if 1 <= t <= T:
                    attend(t - 1)
                if t >= 2:
                    project(t - 2)

            for t in range(T):
                pe.wait_ge(diag_ready, t + 1)
                MM(pb[1][:, t * P:(t + 1) * P], ones[:, :], diag[:, t, :], start=True, stop=True)\
                    .then_inc(dinv_psum, 1)

            def route(f):
                pe.wait_ge(rt_split_lo, 2)
                for t in range(T):
                    at = slice(t * P, (t + 1) * P)
                    for k in range(K):
                        last = mm3(pb[2][:, t * NE:(t + 1) * NE], xT_hi[:, k, at], xT_lo[:, k, at], rt_hi[f][:, k, :],
                                   rt_lo[f][:, k, :], k == 0, k == K - 1)
                last.then_inc(rt_psum, 1)

            def positions(f):
                pe.wait_ge(comb_ready, f + 1)
                for t in range(T):
                    o = pb[3][:, t * NE:(t + 1) * NE]
                    MM(o, before_me[:, :], chosen[:, t, :], start=True, stop=t == 0)
                    for s in range(t):
                        MM(o, ones_h[:, :], chosen[:, s, :], start=False, stop=s == t - 1)
                for t in range(T):
                    last = MM(pb[3][0:1, T * NE:(T + 1) * NE], ones_h[:, 0:1], chosen[:, t, :], start=t == 0,
                              stop=t == T - 1)
                last.then_inc(place_psum, 1)

            def gather(x, e):
                pe.wait_ge(x.slot_ready, e + 1)
                for part, src in enumerate((xn_hi, xn_lo)):
                    for k in range(K):
                        for t in range(T):
                            o = HALF * (k % 2)
                            last = MM(pb[4 + 2 * part + k // 2][:, o:o + x.cols], src[:, t, k * P:(k + 1) * P],
                                      to_slot[x.f][:, t, :], start=t == 0, stop=t == T - 1)
                        if k % 2 == 1:
                            last.then_inc(x.xg_psum, 1)

            def bring_back(x, e):
                pe.wait_ge(x.node_ready, e + 1)
                pe.wait_ge(x.yhi, (e + 1) * x.tiles)
                pe.wait_ge(x.ylo, (e + 1) * x.tiles)
                for t in range(T):
                    for s in range(x.tiles):
                        r = x.rows(s)
                        for y in (y_hi, y_lo):
                            last = MM(pb[4 + t][:, :], to_node[0:r, s, t * P:(t + 1) * P], y[0:r, s, :],
                                      start=s == 0 and y is y_hi, stop=s == x.tiles - 1 and y is y_lo)
                    last.then_inc(x.back_psum, 1)

            def into_hidden(x, e, j):
                b, s = j % 2, e * J + j
                first = isinstance(e, int) and e == 0
                if j % 2 == 0:
                    n = e * PAIRS + j // 2
                    pe.wait_ge(x.whi, n * 2 + 2)
                    pe.wait_ge(x.wlo, n * 2 + 2)
                if not (first and j < 2):
                    if x.f == 0:
                        pe.wait_ge(x.up, s - 1)
                        pe.wait_ge(x.gated, s - 1)
                    else:
                        pe.wait_ge(x.act, s - 1)
                if not x.all and j == 0:
                    pe.wait_ge(x.xghi, 2 * e + 2)
                    pe.wait_ge(x.xglo, 2 * e + 2)
                wh, wl = x.hi(j // 2), x.lo(j // 2)
                for part in range(x.parts):
                    for k in range(K):
                        last = mm3(x.hid_bank(part, b), x.hid_w(wh, part, k, b), x.hid_w(wl, part, k, b),
                                   x.x_hi[:, k, :], x.x_lo[:, k, :], k == 0, k == K - 1)
                last.then_inc(x.hid_psum, 1)

            def out_of_hidden(x, e, j):
                s = e * J + j
                pe.wait_ge(x.ahi, s + 1)
                pe.wait_ge(x.alo, s + 1)
                if j == 0 and not (isinstance(e, int) and e == 0):
                    if x.all:
                        pe.wait_ge(x.o_read, e * T)
                    else:
                        pe.wait_ge(x.yhi, e * x.tiles)
                        pe.wait_ge(x.ylo, e * x.tiles)
                wh, wl = x.out_w(x.hi(j // 2), j % 2), x.out_w(x.lo(j // 2), j % 2)
                for t in range(x.tiles):
                    at = slice(t * P, t * P + x.rows(t))
                    last = mm3(x.out_bank(t), x.ah_b[j % 4][:, at], x.al_b[j % 4][:, at], wh, wl, j == 0, j == J - 1)
                    last.then_inc(x.down, 1)

            def turn(f):
                for bank, src in ((4, place), (5, comb)):
                    for t in range(T):
                        last = nc.tensor.transpose(pb[bank][0:NE, t * P:(t + 1) * P], src[:, t, :], ident[:, :])
                last.then_inc(turned_psum, 1)

            def biases(f):
                pe.wait_ge(turned_ready, f + 1)
                for t in range(T):
                    MM(pb[4 + t][:, :], combT[:, t * P:(t + 1) * P], b_out[f][:, :], start=True, stop=True)\
                        .then_inc(bout_psum, 1)

            def spread(f, half):
                if half == 0:
                    pe.wait_ge(bout_added, T * (f + 1))
                else:
                    pe.wait_ge(spread_act, 4 * f + 2)
                    pe.wait_ge(spread_dve, 4 * f + 2)
                for i in range(4):
                    last = MM(pb[4 + i][:, :], sel[:, 4 * half + i, :], posT, start=True, stop=True)
                last.then_inc(spread_psum, 1)

            def experts(f):
                x = ex[f]

                def step(e, j):
                    into_hidden(x, e, j)
                    if isinstance(e, int) and e == 0:
                        if j == 0:
                            turn(f)
                        if j == 1:
                            biases(f)
                        if j in (2, 4):
                            spread(f, (j - 2) // 2)
                    elif j == 2:
                        bring_back(x, e - 1)
                    if j == J - 1 and not (isinstance(e, int) and e == NE - 1):
                        if isinstance(e, int):
                            pe.wait_ge(spread_act, 4 * (f + 1))
                            pe.wait_ge(spread_dve, 4 * (f + 1))
                        else:
                            pe.wait_ge(x.o_read, e * T)
                        gather(x, e + 1)
                    if j == 0 and not (isinstance(e, int) and e == 0):
                        out_of_hidden(x, e - 1, J - 1)
                    if j >= LAG:
                        out_of_hidden(x, e, j - LAG)
                    if j == J - 1:
                        out_of_hidden(x, e, j - 1)

                pe.wait_ge(xnhi_ready, T * (f + 1))
                pe.wait_ge(xnlo_ready, T * (f + 1))
                gather(x, 0)
                if f == 0:
                    pe.wait_ge(lapf_ready, T)
                for j in range(J):
                    step(0, j)
                with pe.Fori(1, NE - 1) as e:
                    for j in range(J):
                        step(e, j)
                for j in range(J):
                    step(NE - 1, j)
                out_of_hidden(x, NE - 1, J - 1)
                pe.wait_ge(x.o_read, (NE - 1) * T)
                bring_back(x, NE - 1)

            def prime(f):
                x = ov[f]
                pe.sem_inc(x.hid_psum, J)
                pe.sem_inc(x.down, J * T)

            def rest(f):
                x = ov[f]

                def body(e, w):
                    pe.wait_ge(ex[f].o_read, T * NE)
                    for j in range(J):
                        into_hidden(x, e, j)
                        if j >= LAG:
                            out_of_hidden(x, e, j - LAG)
                    for j in range(J - LAG, J):
                        out_of_hidden(x, e, j)

                overflow(f, pe, body)

            transpose_x(1)
            x_split(1)
            pe.wait_ge(x1_ready, T)
            route(0)
            positions(0)
            prime(0)
            experts(0)
            rest(0)

            transpose_x(2)
            pe.wait_ge(laplo_ready, T)

            def through(m, bank, stop):
                for t in range(T):
                    at = slice(t * P, (t + 1) * P)
                    for k in range(K):
                        last = mm3(pb[bank + t][:, :], xT_hi[:, k, at], xT_lo[:, k, at], cheb_at(m, k, 0),
                                   cheb_at(m, k, 1), k == 0, stop and k == K - 1)
                    if stop:
                        last.then_inc(lin_psum, 1)

            def propagate(i, bank):
                pe.wait_ge(bhi_ready, T * i)
                pe.wait_ge(blo_ready, T * i)
                for t in range(T):
                    at = slice(t * P, (t + 1) * P)
                    for r in range(T):
                        last = mm3(pb[bank + t][:, :], lap_hi[:, r, at], lap_lo[:, r, at], bk_hi[:, r, :],
                                   bk_lo[:, r, :], False, r == T - 1)
                    last.then_inc(term_psum, 1)

            for k in range(K):
                pe.wait_ge(xhi_ready, 2 * K + k + 1)
                pe.wait_ge(xlo_ready, 2 * K + k + 1)
                for t in range(T):
                    at = slice(t * P, (t + 1) * P)
                    last = mm3(pb[t][:, :], xT_hi[:, k, at], xT_lo[:, k, at], cheb_at(4, k, 0), cheb_at(4, k, 1),
                               k == 0, k == K - 1)
                    if k == K - 1:
                        last.then_inc(term_psum, 1)
            for i in range(1, 5):
                bank = 4 * (i % 2)
                if i >= 2:
                    pe.wait_ge(term_ready, T * (i - 1))
                through(4 - i, bank, False)
                propagate(i, bank)
            pe.wait_ge(term_ready, 4 * T)
            through(5, 4, True)

            transpose_x(3)
            x_split(3)
            route(1)
            positions(1)
            prime(1)
            experts(1)
            rest(1)


_OUT = ("out", (512, 512))


def kernel(**inputs):
    import numpy as _np
    import concourse.bacc as _bacc
    from concourse import mybir as _mybir
    from concourse.bass_utils import run_bass_kernel_spmd as _run

    g = {k: _np.asarray(v) for k, v in inputs.items()}
    laid = {
        "x": g["x"], "src": g["src"], "dst": g["dst"], "edge_weight": g["edge_weight"],
        "attr": g["edge_attr_16"].reshape(-1, 128, 16).transpose(1, 0, 2),
        "Wq": g["L0_gnn_Wq"], "bq": g["L0_gnn_bq"], "Wk": g["L0_gnn_Wk"], "bk": g["L0_gnn_bk"],
        "Wv": g["L0_gnn_Wv"], "bv": g["L0_gnn_bv"], "Wo": g["L0_gnn_Wo"], "bo": g["L0_gnn_bo"],
        "WeT": g["L0_gnn_We"].T, "be": g["L0_gnn_be"],
        "router_w": g["L0_ffn_router_w"], "router_b": g["L0_ffn_router_b"],
        "gate_up": g["L0_ffn_gate_up_proj"], "gate_up_bias": g["L0_ffn_gate_up_proj_bias"],
        "down": g["L0_ffn_down_proj"], "down_bias": g["L0_ffn_down_proj_bias"],
        "gamma": g["L1_gnn_ln_gamma"], "beta": g["L1_gnn_ln_beta"],
        "cheb_lin": _np.concatenate([g["L1_gnn_cheb_W"].transpose(0, 2, 1), g["L1_gnn_lin_W"].T[None]]),
        "cheb_b": g["L1_gnn_cheb_b"], "lin_b": g["L1_gnn_lin_b"],
        "WrT": g["L1_ffn_Wr"].T, "br": g["L1_ffn_br"],
        "W1": g["L1_ffn_W1"], "b1": g["L1_ffn_b1"], "W2": g["L1_ffn_W2"], "b2": g["L1_ffn_b2"],
    }
    nc = _bacc.Bacc("TRN2", target_bir_lowering=False, num_devices=1)
    arrays, aps = {}, {}
    for name, v in laid.items():
        v = _np.ascontiguousarray(v)
        arrays[f"in_{name}"] = v
        aps[name] = nc.dram_tensor(f"in_{name}", v.shape, _mybir.dt.from_np(v.dtype), kind="ExternalInput").ap()
    out = nc.dram_tensor(_OUT[0], _OUT[1], _mybir.dt.float32, kind="ExternalOutput").ap()
    build_network(nc, aps, out)
    r = _run(nc, [arrays], core_ids=[0])
    return r.results[0][_OUT[0]]
```
